# Optimizing a Trainium2 kernel written in Bass

```python
import numpy as np
import jax
import jax.numpy as jnp

def _softmax(x, axis=-1):
    return jax.nn.softmax(x, axis=axis)
def _gelu(x):
    return jax.nn.gelu(x, approximate=True)
def _silu(x):
    return jax.nn.silu(x)
def _sigmoid(x):
    return jax.nn.sigmoid(x)
def _layernorm(x, axis=-1, eps=1e-5):
    m = jnp.mean(x, axis=axis, keepdims=True)
    v = jnp.var(x, axis=axis, keepdims=True)
    return (x - m) / jnp.sqrt(v + eps)
def _scatter_add(tgt, idx, src, axis=0):
    return tgt.at[idx].add(src)
def _segment_sum(src, seg, n):
    return jax.ops.segment_sum(src, seg, n)

kernel_name = 'mk_conv_seq_d4_conv_nchw192_517194'

def setup_inputs(seed: int = 0):
    np.random.seed(seed)
    _w = jnp.asarray
    def _rec_inputs():
        import jax
        import jax.numpy as jnp
        _gk = jax.random.key(seed)
        x = -0.0005058 + 1 * jax.random.normal(jax.random.fold_in(_gk, 1), (8, 192, 48, 48), jnp.float32)
        return x
    x = _rec_inputs()
    def _L0_conv_setup():
        import jax, jax.numpy as jnp
        import numpy as np
        import math
        D_MODEL = 192
        D_STATE = 16
        D_CONV = 3
        D_INNER = 2 * D_MODEL
        DT_RANK = math.ceil(D_MODEL / 16)
        BATCH, HH, WW = (8, 48, 48)
        DT_MIN, DT_MAX = (0.001, 0.1)
        EPS = 1e-05

        def _silu(v):
            return v * jax.nn.sigmoid(v)

        def _selective_scan(u, delta, A, Bp, Cp, D_param):
            deltaA = jnp.exp(delta[..., None] * A)
            deltaBu = (delta * u)[..., None] * Bp[:, :, None, :]
            a_seq = jnp.moveaxis(deltaA, 1, 0)
            b_seq = jnp.moveaxis(deltaBu, 1, 0)
            c_seq = jnp.moveaxis(Cp, 1, 0)

            def step(h, abc):
                a_t, b_t, c_t = abc
                h = a_t * h + b_t
                y = jnp.einsum('bds,bs->bd', h, c_t)
                return (h, y)
            h0 = jnp.zeros(u.shape[:1] + (u.shape[2], A.shape[1]), dtype=u.dtype)
            _, ys = jax.lax.scan(step, h0, (a_seq, b_seq, c_seq))
            return jnp.moveaxis(ys, 0, 1) + u * D_param
        key = jax.random.key(seed)
        ks = jax.random.split(key, 10)
        x = jax.random.normal(ks[0], (BATCH, D_MODEL, HH, WW), dtype=jnp.float32)
        in_proj_w = jax.random.normal(ks[1], (2 * D_INNER, D_MODEL), dtype=jnp.float32) * D_MODEL ** (-0.5)
        conv_w = jax.random.normal(ks[2], (D_INNER, 1, D_CONV, D_CONV), dtype=jnp.float32) * (1.0 / 3.0)
        conv_b = jnp.zeros((D_INNER,), dtype=jnp.float32)
        x_proj_w = jax.random.normal(ks[3], (DT_RANK + 2 * D_STATE, D_INNER), dtype=jnp.float32) * D_INNER ** (-0.5)
        dt_std = DT_RANK ** (-0.5)
        dt_proj_w = jax.random.uniform(ks[4], (D_INNER, DT_RANK), dtype=jnp.float32, minval=-dt_std, maxval=dt_std)
        u = jax.random.uniform(ks[5], (D_INNER,), dtype=jnp.float32)
        dt_proj_b = jnp.exp(u * (math.log(DT_MAX) - math.log(DT_MIN)) + math.log(DT_MIN))
        A_log = jnp.log(jnp.tile(jnp.arange(1, D_STATE + 1, dtype=jnp.float32)[None, :], (D_INNER, 1)))
        D_param = jnp.ones((D_INNER,), dtype=jnp.float32)
        ln_g = jnp.ones((D_INNER,), dtype=jnp.float32)
        ln_b = jnp.zeros((D_INNER,), dtype=jnp.float32)
        out_proj_w = jax.random.normal(ks[6], (D_MODEL, D_INNER), dtype=jnp.float32) * D_INNER ** (-0.5)
        fuse_w = jax.random.normal(ks[7], (D_MODEL, D_MODEL, 1, 1), dtype=jnp.float32) * D_MODEL ** (-0.5)
        fuse_b = jnp.zeros((D_MODEL,), dtype=jnp.float32)
        return dict(x=x, in_proj_w=in_proj_w, conv_w=conv_w, conv_b=conv_b, x_proj_w=x_proj_w, dt_proj_w=dt_proj_w, dt_proj_b=dt_proj_b, A_log=A_log, D_param=D_param, ln_g=ln_g, ln_b=ln_b, out_proj_w=out_proj_w, fuse_w=fuse_w, fuse_b=fuse_b)
    _L0_conv_all = _L0_conv_setup()
    _L0_conv_in = {k: v for k, v in _L0_conv_all.items() if k in ('in_proj_w', 'conv_w', 'conv_b', 'x_proj_w', 'dt_proj_w', 'dt_proj_b', 'A_log', 'D_param', 'ln_g', 'ln_b', 'out_proj_w', 'fuse_w', 'fuse_b', )}
    del _L0_conv_all

    def _L1_conv_setup():
        import jax, jax.numpy as jnp
        import numpy as np
        DIM = 192
        K = 3
        RED = 4
        B, H, W = (4, 256, 256)
        EPS = 1e-05

        def _make_mask():
            m = np.ones((DIM, 1, K, K), np.float32)
            m[:, :, K // 2, K // 2:] = 0.0
            m[:, :, K // 2 + 1:] = 0.0
            return jnp.asarray(m)
        MASK = _make_mask()
        key = jax.random.key(seed)
        ks = jax.random.split(key, 4)
        r = DIM // RED
        return {'x': jax.random.normal(ks[0], (B, DIM, H, W), jnp.float32), 'w1': jax.random.normal(ks[1], (r, DIM), jnp.float32) * 0.05, 'gamma': jnp.ones((r,), jnp.float32), 'beta': jnp.zeros((r,), jnp.float32), 'running_mean': jnp.zeros((r,), jnp.float32), 'running_var': jnp.ones((r,), jnp.float32), 'w2': jax.random.normal(ks[2], (DIM * K * K, r), jnp.float32) * 0.05, 'b2': jnp.zeros((DIM * K * K,), jnp.float32), 'bias': jnp.zeros((DIM,), jnp.float32)}
    _L1_conv_all = _L1_conv_setup()
    _L1_conv_in = {k: v for k, v in _L1_conv_all.items() if k in ('w1', 'gamma', 'beta', 'running_mean', 'running_var', 'w2', 'b2', 'bias', )}
    del _L1_conv_all

    def _L2_conv_setup():
        import jax, jax.numpy as jnp
        import numpy as np
        EPS = 1e-05

        def _layernorm(x, g, b):
            mu = jnp.mean(x, axis=-1, keepdims=True)
            var = jnp.mean(jnp.square(x - mu), axis=-1, keepdims=True)
            return (x - mu) * jax.lax.rsqrt(var + EPS) * g + b

        def _afno(x, fc1_w, fc1_b, fc2_w, fc2_b):
            xf = jnp.fft.fft2(x, norm='ortho')
            freq = jnp.stack([xf.real, xf.imag], axis=-1)
            h = jax.nn.gelu(freq @ fc1_w.T + fc1_b, approximate=False)
            h = h @ fc2_w.T + fc2_b
            xff = jax.lax.complex(h[..., 0], h[..., 1])
            return jnp.fft.ifft2(xff, norm='ortho').real
        key = jax.random.key(seed)
        ks = jax.random.split(key, 6)
        B, C, H, W = (4, 192, 128, 128)
        hid_afno, d_ff = (16, 768)
        return {'x': jax.random.normal(ks[0], (B, C, H, W), dtype=jnp.float32), 'fc1_w': jax.random.normal(ks[1], (hid_afno, 2), dtype=jnp.float32) * 0.02, 'fc1_b': jnp.zeros((hid_afno,), jnp.float32), 'fc2_w': jax.random.normal(ks[2], (2, hid_afno), dtype=jnp.float32) * 0.02, 'fc2_b': jnp.zeros((2,), jnp.float32), 'mlp1_w': jax.random.normal(ks[3], (d_ff, C), dtype=jnp.float32) * 0.02, 'mlp1_b': jnp.zeros((d_ff,), jnp.float32), 'mlp2_w': jax.random.normal(ks[4], (C, d_ff), dtype=jnp.float32) * 0.02, 'mlp2_b': jnp.zeros((C,), jnp.float32), 'n1_g': jnp.ones((C,), jnp.float32), 'n1_b': jnp.zeros((C,), jnp.float32), 'n2_g': jnp.ones((C,), jnp.float32), 'n2_b': jnp.zeros((C,), jnp.float32)}
    _L2_conv_all = _L2_conv_setup()
    _L2_conv_in = {k: v for k, v in _L2_conv_all.items() if k in ('fc1_w', 'fc1_b', 'fc2_w', 'fc2_b', 'mlp1_w', 'mlp1_b', 'mlp2_w', 'mlp2_b', 'n1_g', 'n1_b', 'n2_g', 'n2_b', )}
    del _L2_conv_all

    def _L3_conv_setup():
        import jax, jax.numpy as jnp
        import numpy as np
        B, DIM, H, W = (2, 192, 256, 256)
        WIN = 4
        EPS = 1e-05

        def _cd_conj(x):
            if len(x) == 1:
                return x
            h = len(x) // 2
            return np.concatenate([_cd_conj(x[:h]), -x[h:]])

        def _cd_mult(a, b):
            n = len(a)
            if n == 1:
                return a * b
            h = n // 2
            a1, a2, b1, b2 = (a[:h], a[h:], b[:h], b[h:])
            c1 = _cd_mult(a1, b1) - _cd_mult(_cd_conj(b2), a2)
            c2 = _cd_mult(b2, a1) + _cd_mult(a2, _cd_conj(b1))
            return np.concatenate([c1, c2])

        def _sedenion_table(n=16):
            eye = np.eye(n, dtype=np.float32)
            M = np.zeros((n, n, n), dtype=np.float32)
            for i in range(n):
                for j in range(n):
                    M[i, j] = _cd_mult(eye[i], eye[j])
            return M
        SED_TABLE = jnp.asarray(_sedenion_table(16))

        def layer_norm(x, g, b):
            m = x.mean(-1, keepdims=True)
            v = ((x - m) ** 2).mean(-1, keepdims=True)
            return (x - m) * jax.lax.rsqrt(v + EPS) * g + b

        def get_window(x):
            b, c, h, w = x.shape
            x = x.reshape(b, c, h // WIN, WIN, w // WIN, WIN)
            x = x.transpose(0, 2, 4, 3, 5, 1)
            return x.reshape(b, h // WIN, w // WIN, WIN * WIN * c)

        def reverse_window(x, c):
            b, hh, ww, _ = x.shape
            x = x.reshape(b, hh, ww, WIN, WIN, c)
            x = x.transpose(0, 5, 1, 3, 2, 4)
            return x.reshape(b, c, hh * WIN, ww * WIN)

        def sedenion_full_weight(w_sed):
            d = w_sed.shape[1]
            wf = jnp.einsum('ijk,jde->idke', SED_TABLE, w_sed)
            return wf.reshape(16 * d, 16 * w_sed.shape[2])
        key = jax.random.key(seed)
        ks = jax.random.split(key, 8)
        d, dh = (DIM, 4 * DIM)
        s = 0.02
        return {'x': jax.random.normal(ks[0], (B, DIM, H, W), jnp.float32), 'norm1_g': jnp.ones((d,), jnp.float32), 'norm1_b': jnp.zeros((d,), jnp.float32), 'w_sed': jax.random.normal(ks[1], (16, d, d), jnp.float32) * s, 'proj_w': jax.random.normal(ks[2], (d, d), jnp.float32) * s, 'proj_b': jnp.zeros((d,), jnp.float32), 'norm2_g': jnp.ones((d,), jnp.float32), 'norm2_b': jnp.zeros((d,), jnp.float32), 'fc1_w': jax.random.normal(ks[3], (d, dh), jnp.float32) * s, 'fc1_b': jnp.zeros((dh,), jnp.float32), 'fc2_w': jax.random.normal(ks[4], (dh, d), jnp.float32) * s, 'fc2_b': jnp.zeros((d,), jnp.float32)}
    _L3_conv_all = _L3_conv_setup()
    _L3_conv_in = {k: v for k, v in _L3_conv_all.items() if k in ('norm1_g', 'norm1_b', 'w_sed', 'proj_w', 'proj_b', 'norm2_g', 'norm2_b', 'fc1_w', 'fc1_b', 'fc2_w', 'fc2_b', )}
    del _L3_conv_all

    return {
        "x": x,
        "L0_conv_in_proj_w": _L0_conv_in["in_proj_w"],
        "L0_conv_conv_w": _L0_conv_in["conv_w"],
        "L0_conv_conv_b": _L0_conv_in["conv_b"],
        "L0_conv_x_proj_w": _L0_conv_in["x_proj_w"],
        "L0_conv_dt_proj_w": _L0_conv_in["dt_proj_w"],
        "L0_conv_dt_proj_b": _L0_conv_in["dt_proj_b"],
        "L0_conv_A_log": _L0_conv_in["A_log"],
        "L0_conv_D_param": _L0_conv_in["D_param"],
        "L0_conv_ln_g": _L0_conv_in["ln_g"],
        "L0_conv_ln_b": _L0_conv_in["ln_b"],
        "L0_conv_out_proj_w": _L0_conv_in["out_proj_w"],
        "L0_conv_fuse_w": _L0_conv_in["fuse_w"],
        "L0_conv_fuse_b": _L0_conv_in["fuse_b"],
        "L1_conv_w1": _L1_conv_in["w1"],
        "L1_conv_gamma": _L1_conv_in["gamma"],
        "L1_conv_beta": _L1_conv_in["beta"],
        "L1_conv_running_mean": _L1_conv_in["running_mean"],
        "L1_conv_running_var": _L1_conv_in["running_var"],
        "L1_conv_w2": _L1_conv_in["w2"],
        "L1_conv_b2": _L1_conv_in["b2"],
        "L1_conv_bias": _L1_conv_in["bias"],
        "L2_conv_fc1_w": _L2_conv_in["fc1_w"],
        "L2_conv_fc1_b": _L2_conv_in["fc1_b"],
        "L2_conv_fc2_w": _L2_conv_in["fc2_w"],
        "L2_conv_fc2_b": _L2_conv_in["fc2_b"],
        "L2_conv_mlp1_w": _L2_conv_in["mlp1_w"],
        "L2_conv_mlp1_b": _L2_conv_in["mlp1_b"],
        "L2_conv_mlp2_w": _L2_conv_in["mlp2_w"],
        "L2_conv_mlp2_b": _L2_conv_in["mlp2_b"],
        "L2_conv_n1_g": _L2_conv_in["n1_g"],
        "L2_conv_n1_b": _L2_conv_in["n1_b"],
        "L2_conv_n2_g": _L2_conv_in["n2_g"],
        "L2_conv_n2_b": _L2_conv_in["n2_b"],
        "L3_conv_norm1_g": _L3_conv_in["norm1_g"],
        "L3_conv_norm1_b": _L3_conv_in["norm1_b"],
        "L3_conv_w_sed": _L3_conv_in["w_sed"],
        "L3_conv_proj_w": _L3_conv_in["proj_w"],
        "L3_conv_proj_b": _L3_conv_in["proj_b"],
        "L3_conv_norm2_g": _L3_conv_in["norm2_g"],
        "L3_conv_norm2_b": _L3_conv_in["norm2_b"],
        "L3_conv_fc1_w": _L3_conv_in["fc1_w"],
        "L3_conv_fc1_b": _L3_conv_in["fc1_b"],
        "L3_conv_fc2_w": _L3_conv_in["fc2_w"],
        "L3_conv_fc2_b": _L3_conv_in["fc2_b"],
    }

def reference(x, L0_conv_in_proj_w, L0_conv_conv_w, L0_conv_conv_b, L0_conv_x_proj_w, L0_conv_dt_proj_w, L0_conv_dt_proj_b, L0_conv_A_log, L0_conv_D_param, L0_conv_ln_g, L0_conv_ln_b, L0_conv_out_proj_w, L0_conv_fuse_w, L0_conv_fuse_b, L1_conv_w1, L1_conv_gamma, L1_conv_beta, L1_conv_running_mean, L1_conv_running_var, L1_conv_w2, L1_conv_b2, L1_conv_bias, L2_conv_fc1_w, L2_conv_fc1_b, L2_conv_fc2_w, L2_conv_fc2_b, L2_conv_mlp1_w, L2_conv_mlp1_b, L2_conv_mlp2_w, L2_conv_mlp2_b, L2_conv_n1_g, L2_conv_n1_b, L2_conv_n2_g, L2_conv_n2_b, L3_conv_norm1_g, L3_conv_norm1_b, L3_conv_w_sed, L3_conv_proj_w, L3_conv_proj_b, L3_conv_norm2_g, L3_conv_norm2_b, L3_conv_fc1_w, L3_conv_fc1_b, L3_conv_fc2_w, L3_conv_fc2_b):
    import jax
    import jax.numpy as jnp
    def _L0_conv_ref(x, in_proj_w, conv_w, conv_b, x_proj_w, dt_proj_w, dt_proj_b, A_log, D_param, ln_g, ln_b, out_proj_w, fuse_w, fuse_b):
        import jax, jax.numpy as jnp
        import numpy as np
        import math
        D_MODEL = 192
        D_STATE = 16
        D_CONV = 3
        D_INNER = 2 * D_MODEL
        DT_RANK = math.ceil(D_MODEL / 16)
        BATCH, HH, WW = (8, 48, 48)
        DT_MIN, DT_MAX = (0.001, 0.1)
        EPS = 1e-05

        def _silu(v):
            return v * jax.nn.sigmoid(v)

        def _selective_scan(u, delta, A, Bp, Cp, D_param):
            deltaA = jnp.exp(delta[..., None] * A)
            deltaBu = (delta * u)[..., None] * Bp[:, :, None, :]
            a_seq = jnp.moveaxis(deltaA, 1, 0)
            b_seq = jnp.moveaxis(deltaBu, 1, 0)
            c_seq = jnp.moveaxis(Cp, 1, 0)

            def step(h, abc):
                a_t, b_t, c_t = abc
                h = a_t * h + b_t
                y = jnp.einsum('bds,bs->bd', h, c_t)
                return (h, y)
            h0 = jnp.zeros(u.shape[:1] + (u.shape[2], A.shape[1]), dtype=u.dtype)
            _, ys = jax.lax.scan(step, h0, (a_seq, b_seq, c_seq))
            return jnp.moveaxis(ys, 0, 1) + u * D_param
        Bn, C, H, W = x.shape
        L = H * W
        x_hwc = jnp.transpose(x, (0, 2, 3, 1))
        xz = jnp.einsum('bhwc,oc->bhwo', x_hwc, in_proj_w)
        xin, z = jnp.split(xz, 2, axis=-1)
        xin_c = jnp.transpose(xin, (0, 3, 1, 2))
        conv = jax.lax.conv_general_dilated(xin_c, conv_w, window_strides=(1, 1), padding='SAME', feature_group_count=D_INNER, dimension_numbers=('NCHW', 'OIHW', 'NCHW')) + conv_b[None, :, None, None]
        xact = _silu(conv)
        x_flat = jnp.transpose(xact.reshape(Bn, D_INNER, L), (0, 2, 1))
        xp = jnp.einsum('bld,od->blo', x_flat, x_proj_w)
        dt_low = xp[..., :DT_RANK]
        Bp = xp[..., DT_RANK:DT_RANK + D_STATE]
        Cp = xp[..., DT_RANK + D_STATE:]
        dt = jnp.einsum('blr,dr->bld', dt_low, dt_proj_w)
        delta = jax.nn.softplus(dt + dt_proj_b)
        A = -jnp.exp(A_log)
        y = _selective_scan(x_flat, delta, A, Bp, Cp, D_param)
        out = y.reshape(Bn, H, W, D_INNER)
        mu = out.mean(axis=-1, keepdims=True)
        var = out.var(axis=-1, keepdims=True)
        out = (out - mu) * jax.lax.rsqrt(var + EPS) * ln_g + ln_b
        out = out * _silu(z)
        out = jnp.einsum('bhwd,od->bhwo', out, out_proj_w)
        out_c = jnp.transpose(out, (0, 3, 1, 2))
        fused = jnp.einsum('bchw,oc->bohw', out_c, fuse_w[:, :, 0, 0]) + fuse_b[None, :, None, None]
        m = fused.mean(axis=(2, 3), keepdims=True)
        v = fused.var(axis=(2, 3), keepdims=True)
        normed = (fused - m) * jax.lax.rsqrt(v + EPS)
        return x + normed

    def _L1_conv_ref(x, w1, gamma, beta, running_mean, running_var, w2, b2, bias):
        import jax, jax.numpy as jnp
        import numpy as np
        DIM = 192
        K = 3
        RED = 4
        B, H, W = (4, 256, 256)
        EPS = 1e-05

        def _make_mask():
            m = np.ones((DIM, 1, K, K), np.float32)
            m[:, :, K // 2, K // 2:] = 0.0
            m[:, :, K // 2 + 1:] = 0.0
            return jnp.asarray(m)
        MASK = _make_mask()
        b, c, h, w = x.shape
        pooled = x.mean(axis=(2, 3))
        t = pooled @ w1.T
        t = gamma * (t - running_mean) * jax.lax.rsqrt(running_var + EPS) + beta
        t = jax.nn.relu(t)
        wt = t @ w2.T + b2
        wt = wt.reshape(b * DIM, 1, K, K) * jnp.tile(MASK, (b, 1, 1, 1))
        out = jax.lax.conv_general_dilated(x.reshape(1, b * c, h, w), wt, window_strides=(1, 1), padding=((1, 1), (1, 1)), feature_group_count=b * DIM, dimension_numbers=('NCHW', 'OIHW', 'NCHW'))
        out = out + jnp.tile(bias, (b,))[None, :, None, None]
        return out.reshape(b, c, h, w)

    def _L2_conv_ref(x, fc1_w, fc1_b, fc2_w, fc2_b, mlp1_w, mlp1_b, mlp2_w, mlp2_b, n1_g, n1_b, n2_g, n2_b):
        import jax, jax.numpy as jnp
        import numpy as np
        EPS = 1e-05

        def _layernorm(x, g, b):
            mu = jnp.mean(x, axis=-1, keepdims=True)
            var = jnp.mean(jnp.square(x - mu), axis=-1, keepdims=True)
            return (x - mu) * jax.lax.rsqrt(var + EPS) * g + b

        def _afno(x, fc1_w, fc1_b, fc2_w, fc2_b):
            xf = jnp.fft.fft2(x, norm='ortho')
            freq = jnp.stack([xf.real, xf.imag], axis=-1)
            h = jax.nn.gelu(freq @ fc1_w.T + fc1_b, approximate=False)
            h = h @ fc2_w.T + fc2_b
            xff = jax.lax.complex(h[..., 0], h[..., 1])
            return jnp.fft.ifft2(xff, norm='ortho').real
        skip1 = x
        xn = _layernorm(x.transpose(0, 2, 3, 1), n1_g, n1_b).transpose(0, 3, 1, 2)
        x = skip1 + _afno(xn, fc1_w, fc1_b, fc2_w, fc2_b)
        x_perm = x.transpose(0, 2, 3, 1)
        xn2 = _layernorm(x_perm, n2_g, n2_b)
        h = jax.nn.gelu(xn2 @ mlp1_w.T + mlp1_b, approximate=False) @ mlp2_w.T + mlp2_b
        out = (h + x_perm).transpose(0, 3, 1, 2)
        return out

    def _L3_conv_ref(x, norm1_g, norm1_b, w_sed, proj_w, proj_b, norm2_g, norm2_b, fc1_w, fc1_b, fc2_w, fc2_b):
        import jax, jax.numpy as jnp
        import numpy as np
        B, DIM, H, W = (2, 192, 256, 256)
        WIN = 4
        EPS = 1e-05

        def _cd_conj(x):
            if len(x) == 1:
                return x
            h = len(x) // 2
            return np.concatenate([_cd_conj(x[:h]), -x[h:]])

        def _cd_mult(a, b):
            n = len(a)
            if n == 1:
                return a * b
            h = n // 2
            a1, a2, b1, b2 = (a[:h], a[h:], b[:h], b[h:])
            c1 = _cd_mult(a1, b1) - _cd_mult(_cd_conj(b2), a2)
            c2 = _cd_mult(b2, a1) + _cd_mult(a2, _cd_conj(b1))
            return np.concatenate([c1, c2])

        def _sedenion_table(n=16):
            eye = np.eye(n, dtype=np.float32)
            M = np.zeros((n, n, n), dtype=np.float32)
            for i in range(n):
                for j in range(n):
                    M[i, j] = _cd_mult(eye[i], eye[j])
            return M
        SED_TABLE = jnp.asarray(_sedenion_table(16))

        def layer_norm(x, g, b):
            m = x.mean(-1, keepdims=True)
            v = ((x - m) ** 2).mean(-1, keepdims=True)
            return (x - m) * jax.lax.rsqrt(v + EPS) * g + b

        def get_window(x):
            b, c, h, w = x.shape
            x = x.reshape(b, c, h // WIN, WIN, w // WIN, WIN)
            x = x.transpose(0, 2, 4, 3, 5, 1)
            return x.reshape(b, h // WIN, w // WIN, WIN * WIN * c)

        def reverse_window(x, c):
            b, hh, ww, _ = x.shape
            x = x.reshape(b, hh, ww, WIN, WIN, c)
            x = x.transpose(0, 5, 1, 3, 2, 4)
            return x.reshape(b, c, hh * WIN, ww * WIN)

        def sedenion_full_weight(w_sed):
            d = w_sed.shape[1]
            wf = jnp.einsum('ijk,jde->idke', SED_TABLE, w_sed)
            return wf.reshape(16 * d, 16 * w_sed.shape[2])
        b, c, h, w = x.shape
        xn = layer_norm(x.transpose(0, 2, 3, 1), norm1_g, norm1_b).transpose(0, 3, 1, 2)
        xw = get_window(xn)
        wf = sedenion_full_weight(w_sed)
        xw = xw @ wf
        x1 = reverse_window(xw, c)
        y = x1.transpose(0, 2, 3, 1)
        y = jax.nn.gelu(y, approximate=False)
        y = y @ proj_w + proj_b
        x = x + y.transpose(0, 3, 1, 2)
        hbr = layer_norm(x.transpose(0, 2, 3, 1), norm2_g, norm2_b)
        hbr = jax.nn.gelu(hbr @ fc1_w + fc1_b, approximate=False)
        hbr = hbr @ fc2_w + fc2_b
        x = x + hbr.transpose(0, 3, 1, 2)
        return x

    def _gn(v, G=32, eps=1e-5):
        B_, C_, H_, W_ = v.shape
        g = v.reshape(B_, G, C_ // G, H_, W_)
        m = jnp.mean(g, axis=(2, 3, 4), keepdims=True)
        s = jnp.var(g, axis=(2, 3, 4), keepdims=True)
        return ((g - m) / jnp.sqrt(s + eps)).reshape(v.shape)

    def _ln_c(v, eps=1e-6):
        m = jnp.mean(v, axis=1, keepdims=True)
        s = jnp.var(v, axis=1, keepdims=True)
        return (v - m) / jnp.sqrt(s + eps)

    def _ln_t(v, eps=1e-5):
        m = jnp.mean(v, axis=-1, keepdims=True)
        s = jnp.var(v, axis=-1, keepdims=True)
        return (v - m) / jnp.sqrt(s + eps)

    def _to_tokens(v):
        B_, C_, H_, W_ = v.shape
        return v.reshape(B_, C_, H_ * W_).transpose(0, 2, 1)
    def _from_tokens(t, like):
        B_, C_, H_, W_ = like.shape
        return t.transpose(0, 2, 1).reshape(B_, C_, H_, W_)

    x = _L0_conv_ref(x, L0_conv_in_proj_w, L0_conv_conv_w, L0_conv_conv_b, L0_conv_x_proj_w, L0_conv_dt_proj_w, L0_conv_dt_proj_b, L0_conv_A_log, L0_conv_D_param, L0_conv_ln_g, L0_conv_ln_b, L0_conv_out_proj_w, L0_conv_fuse_w, L0_conv_fuse_b)
    x = _L1_conv_ref(x, L1_conv_w1, L1_conv_gamma, L1_conv_beta, L1_conv_running_mean, L1_conv_running_var, L1_conv_w2, L1_conv_b2, L1_conv_bias)
    x = _L2_conv_ref(x, L2_conv_fc1_w, L2_conv_fc1_b, L2_conv_fc2_w, L2_conv_fc2_b, L2_conv_mlp1_w, L2_conv_mlp1_b, L2_conv_mlp2_w, L2_conv_mlp2_b, L2_conv_n1_g, L2_conv_n1_b, L2_conv_n2_g, L2_conv_n2_b)
    x = _L3_conv_ref(x, L3_conv_norm1_g, L3_conv_norm1_b, L3_conv_w_sed, L3_conv_proj_w, L3_conv_proj_b, L3_conv_norm2_g, L3_conv_norm2_b, L3_conv_fc1_w, L3_conv_fc1_b, L3_conv_fc2_w, L3_conv_fc2_b)
    return x


_drawn_inputs = setup_inputs


def setup_inputs(seed=0):
    import zlib

    import numpy as np

    out = dict(_drawn_inputs(seed))
    spreads = {'L0_conv_conv_b': (0.0, 0.1),
     'L0_conv_D_param': (1.0, 0.2),
     'L0_conv_ln_g': (1.0, 0.2),
     'L0_conv_ln_b': (0.0, 0.1),
     'L0_conv_fuse_b': (0.0, 0.8),
     'L1_conv_gamma': (1.0, 0.2),
     'L1_conv_beta': (0.0, 0.1),
     'L1_conv_running_mean': (0.0, 0.1),
     'L1_conv_running_var': (1.0, 0.6),
     'L1_conv_b2': (0.0, 0.1),
     'L1_conv_bias': (0.0, 0.1),
     'L2_conv_fc1_b': (0.0, 0.8),
     'L2_conv_fc2_b': (0.0, 0.275),
     'L2_conv_mlp1_b': (0.0, 0.1),
     'L2_conv_mlp2_b': (0.0, 0.1),
     'L2_conv_n1_g': (1.0, 0.6),
     'L2_conv_n1_b': (0.0, 0.8),
     'L2_conv_n2_g': (1.0, 0.2),
     'L2_conv_n2_b': (0.0, 0.393),
     'L3_conv_norm1_g': (1.0, 0.2),
     'L3_conv_norm1_b': (0.0, 0.1),
     'L3_conv_proj_b': (0.0, 0.1),
     'L3_conv_norm2_g': (1.0, 0.2),
     'L3_conv_norm2_b': (0.0, 0.447),
     'L3_conv_fc1_b': (0.0, 0.1),
     'L3_conv_fc2_b': (0.0, 0.1)}
    factors = {'L0_conv_dt_proj_b': 4.192, 'L2_conv_fc1_w': 8.0, 'L2_conv_fc2_w': 5.169}
    for name, (base, spread) in spreads.items():
        noise = np.random.default_rng([zlib.crc32(name.encode()), seed]).standard_normal(out[name].shape)
        drawn = base * np.exp(spread * noise) if base else spread * noise
        out[name] = jnp.asarray(drawn.astype(out[name].dtype))
    for name, factor in factors.items():
        out[name] = (out[name] * factor).astype(out[name].dtype)
    return out
```

```python
from contextlib import ExitStack

import numpy as np
import concourse.bass as bass
from concourse import mybir

F32 = mybir.dt.float32
ALU = mybir.AluOpType
ACT = mybir.ActivationFunctionType
AXX = mybir.AxisListType.X

H = W = 48
L = H * W
C = 192
CH = 96
DI = 384
ND = DI // 128
NS = 16
R = 12
FF = 768
NF = FF // 128
Q = 384
TR = 16
TT = TR * W
NT = H // TR
WH = 24
KH = 25
GRP = 6
HID = 16
PAIR = 23 * C // 12
WIN = 4
NW = (H // WIN) * (W // WIN)
EPS = 1e-5


class Tally:

    def __init__(self, sem):
        self.sem, self.n = sem, 0

    def inc(self, ins):
        self.n += 1
        ins.then_inc(self.sem, 1)
        return self.n


def sedenion_signs():
    def conj(x):
        if len(x) == 1:
            return x
        h = len(x) // 2
        return np.concatenate([conj(x[:h]), -x[h:]])

    def mult(a, b):
        if len(a) == 1:
            return a * b
        h = len(a) // 2
        a1, a2, b1, b2 = a[:h], a[h:], b[:h], b[h:]
        return np.concatenate([mult(a1, b1) - mult(conj(b2), a2), mult(b2, a1) + mult(a2, conj(b1))])

    eye = np.eye(16)
    return [[int(mult(eye[i], eye[i ^ k])[k]) for k in range(16)] for i in range(16)]


def dft_constants():
    n = np.arange(48)
    cos = np.cos(2 * np.pi * np.outer(n, n) / 48)
    sin = np.sin(2 * np.pi * np.outer(n, n) / 48)
    fwd = np.concatenate([cos[:KH], -sin[1:24]]) / 48.0
    inv = np.concatenate([cos[:KH], -sin[1:24]]) / 48.0
    row_f = np.zeros((96, 96))
    row_i = np.zeros((96, 96))
    for a in range(2):
        row_f[a * 48:a * 48 + 48, a * 48:a * 48 + 48] = fwd.T
        row_i[a * 48:a * 48 + 48, a * 48:a * 48 + 48] = inv
    col = np.stack([np.concatenate([cos, sin]), np.concatenate([-sin, cos]),
                    np.concatenate([cos, -sin]), np.concatenate([-sin, -cos])], 1)
    back = np.stack([np.concatenate([cos, sin], 1), np.concatenate([-sin, cos], 1),
                     np.concatenate([cos, -sin], 1), np.concatenate([-sin, -cos], 1)], 1)
    back = back.reshape(GRP, 8, 1, 4, 96).repeat(HID, 2).reshape(GRP, 128, 4, 96).transpose(1, 2, 0, 3)
    return (row_f.astype(np.float32), row_i.astype(np.float32), col.astype(np.float32),
            np.ascontiguousarray(back).astype(np.float32), np.eye(128, dtype=np.float32))


class Core:

    def __init__(self, nc, ctx, d):
        self.nc, self.ctx, self.d = nc, ctx, d
        self.groups = {}
        self.group = None

    def sb(self, name, shape):
        return self.ctx.enter_context(self.nc.sbuf_tensor(name, shape, F32))

    def sem(self, name):
        s = self.ctx.enter_context(self.nc.semaphore(name))
        self.groups.setdefault(self.group, []).append(s.num)
        return s

    def clear(self, group):
        nums = self.groups[group]
        assert nums == list(range(nums[0], nums[-1] + 1))
        with self.nc.Block() as block:
            @block.sync
            def _(sp):
                sp.sem_clear(range(nums[0], nums[-1] + 1))



LOADS = dict(w_in=[96, 2, 768], conv_w=[128, ND * 9], vec384=[128, 5, ND], a_log=[128, ND * NS],
             w_xp=[128, ND, R + 2 * NS], w_dt=[R, DI], vec192=[96, 2, 2], w1=[96, 2, 48], bn=[48, 4],
             w2=[48, 4, C], b2=[96, 2, 4], fc1b=[128, 1], fc2v=[128, 2], fc2b=[1, 1],
             m1=[96, 2, FF], m1b=[128, NF], m2=[128, NF, C], rows=[96, 11, C], f1=[96, 2, FF], f1b=[128, NF],
             f2=[128, NF, C], proj=[96, 2, C], row_f=[96, 96], row_i=[96, 96], ident=[128, 128])
CONV_B, D_PAR, LN_G, LN_B, DT_B = range(5)
N1G, N1B, N2G, N2B, M2B, L3N1G, L3N1B, L3N2G, L3N2B, PROJ_B, F2B = range(11)


def setup(k):
    nc, d = k.nc, k.d
    k.group = "setup"
    loaded, built, tmp_s, mm, done = (k.sem(n) for n in ("su_loaded", "su_built", "su_tmp", "su_mm", "su_done"))
    late = ("out_w", "fuse_w", "fc1w", "col", "back")
    ar = k.arena
    out_w = ar[0:96, 0:768].rearrange("p (a n) -> p a n", a=2)
    fuse_w = ar[0:96, 768:1152].rearrange("p (a n) -> p a n", a=2)
    fc1w = ar[0:96, 1152:1184].rearrange("p (a n) -> p a n", a=2)
    col = ar[0:96, 1184:1376].rearrange("p (a n) -> p a n", a=4)
    back = ar[:, 1376:1376 + 2304].rearrange("p (s g n) -> p s g n", s=4, g=GRP)
    tmp = ar[:, 4096:4864]
    tmp2 = ar[:, 4864:5632]
    n_load = len(LOADS) + len(late)

    with nc.Block() as block:
        @block.sync
        def _(sp):
            for name in LOADS:
                sp.dma_start(k.t[name][:], d[name]).then_inc(loaded, 16)
            for name, to in zip(late, (out_w, fuse_w, fc1w, col, back)):
                sp.dma_start(to, d[name]).then_inc(loaded, 16)

        @block.gpsimd
        def _(pool):
            nc.gpsimd.memset(k.ones[:], 1.0 / DI).then_inc(built, 1)
            nc.gpsimd.memset(k.eps[:], EPS).then_inc(built, 1)

        @block.scalar
        def _(act):
            act.wait_ge(loaded, 16 * n_load)
            act.wait_ge(built, 2)
            nc.scalar.activation(k.A[:], k.t["a_log"][:], ACT.Exp).then_inc(done, 1)
            nc.scalar.activation(k.bn_r[:], k.t["bn"][:, 3:4], ACT.Sqrt, bias=k.eps[0:48, :]).then_inc(done, 1)

        @block.vector
        def _(dve):
            own = Tally(tmp_s)

            def link(ins):
                dve.wait_ge(tmp_s, own.inc(ins))

            dve.wait_ge(loaded, 16 * n_load)
            dve.wait_ge(done, 2)
            link(nc.vector.tensor_scalar(k.A[:], k.A[:], -1.0, None, ALU.mult))
            link(nc.vector.reciprocal(k.bn_r[:], k.bn_r[:]))
            for t in range(ND * 9):
                own.inc(nc.vector.tensor_scalar(k.diag[:, t, :], k.t["ident"][:], k.t["conv_w"][:, t:t + 1], None, ALU.mult))
            for s in range(2):
                for part, to in ((0, tmp), (1, tmp2)):
                    own.inc(nc.vector.tensor_tensor(
                        to[0:96, :].rearrange("p (n k) -> p n k", k=HID),
                        col[:, 2 * s + part, :].unsqueeze(2).to_broadcast([96, 48, HID]),
                        fc1w[:, part, :].unsqueeze(1).to_broadcast([96, 48, HID]), ALU.mult))
                dve.wait_ge(tmp_s, own.n)
                link(nc.vector.tensor_tensor(k.G[:, s, :], tmp[0:96, :], tmp2[0:96, :], ALU.add))
            for s in range(2):
                link(nc.vector.tensor_scalar(tmp[:, 0:576], back[:, 2 * s, :, :].rearrange("p g n -> p (g n)"),
                                             k.t["fc2v"][:, 0:1], None, ALU.mult))
                link(nc.vector.scalar_tensor_tensor(
                    k.V[:, s, :, :].rearrange("p g n -> p (g n)"), back[:, 2 * s + 1, :, :].rearrange("p g n -> p (g n)"),
                    k.t["fc2v"][:, 1:2], tmp[:, 0:576], ALU.mult, ALU.add))
            link(nc.vector.tensor_scalar(k.t["fc2b"][:], k.t["fc2b"][:], 48.0, None, ALU.mult))
            dve.wait_ge(mm, ND)
            link(nc.vector.tensor_copy(k.w_of[:], k.P[:, 0:ND, 0:C]))

        @block.tensor
        def _(pe):
            pe.wait_ge(loaded, 16 * n_load)
            for m in range(ND):
                for kc in range(2):
                    last = nc.tensor.matmul(k.P[:, m, 0:C], out_w[:, kc, m * 128:m * 128 + 128], fuse_w[:, kc, :],
                                            start=kc == 0, stop=kc == 1)
                last.then_inc(mm, 1)



def in_projection(k, b):
    nc = k.nc
    loaded, mm, copied, border = (k.sem(n) for n in ("ip_loaded", "ip_mm", "ip_copied", "ip_border"))
    n_mm = ND * 6
    with nc.Block() as block:
        @block.sync
        def _(sp):
            sp.dma_start(k.x[:], k.d["x"][b].rearrange("(a p) n -> p a n", p=96)).then_inc(loaded, 16)

        @block.vector
        def _(dve):
            nc.vector.memset(k.xin[:, :, 0, :], 0.0).then_inc(border, 1)
            nc.vector.memset(k.xin[:, :, H + 1, :], 0.0).then_inc(border, 1)
            nc.vector.memset(k.xin[:, :, 1:H + 1, 0], 0.0).then_inc(border, 1)
            nc.vector.memset(k.xin[:, :, 1:H + 1, W + 1], 0.0).then_inc(border, 1)
            nc.vector.memset(k.state[:], 0.0).then_inc(border, 1)

        @block.tensor
        def _(pe):
            pe.wait_ge(loaded, 16)
            for n in range(n_mm):
                m, q = divmod(n, 6)
                if n >= 8:
                    pe.wait_ge(copied, n - 7)
                for kc in range(2):
                    last = nc.tensor.matmul(k.P[:, n % 8, 0:Q], k.t["w_in"][:, kc, m * 128:m * 128 + 128],
                                            k.x[:, kc, q * Q:q * Q + Q], start=kc == 0, stop=kc == 1)
                last.then_inc(mm, 1)

        @block.scalar
        def _(act):
            for n in range(n_mm):
                m, q = divmod(n, 6)
                act.wait_ge(mm, n + 1)
                nc.scalar.activation(k.xin[:, m, 1 + 8 * q:9 + 8 * q, 1:W + 1],
                                     k.P[:, n % 8, 0:Q].rearrange("p (r c) -> p r c", c=W), ACT.Copy).then_inc(copied, 1)


def conv_and_dt(k, tc):
    nc, v = k.nc, k.t["vec384"]
    conv, u_done, xp_mm, xp_done, dt_mm, soft, biased, z_mm, bc_out, z_done, delta = (
        k.sem(n) for n in ("cd_conv", "cd_u", "cd_xp_mm", "cd_xp", "cd_dt_mm", "cd_soft", "cd_biased", "cd_z_mm",
                           "cd_bc", "cd_z", "cd_delta"))
    pair = [k.P[:, 2 * m:2 * m + 2, 0:Q] for m in range(ND)]

    def two(t, m):
        return t[:, m, :].rearrange("p (a n) -> p a n", a=2)

    with nc.Block() as block:
        @block.tensor
        def _(pe):
            for m in range(ND):
                for hf in range(2):
                    for tap in range(9):
                        dy, dx = divmod(tap, 3)
                        last = nc.tensor.matmul(k.P[:, 2 * m + hf, 0:Q].rearrange("p (r c) -> p r c", c=W),
                                                k.diag[:, m * 9 + tap, :],
                                                k.xin[:, m, bass.ds(tc * TR + (8 * hf + dy), 8), dx:dx + W],
                                                start=tap == 0, stop=tap == 8)
                last.then_inc(conv, 1)
            for hf in range(2):
                for m in range(ND):
                    pe.wait_ge(u_done, m + 1)
                    last = nc.tensor.matmul(k.P[0:R + 2 * NS, 6 + hf, 0:Q], k.t["w_xp"][:, m, :],
                                            k.u[:, m, hf * Q:hf * Q + Q], start=m == 0, stop=m == ND - 1)
            last.then_inc(xp_mm, 1)
            pe.wait_ge(xp_done, 1)
            for m in range(ND):
                for hf in range(2):
                    last = nc.tensor.matmul(k.P[:, 2 * m + hf, 0:Q], k.t["w_dt"][:, m * 128:m * 128 + 128],
                                            k.xp[0:R, hf * Q:hf * Q + Q], start=True, stop=True)
                last.then_inc(dt_mm, 1)
            for m in range(ND):
                pe.wait_ge(biased, m + 1)
                for hf in range(2):
                    for kc in range(2):
                        last = nc.tensor.matmul(k.P[:, 2 * m + hf, 0:Q],
                                                k.t["w_in"][:, kc, DI + m * 128:DI + m * 128 + 128],
                                                k.x[:, kc, bass.ds(tc * TT + hf * Q, Q)], start=kc == 0, stop=kc == 1)
                last.then_inc(z_mm, 1)

        @block.scalar
        def _(act):
            for m in range(ND):
                act.wait_ge(conv, m + 1)
                nc.scalar.activation(two(k.u, m), pair[m], ACT.Silu, bias=v[:, CONV_B, m:m + 1]).then_inc(u_done, 1)
            act.wait_ge(xp_mm, 1)
            nc.scalar.activation(k.xp[:].rearrange("p (a n) -> p a n", a=2), k.P[0:R + 2 * NS, 6:8, 0:Q],
                                 ACT.Copy).then_inc(xp_done, 1)
            act.wait_ge(biased, ND)
            nc.scalar.activation(k.delta[:], k.du[:], ACT.Abs).then_inc(soft, 1)
            act.wait_ge(soft, 1)
            nc.scalar.activation(k.delta[:], k.delta[:], ACT.Exp, scale=-1.0).then_inc(soft, 1)
            act.wait_ge(soft, 2)
            nc.scalar.activation(k.delta[:], k.delta[:], ACT.Ln, bias=1.0).then_inc(soft, 1)
            for m in range(ND):
                act.wait_ge(z_mm, m + 1)
                nc.scalar.activation(two(k.sz, m), pair[m], ACT.Silu).then_inc(z_done, 1)

        @block.sync
        def _(sp):
            sp.wait_ge(xp_done, 1)
            sp.dma_start(k.d["bc"], k.xp[R:R + 2 * NS, :]).then_inc(bc_out, 16)
            sp.wait_ge(bc_out, 16)

        @block.vector
        def _(dve):
            for m in range(ND):
                dve.wait_ge(dt_mm, m + 1)
                nc.vector.tensor_scalar(two(k.du, m), pair[m], v[:, DT_B, m:m + 1], None, ALU.add).then_inc(biased, 1)
            dve.wait_ge(biased, ND)
            dve.wait_ge(soft, 3)
            for m in range(ND):
                nc.vector.scalar_tensor_tensor(k.delta[:, m, :], k.du[:, m, :], 0.0, k.delta[:, m, :],
                                               ALU.max, ALU.add).then_inc(delta, 1)
            for m in range(ND):
                dve.wait_ge(delta, m + 1)
                dve.wait_ge(u_done, m + 1)
                nc.vector.tensor_tensor(k.du[:, m, :], k.delta[:, m, :], k.u[:, m, :], ALU.mult).then_inc(delta, 1)


def scan(k):
    nc = k.nc
    bc_in, decay, inp, scanned, kept, read_out, summed = (
        k.sem(n) for n in ("sc_bc", "sc_decay", "sc_input", "sc_scanned", "sc_kept", "sc_times_c", "sc_summed"))
    bc_in1 = k.sem("sc_bc1")
    N = NS * ND

    with nc.Block() as block:
        @block.sync
        def _(sp):
            for s in range(NS):
                if s >= 2:
                    sp.wait_ge(inp, ND * (s - 1))
                    sp.wait_ge(read_out, ND * (s - 1))
                src = k.d["bc"].rearrange("(a s) n -> s a n", a=2)[s:s + 1].to_broadcast([128, 2, TT])
                sp.dma_start(k.bc[:, s % 2, :, :], src).then_inc((bc_in, bc_in1)[s % 2], 16)

        @block.scalar
        def _(act):
            for n in range(N + 1):
                if n < N:
                    s, m = divmod(n, ND)
                    if n >= 2:
                        act.wait_ge(scanned, n - 1)
                    nc.scalar.activation(k.a[:, n % 2, :], k.delta[:, m, :], ACT.Exp,
                                         scale=k.A[:, m * NS + s:m * NS + s + 1]).then_inc(decay, 1)
                if n >= 1:
                    s, m = divmod(n - 1, ND)
                    act.wait_ge(scanned, n)
                    nc.scalar.activation(k.state[:, m * NS + s:m * NS + s + 1], k.h[:, (n - 1) % 2, TT - 1:TT],
                                         ACT.Copy).then_inc(kept, 1)

        @block.vector
        def _(dve):
            for n in range(N):
                s, m = divmod(n, ND)
                if m == 0:
                    dve.wait_ge((bc_in, bc_in1)[s % 2], 16 * (s // 2 + 1))
                if n >= 2:
                    dve.wait_ge(scanned, n - 1)
                nc.vector.tensor_tensor(k.bu[:, n % 2, :], k.du[:, m, :], k.bc[:, s % 2, 0, :], ALU.mult).then_inc(inp, 1)
                dve.wait_ge(decay, n + 1)
                dve.wait_ge(inp, n + 1)
                if n >= 2:
                    dve.wait_ge(read_out, n - 1)
                    dve.wait_ge(kept, n - 1)
                nc.vector.tensor_tensor_scan(k.h[:, n % 2, :], k.a[:, n % 2, :], k.bu[:, n % 2, :],
                                             k.state[:, m * NS + s:m * NS + s + 1], ALU.mult, ALU.add).then_inc(scanned, 1)

        @block.gpsimd
        def _(pool):
            for n in range(N):
                s, m = divmod(n, ND)
                if m == 0:
                    pool.wait_ge((bc_in, bc_in1)[s % 2], 16 * (s // 2 + 1))
                pool.wait_ge(scanned, n + 1)
                if n >= 2:
                    pool.wait_ge(summed, n - 1)
                nc.gpsimd.tensor_tensor(k.g[:, n % 2, :], k.h[:, n % 2, :], k.bc[:, s % 2, 1, :], ALU.mult).then_inc(read_out, 1)

        @block.tensor
        def _(pe):
            for n in range(N):
                s, m = divmod(n, ND)
                pe.wait_ge(read_out, n + 1)
                for hf in range(2):
                    last = nc.tensor.matmul(k.P[:, 2 * m + hf, 0:Q], k.t["ident"][:], k.g[:, n % 2, hf * Q:hf * Q + Q],
                                            start=s == 0, stop=s == NS - 1)
                last.then_inc(summed, 1)


def norm_and_out(k, tc):
    nc, v = k.nc, k.t["vec384"]
    y_done, mean_mm, cent, sq, var_mm, root, rstd, norm, gate, out_mm, out = (
        k.sem(n) for n in ("no_y", "no_mean", "no_cent", "no_sq", "no_var", "no_root", "no_rstd", "no_norm", "no_gate",
                           "no_out_mm", "no_out"))

    def two(t, m):
        return t[:, m, :].rearrange("p (a n) -> p a n", a=2)

    with nc.Block() as block:
        @block.vector
        def _(dve):
            for m in range(ND):
                nc.vector.scalar_tensor_tensor(two(k.y, m), two(k.u, m), v[:, D_PAR, m:m + 1],
                                               k.P[:, 2 * m:2 * m + 2, 0:Q], ALU.mult, ALU.add).then_inc(y_done, 1)
            dve.wait_ge(mean_mm, 1)
            dve.wait_ge(y_done, ND)
            for m in range(ND):
                nc.vector.tensor_tensor(two(k.y, m), two(k.y, m), k.P[:, 6:8, 0:Q], ALU.subtract).then_inc(cent, 1)
            dve.wait_ge(root, 1)
            nc.vector.reciprocal(k.rstd[:], k.rstd[:]).then_inc(rstd, 1)
            dve.wait_ge(rstd, 1)
            dve.wait_ge(cent, ND)
            for m in range(ND):
                nc.vector.tensor_tensor(k.y[:, m, :], k.y[:, m, :], k.rstd[:], ALU.mult).then_inc(norm, 1)
            for m in range(ND):
                dve.wait_ge(norm, m + 1)
                nc.vector.tensor_scalar(k.y[:, m, :], k.y[:, m, :], v[:, LN_G, m:m + 1], v[:, LN_B, m:m + 1],
                                        ALU.mult, ALU.add).then_inc(norm, 1)
            for m in range(ND):
                dve.wait_ge(norm, ND + m + 1)
                nc.vector.tensor_tensor(k.y[:, m, :], k.y[:, m, :], k.sz[:, m, :], ALU.mult).then_inc(gate, 1)

        @block.tensor
        def _(pe):
            for hf in range(2):
                for m in range(ND):
                    pe.wait_ge(y_done, m + 1)
                    last = nc.tensor.matmul(k.P[:, 6 + hf, 0:Q], k.ones[:], k.y[:, m, hf * Q:hf * Q + Q],
                                            start=m == 0, stop=m == ND - 1)
            last.then_inc(mean_mm, 1)
            for hf in range(2):
                for m in range(ND):
                    pe.wait_ge(sq, m + 1)
                    last = nc.tensor.matmul(k.P[:, hf, 0:Q], k.ones[:], k.du[:, m, hf * Q:hf * Q + Q],
                                            start=m == 0, stop=m == ND - 1)
            last.then_inc(var_mm, 1)
            for mo in range(2):
                for hf in range(2):
                    for m in range(ND):
                        pe.wait_ge(gate, m + 1)
                        last = nc.tensor.matmul(k.P[0:96, 2 + 2 * mo + hf, 0:Q], k.w_of[:, m, mo * 96:mo * 96 + 96],
                                                k.y[:, m, hf * Q:hf * Q + Q], start=m == 0, stop=m == ND - 1)
                last.then_inc(out_mm, 1)

        @block.scalar
        def _(act):
            for m in range(ND):
                act.wait_ge(cent, m + 1)
                nc.scalar.activation(k.du[:, m, :], k.y[:, m, :], ACT.Square).then_inc(sq, 1)
            act.wait_ge(var_mm, 1)
            nc.scalar.activation(k.rstd[:].rearrange("p (a n) -> p a n", a=2), k.P[:, 0:2, 0:Q], ACT.Sqrt,
                                 bias=k.eps[:]).then_inc(root, 1)
            for mo in range(2):
                act.wait_ge(out_mm, mo + 1)
                nc.scalar.activation(k.x[:, mo, bass.ds(tc * TT, TT)].rearrange("p (a n) -> p a n", a=2),
                                     k.P[0:96, 2 + 2 * mo:4 + 2 * mo, 0:Q], ACT.Identity,
                                     bias=k.t["vec192"][:, 0, mo:mo + 1]).then_inc(out, 1)



def instance_norm_and_conv(k, b):
    nc, t = k.nc, k.t
    loaded, st, root, x1, pooled, t_mm, tvec, w_mm, w_s, conv, own = (
        k.sem(n) for n in ("in_loaded", "in_stats", "in_root", "in_x1", "in_pooled", "in_t_mm", "in_t", "in_w_mm",
                           "in_w", "in_conv", "in_own"))
    with nc.Block() as block:
        @block.sync
        def _(sp):
            sp.dma_start(k.xres[:], k.d["x"][b].rearrange("(a p) n -> p a n", p=96)).then_inc(loaded, 16)

        @block.vector
        def _(dve):
            c = Tally(own)

            def link(ins):
                dve.wait_ge(own, c.inc(ins))

            c.inc(nc.vector.memset(k.x1p[:, :, 0, :], 0.0))
            c.inc(nc.vector.memset(k.x1p[:, :, 1:H + 1, 0], 0.0))
            c.inc(nc.vector.memset(k.x1p[:, :, 1:H + 1, W + 1], 0.0))
            for mo in range(2):
                for q in range(6):
                    c.inc(nc.vector.bn_stats(k.st[:, (mo * 6 + q) * 6:(mo * 6 + q) * 6 + 6], k.x[:, mo, q * Q:q * Q + Q]))
            dve.wait_ge(own, c.n)
            for mo in range(2):
                c.inc(nc.vector.bn_aggr(k.mv[:, mo, :], k.st[:, mo * 36:mo * 36 + 36]))
            dve.wait_ge(own, c.n)
            nc.vector.tensor_copy(k.rs[:, 0:2], k.mv[:, 0:2, 1]).then_inc(st, 1)
            dve.wait_ge(root, 1)
            link(nc.vector.reciprocal(k.rs[:, 0:2], k.rs[:, 0:2]))
            for mo in range(2):
                c.inc(nc.vector.tensor_scalar(k.x[:, mo, :], k.x[:, mo, :], k.mv[:, mo, 0:1], k.rs[:, mo:mo + 1],
                                              ALU.subtract, ALU.mult))
            dve.wait_ge(own, c.n)
            dve.wait_ge(loaded, 16)
            for mo in range(2):
                nc.vector.tensor_tensor(k.x1p[:, mo, 1:H + 1, 1:W + 1], k.x[:, mo, :].rearrange("p (r c) -> p r c", c=W),
                                        k.xres[:, mo, :].rearrange("p (r c) -> p r c", c=W), ALU.add).then_inc(x1, 1)
            dve.wait_ge(t_mm, 1)
            bn = t["bn"]
            link(nc.vector.tensor_scalar(k.tv[:], k.P[0:48, 0, 0:1], bn[:, 2:3], bn[:, 0:1], ALU.subtract, ALU.mult))
            link(nc.vector.tensor_scalar(k.tv[:], k.tv[:], k.bn_r[:, 0:1], bn[:, 1:2], ALU.mult, ALU.add))
            nc.vector.tensor_scalar(k.tv[:], k.tv[:], 0.0, None, ALU.max).then_inc(tvec, 1)
            dve.wait_ge(w_mm, 1)
            link(nc.vector.tensor_tensor(k.wts[:], k.P[0:96, 1, 0:8], t["b2"][:].rearrange("p a n -> p (a n)"), ALU.add))
            for tap, (dy, dx) in enumerate(((0, 0), (0, 1), (0, 2), (1, 0))):
                for mo in range(2):
                    src = k.x1p[:, mo, dy:dy + H, dx:dx + W]
                    dst = k.x2[:, mo, :].rearrange("p (r c) -> p r c", c=W)
                    wt = k.wts[:, mo * 4 + tap:mo * 4 + tap + 1]
                    if tap == 0:
                        ins = nc.vector.tensor_scalar(dst, src, wt, t["vec192"][:, 1, mo:mo + 1], ALU.mult, ALU.add)
                    else:
                        dve.wait_ge(conv, 2 * (tap - 1) + mo + 1)
                        if tap == 3:
                            for a in range(2):
                                cols = slice(a * WH, a * WH + WH)
                                nc.vector.scalar_tensor_tensor(
                                    k.x2t[:, mo, :, a * H:a * H + H].rearrange("p w h -> p h w"),
                                    src[:, :, cols], wt, dst[:, :, cols], ALU.mult, ALU.add).then_inc(conv, 1)
                            continue
                        ins = nc.vector.scalar_tensor_tensor(dst, src, wt, dst, ALU.mult, ALU.add)
                    ins.then_inc(conv, 1)

        @block.scalar
        def _(act):
            act.wait_ge(st, 1)
            nc.scalar.activation(k.rs[:, 0:2], k.rs[:, 0:2], ACT.Sqrt, bias=k.eps[0:96, :]).then_inc(root, 1)
            act.wait_ge(x1, 2)
            for mo in range(2):
                act.wait_ge(pooled, mo) if mo else None
                nc.scalar.activation(k.xres[:, 0, :].rearrange("p (r c) -> p r c", c=W), k.x1p[:, mo, 1:H + 1, 1:W + 1],
                                     ACT.Copy, scale=1.0 / L, accum_out=k.pool[:, mo:mo + 1]).then_inc(pooled, 1)

        @block.tensor
        def _(pe):
            pe.wait_ge(pooled, 2)
            for kc in range(2):
                last = nc.tensor.matmul(k.P[0:48, 0, 0:1], t["w1"][:, kc, :], k.pool[:, kc:kc + 1], start=kc == 0, stop=kc == 1)
            last.then_inc(t_mm, 1)
            pe.wait_ge(tvec, 1)
            for mo in range(2):
                for tap in range(4):
                    last = nc.tensor.matmul(k.P[0:96, 1, mo * 4 + tap:mo * 4 + tap + 1], t["w2"][:, tap, mo * 96:mo * 96 + 96],
                                            k.tv[:], start=True, stop=True)
            last.then_inc(w_mm, 1)



def to_token_major(k):
    nc = k.nc
    tr, copied = k.sem("tt_tr"), k.sem("tt_copied")
    with nc.Block() as block:
        @block.tensor
        def _(pe):
            for n in range(WH // 2):
                if n >= 8:
                    pe.wait_ge(copied, n - 7)
                for w in range(2):
                    for kc in range(2):
                        last = nc.tensor.transpose(k.P[0:96, n % 8, w * C + kc * 96:w * C + kc * 96 + 96],
                                                   k.x2t[:, kc, 2 * n + w, :],
                                                   k.t["ident"][0:96, 0:96])
                last.then_inc(tr, 1)

        @block.scalar
        def _(act):
            for n in range(WH // 2):
                act.wait_ge(tr, n + 1)
                nc.scalar.activation(k.xT[:, 2 * n:2 * n + 2, :], k.P[0:96, n % 8, 0:2 * C].rearrange("p (w c) -> p w c", c=C),
                                     ACT.Copy).then_inc(copied, 1)


def layer_norm(k, tag, src, dst, g, b, transposed=None, add_bias=None):
    nc, rows = k.nc, k.t["rows"]
    stat, aggr, root, rinv, norm, scaled, shifted, biased, tr, copied = (
        k.sem(tag + n) for n in ("_stat", "_aggr", "_root", "_rinv", "_norm", "_scaled", "_shifted", "_biased", "_tr", "_tcopied"))
    half = WH // 2

    def row(i, n):
        return rows[:, i, :].unsqueeze(1).to_broadcast([96, n, C])

    with nc.Block() as block:
        @block.vector
        def _(dve):
            for w in range(WH):
                nc.vector.bn_stats(k.st[:, w * 6:w * 6 + 6], src[:, w, :]).then_inc(stat, 1)
            for w in range(WH):
                dve.wait_ge(stat, w + 1)
                nc.vector.bn_aggr(k.mv[:, w, :], k.st[:, w * 6:w * 6 + 6]).then_inc(aggr, 1)
            dve.wait_ge(root, 1)
            nc.vector.reciprocal(k.rs[:], k.rs[:]).then_inc(rinv, 1)
            dve.wait_ge(rinv, 1)
            for w in range(WH):
                nc.vector.tensor_scalar(dst[:, w, :], src[:, w, :], k.mv[:, w, 0:1], k.rs[:, w:w + 1],
                                        ALU.subtract, ALU.mult).then_inc(norm, 1)
            for j in range(4):
                dve.wait_ge(norm, 6 * j + 6)
                part = dst[:, 6 * j:6 * j + 6, :]
                nc.vector.tensor_tensor(part, part, row(g, 6), ALU.mult).then_inc(scaled, 1)
                dve.wait_ge(scaled, j + 1)
                nc.vector.tensor_tensor(part, part, row(b, 6), ALU.add).then_inc(shifted, 1)

        @block.scalar
        def _(act):
            act.wait_ge(aggr, WH)
            nc.scalar.activation(k.rs[:], k.mv[:, :, 1], ACT.Sqrt, bias=k.eps[0:96, :]).then_inc(root, 1)
            if transposed is not None:
                for n in range(half):
                    act.wait_ge(tr, n + 1)
                    nc.scalar.activation(transposed[:, :, 2 * n:2 * n + 2, :],
                                         k.P[0:96, n % 8, 0:2 * C].rearrange("p (a w n) -> p a w n", a=2, w=2),
                                         ACT.Copy).then_inc(copied, 1)

        @block.gpsimd
        def _(pool):
            if add_bias is not None:
                pool.wait_ge(norm, WH)
                nc.gpsimd.tensor_tensor(src, src, row(add_bias, WH), ALU.add).then_inc(biased, 1)

        @block.tensor
        def _(pe):
            if transposed is not None:
                for n in range(half):
                    pe.wait_ge(shifted, n // 3 + 1)
                    if n >= 8:
                        pe.wait_ge(copied, n - 7)
                    for kc in range(2):
                        for w in range(2):
                            at = kc * C + w * 96
                            last = nc.tensor.transpose(k.P[0:96, n % 8, at:at + 96], dst[:, 2 * n + w, kc * 96:kc * 96 + 96],
                                                       k.t["ident"][0:96, 0:96])
                    last.then_inc(tr, 1)


def channel_mlp(k, tag, src, res, out, w1, b1, w2, store=None):
    nc, t = k.nc, k.t
    up, act_done, down, added, stored = (k.sem(tag + n) for n in ("_up", "_gelu", "_down", "_added", "_stored"))
    NCH = 6
    with nc.Block() as block:
        @block.tensor
        def _(pe):
            def first(j):
                for m in range(NF):
                    n = j * NF + m
                    if n >= 4:
                        pe.wait_ge(act_done, n - 3)
                    for kc in range(2):
                        last = nc.tensor.matmul(k.P[:, n % 4, 0:Q], t[w1][:, kc, m * 128:m * 128 + 128],
                                                src[:, kc, 4 * j:4 * j + 4, :].rearrange("p w n -> p (w n)"),
                                                start=kc == 0, stop=kc == 1)
                    last.then_inc(up, 1)

            def second(j):
                pe.wait_ge(act_done, NF * (j + 1))
                for w in range(4):
                    n = 4 * j + w
                    if n >= 4:
                        pe.wait_ge(added, n - 3)
                    for m in range(NF):
                        last = nc.tensor.matmul(k.P[0:96, 4 + n % 4, 0:C], k.hid[:, j % 2, m, w * 96:w * 96 + 96],
                                                t[w2][:, m, :], start=m == 0, stop=m == NF - 1)
                    last.then_inc(down, 1)

            first(0)
            for j in range(NCH):
                if j + 1 < NCH:
                    first(j + 1)
                second(j)

        @block.scalar
        def _(act):
            for j in range(NCH):
                if j >= 2:
                    act.wait_ge(down, 4 * (j - 1))
                for m in range(NF):
                    n = j * NF + m
                    act.wait_ge(up, n + 1)
                    nc.scalar.activation(k.hid[:, j % 2, m, :], k.P[:, n % 4, 0:Q], ACT.Gelu,
                                         bias=t[b1][:, m:m + 1]).then_inc(act_done, 1)

        @block.vector
        def _(dve):
            for n in range(WH):
                dve.wait_ge(down, n + 1)
                nc.vector.tensor_tensor(out[:, n, :], k.P[0:96, 4 + n % 4, 0:C], res[:, n, :], ALU.add).then_inc(added, 1)

        @block.sync
        def _(sp):
            if store is not None:
                for j in range(4):
                    sp.wait_ge(added, 6 * j + 6)
                    sp.dma_start(store[:, 6 * j:6 * j + 6, :], out[:, 6 * j:6 * j + 6, :]).then_inc(stored, 16)
                sp.wait_ge(stored, 64)



def rows_dft(k):
    nc = k.nc
    mm, copied, out, back, zero = (k.sem(n) for n in ("rd_mm", "rd_copied", "rd_out", "rd_back", "rd_zero"))
    scr = k.d["spec_in"]
    with nc.Block() as block:
        @block.tensor
        def _(pe):
            for n in range(12):
                if n >= 8:
                    pe.wait_ge(copied, n - 7)
                nc.tensor.matmul(k.P[0:96, n % 8, 0:Q], k.t["row_f"][:],
                                 k.xn[:, 2 * n:2 * n + 2, :].rearrange("p w c -> p (w c)"), start=True, stop=True).then_inc(mm, 1)

        @block.scalar
        def _(act):
            for n in range(12):
                act.wait_ge(mm, n + 1)
                nc.scalar.activation(k.spec[:, n * Q:n * Q + Q], k.P[0:96, n % 8, 0:Q], ACT.Copy).then_inc(copied, 1)

        @block.vector
        def _(dve):
            nc.vector.memset(k.Rb[:, 23 * C:25 * C], 0.0).then_inc(zero, 1)

        @block.sync
        def _(sp):
            for j in range(3):
                sp.wait_ge(copied, 4 * j + 4)
                for a in range(2):
                    sp.dma_start(scr[:, a * WH + 8 * j:a * WH + 8 * j + 8, :],
                                 k.spec[a * 48:a * 48 + 48, 8 * j * C:(8 * j + 8) * C].rearrange("p (w c) -> p w c", c=C)
                                 ).then_inc(out, 16)
            sp.wait_ge(out, 96)
            sp.wait_ge(zero, 1)
            Rk = k.Rb[:].rearrange("p (k c) -> p k c", c=C)
            sp.dma_start(Rk[0:48, 0:23, :], scr[1:24].rearrange("k w c -> w k c")).then_inc(back, 16)
            sp.dma_start(Rk[48:96, 0:23, :], scr[25:48].rearrange("k w c -> w k c")).then_inc(back, 16)
            sp.dma_start(Rk[0:48, 23, :], scr[0]).then_inc(back, 16)
            sp.dma_start(Rk[0:48, 24, :], scr[24]).then_inc(back, 16)
            sp.wait_ge(back, 64)


def frequencies(k):
    nc = k.nc
    hid_mm, gel, acc_mm, got, out, back = (k.sem(n) for n in ("fq_hid", "fq_gelu", "fq_acc", "fq_got", "fq_out", "fq_back"))
    scr = k.d["spec_out"]
    chunks = [(PAIR * j, PAIR, 2) for j in range(12)] + [(23 * C, 2 * C, 1)]
    steps = [(j, s, half) for j, (_, _, ns) in enumerate(chunks) for s in range(ns) for half in range(2)]
    ends = {}
    for n, (j, _, _) in enumerate(steps):
        ends[j] = n

    with nc.Block() as block:
        @block.tensor
        def _(pe):
            def hidden(n):
                j, s, half = steps[n]
                c0, nc_, _ = chunks[j]
                if n >= 2:
                    pe.wait_ge(gel, n - 1)
                for g in range(3):
                    last = nc.tensor.matmul(k.P[:, 3 * (n % 2) + g, 0:nc_],
                                            k.G[:, s, (3 * half + g) * 128:(3 * half + g) * 128 + 128],
                                            k.Rb[:, c0:c0 + nc_], start=True, stop=True)
                last.then_inc(hid_mm, 1)

            def back_to_w(n):
                j, s, half = steps[n]
                c0, nc_, ns = chunks[j]
                pe.wait_ge(gel, n + 1)
                if j >= 2 and s == 0 and half == 0:
                    pe.wait_ge(got, j - 1)
                for g in range(3):
                    last = nc.tensor.matmul(k.P[0:96, 6 + j % 2, 0:nc_], k.V[:, s, 3 * half + g, :],
                                            k.fh[:, n % 3, g, 0:nc_], start=(s == 0 and half == 0 and g == 0),
                                            stop=(s == ns - 1 and half == 1 and g == 2))
                last.then_inc(acc_mm, 1)

            hidden(0)
            for n in range(len(steps)):
                if n + 1 < len(steps):
                    hidden(n + 1)
                back_to_w(n)

        @block.scalar
        def _(act):
            for n, (j, s, half) in enumerate(steps):
                nc_ = chunks[j][1]
                act.wait_ge(hid_mm, n + 1)
                if n >= 3:
                    act.wait_ge(acc_mm, n - 2)
                b = 3 * (n % 2)
                nc.scalar.activation(k.fh[:, n % 3, :, 0:nc_], k.P[:, b:b + 3, 0:nc_], ACT.Gelu,
                                     bias=k.t["fc1b"][:, 0:1]).then_inc(gel, 1)

        @block.vector
        def _(dve):
            for j, (c0, nc_, _) in enumerate(chunks):
                dve.wait_ge(acc_mm, ends[j] + 1)
                nc.vector.tensor_copy(k.gb[:, c0:c0 + nc_], k.P[0:96, 6 + j % 2, 0:nc_]).then_inc(got, 1)

        @block.sync
        def _(sp):
            gk = k.gb[:].rearrange("p (k c) -> p k c", c=C)
            sp.wait_ge(got, 12)
            sp.dma_start(scr[1:24].rearrange("k w c -> w k c"), gk[0:48, 0:23, :]).then_inc(out, 16)
            sp.dma_start(scr[25:48].rearrange("k w c -> w k c"), gk[48:96, 0:23, :]).then_inc(out, 16)
            sp.wait_ge(got, 13)
            sp.dma_start(scr[0], gk[0:48, 23, :]).then_inc(out, 16)
            sp.dma_start(scr[24], gk[0:48, 24, :]).then_inc(out, 16)
            sp.wait_ge(out, 64)
            for a in range(2):
                sp.dma_start(k.spec[a * 48:a * 48 + 48, :].rearrange("p (w c) -> p w c", c=C),
                             scr[:, a * WH:a * WH + WH, :]).then_inc(back, 16)
            sp.wait_ge(back, 32)


def rows_inverse(k):
    nc = k.nc
    mm, added, fixed = (k.sem(n) for n in ("ri_mm", "ri_added", "ri_fixed"))
    with nc.Block() as block:
        @block.tensor
        def _(pe):
            for n in range(12):
                if n >= 8:
                    pe.wait_ge(added, n - 7)
                nc.tensor.matmul(k.P[0:96, n % 8, 0:Q], k.t["row_i"][:], k.spec[:, n * Q:n * Q + Q],
                                 start=True, stop=True).then_inc(mm, 1)

        @block.vector
        def _(dve):
            for n in range(12):
                dve.wait_ge(mm, n + 1)
                part = k.xT[:, 2 * n:2 * n + 2, :].rearrange("p w c -> p (w c)")
                nc.vector.tensor_tensor(part, k.P[0:96, n % 8, 0:Q], part, ALU.add).then_inc(added, 1)
            dve.wait_ge(added, 1)
            nc.vector.tensor_scalar(k.xT[0:1, 0, :], k.xT[0:1, 0, :], k.t["fc2b"][:, 0:1], None, ALU.add).then_inc(fixed, 1)



def sedenion(k):
    nc = k.nc
    loaded, neg, mm, gel, pr_mm, added = (k.sem(n) for n in ("se_w", "se_neg", "se_mm", "se_gelu", "se_proj", "se_added"))
    sign = sedenion_signs()

    def tokens(t, kc, i):
        ih, iw = divmod(i, WIN)
        v = t[:, kc, :, :].rearrange("p (b w) (a r h) -> p w h b a r", w=WIN, a=2, h=WIN)
        return v[:, iw, ih, :, :, :]

    with nc.Block() as block:
        @block.sync
        def _(sp):
            for j in range(4):
                sp.dma_start(k.wsed[:, :, 4 * j:4 * j + 4, :], k.d["wsed"][:, :, 4 * j:4 * j + 4, :]).then_inc(loaded, 16)

        @block.gpsimd
        def _(pool):
            pass

        @block.vector
        def _(dve):
            for kc in range(2):
                nc.vector.tensor_scalar(k.cmn[:, kc, :, :], k.cm[:, kc, :, :], -1.0, None, ALU.mult).then_inc(neg, 1)
            for n in range(WH):
                dve.wait_ge(pr_mm, n + 1)
                nc.vector.tensor_tensor(k.xT[:, n, :], k.P[0:96, n % 8, 0:C], k.xT[:, n, :], ALU.add).then_inc(added, 1)

        @block.tensor
        def _(pe):
            pe.wait_ge(loaded, 64)
            pe.wait_ge(neg, 2)
            for n in range(32):
                kk, mo = divmod(n, 2)
                if n >= 8:
                    pe.wait_ge(gel, n - 7)
                for kc in range(2):
                    for i in range(16):
                        src = k.cm if sign[i][kk] > 0 else k.cmn
                        last = nc.tensor.matmul(k.P[0:96, n % 8, 0:NW].rearrange("p (b a r) -> p b a r", b=6, a=2),
                                                k.wsed[:, kc, i ^ kk, mo * 96:mo * 96 + 96],
                                                tokens(src, kc, i), start=(kc == 0 and i == 0), stop=(kc == 1 and i == 15))
                last.then_inc(mm, 1)
            pe.wait_ge(gel, 32)
            for n in range(WH):
                if n >= 8:
                    pe.wait_ge(added, n - 7)
                for kc in range(2):
                    last = nc.tensor.matmul(k.P[0:96, n % 8, 0:C], k.yg[:, kc, n, :], k.t["proj"][:, kc, :],
                                            start=kc == 0, stop=kc == 1)
                last.then_inc(pr_mm, 1)

        @block.scalar
        def _(act):
            for n in range(32):
                kk, mo = divmod(n, 2)
                act.wait_ge(mm, n + 1)
                nc.scalar.activation(tokens(k.yg, mo, kk), k.P[0:96, n % 8, 0:NW].rearrange("p (b a r) -> p b a r", b=6, a=2),
                                     ACT.Gelu).then_inc(gel, 1)



def layers_kernel(nc, d, nb):
    with ExitStack() as ctx:
        k = Core(nc, ctx, d)
        k.t = {name: k.sb(name, shape) for name, shape in LOADS.items()}
        k.ones = k.sb("ones_over_di", [128, 128])
        k.eps = k.sb("eps", [128, 1])
        k.A = k.sb("A", [128, ND * NS])
        k.bn_r = k.sb("bn_rstd", [48, 1])
        k.diag = k.sb("conv_diag", [128, ND * 9, 128])
        k.G = k.sb("dft_fc1", [96, 2, GRP * 128])
        k.V = k.sb("fc2_idft", [128, 2, GRP, 96])
        k.w_of = k.sb("w_out_fuse", [128, ND, C])
        k.state = k.sb("state", [128, ND * NS])
        k.st = k.sb("bn_parts", [96, WH * 6])
        k.mv = k.sb("mean_var", [96, WH, 2])
        k.rs = k.sb("rstd_tok", [96, WH])
        k.pool = k.sb("pooled", [96, 2])
        k.tv = k.sb("t_vec", [48, 1])
        k.wts = k.sb("tap_weights", [96, 8])
        k.arena = ctx.enter_context(nc.sbuf_tensor("arena", [128, ARENA], F32))
        at = [0]

        def part(parts, *shape):
            n = int(np.prod(shape))
            v = k.arena[0:parts, at[0]:at[0] + n]
            at[0] += n
            names = "abcd"[:len(shape)]
            if len(shape) == 1:
                return v
            return v.rearrange(f"p ({' '.join(names)}) -> p {' '.join(names)}", **{c: s for c, s in zip(names, shape)})

        k.x = part(96, 2, L)
        common = at[0]
        k.xin = part(128, ND, H + 2, W + 2)
        k.u, k.sz, k.delta, k.du = (part(128, ND, TT) for _ in range(4))
        scan_at = at[0]
        k.a, k.bu, k.h, k.g = (part(128, 2, TT) for _ in range(4))
        k.bc = part(128, 2, 2, TT)
        k.xp = part(R + 2 * NS, TT)
        used = at[0]
        at[0] = scan_at
        k.y = part(128, ND, TT)
        k.rstd = part(128, TT)
        used = max(used, at[0])
        at[0] = common
        k.xres = part(96, 2, L)
        k.x2t = k.xres.rearrange("p a (w n) -> p a w n", n=96)
        k.x1p = part(96, 2, H + 1, W + 2)
        k.x2 = part(96, 2, L)
        at[0] = 0
        k.xT = part(96, WH, C)
        k.xn = part(96, WH, C)
        second = at[0]
        k.spec = part(96, WH * C)
        k.Rb = part(96, KH * C)
        k.gb = part(96, KH * C)
        k.fh = part(128, 3, 3, 2 * C)
        used = max(used, at[0])
        at[0] = second
        k.cm = part(96, 2, WH, 96)
        k.cmn = part(96, 2, WH, 96)
        k.hid = part(128, 2, NF, Q)
        at[0] = second + 4 * L
        k.yg = part(96, 2, WH, 96)
        k.wsed = part(96, 2, 16, C)
        used = max(used, at[0])
        assert used <= ARENA, used
        k.P = ctx.enter_context(nc.psum_tensor("psum", [128, 8, 512], F32))

        setup(k)
        with nc.Fori(0, nb) as b:
            k.group = "batch"
            in_projection(k, b)
            with nc.Fori(0, NT) as tc:
                k.group = "piece"
                conv_and_dt(k, tc)
                scan(k)
                norm_and_out(k, tc)
                k.clear("piece")
            k.group = "batch2"
            instance_norm_and_conv(k, b)
            to_token_major(k)
            layer_norm(k, "n1", k.xT, k.xn, N1G, N1B)
            rows_dft(k)
            frequencies(k)
            rows_inverse(k)
            layer_norm(k, "n2", k.xT, k.xn, N2G, N2B, transposed=k.cm, add_bias=M2B)
            channel_mlp(k, "ml", k.cm, k.xT, k.xT, "m1", "m1b", "m2")
            layer_norm(k, "n3", k.xT, k.xn, L3N1G, L3N1B, transposed=k.cm, add_bias=PROJ_B)
            sedenion(k)
            layer_norm(k, "n4", k.xT, k.xn, L3N2G, L3N2B, transposed=k.cm, add_bias=F2B)
            channel_mlp(k, "fc", k.cm, k.xT, k.xn, "f1", "f1b", "f2", store=d["out"][b])
            k.clear("batch")
            k.clear("batch2")


ARENA = 33500


def laid_out(i):
    nb = i["x"].shape[0]

    def v384(v):
        return v.reshape(ND, 128).T

    def v192(v):
        return v.reshape(2, 96).T

    def halves(w):
        return w.reshape(2, 96, -1).transpose(1, 0, 2)

    def chunks(w):
        return w.reshape(-1, 128, w.shape[-1]).transpose(1, 0, 2)

    row_f, row_i, col, back, ident = dft_constants()
    rows = [i[n] for n in ("L2_conv_n1_g", "L2_conv_n1_b", "L2_conv_n2_g", "L2_conv_n2_b", "L2_conv_mlp2_b",
                           "L3_conv_norm1_g", "L3_conv_norm1_b", "L3_conv_norm2_g", "L3_conv_norm2_b",
                           "L3_conv_proj_b", "L3_conv_fc2_b")]
    out = dict(
        x=i["x"].reshape(nb, C, L),
        w_in=halves(i["L0_conv_in_proj_w"].T), conv_w=i["L0_conv_conv_w"].reshape(ND, 128, 9).transpose(1, 0, 2).reshape(128, 27),
        vec384=np.stack([v384(i["L0_conv_" + n]) for n in ("conv_b", "D_param", "ln_g", "ln_b", "dt_proj_b")], 1),
        a_log=i["L0_conv_A_log"].reshape(ND, 128, NS).transpose(1, 0, 2).reshape(128, ND * NS),
        w_xp=chunks(i["L0_conv_x_proj_w"].T), w_dt=i["L0_conv_dt_proj_w"].T,
        vec192=np.stack([v192(i["L0_conv_fuse_b"]), v192(i["L1_conv_bias"])], 1),
        w1=halves(i["L1_conv_w1"].T),
        bn=np.stack([i["L1_conv_" + n] for n in ("gamma", "beta", "running_mean", "running_var")], 1),
        w2=i["L1_conv_w2"].reshape(C, 9, 48)[:, :4].transpose(2, 1, 0),
        b2=i["L1_conv_b2"].reshape(2, 96, 9)[:, :, :4].transpose(1, 0, 2),
        fc1b=np.tile(i["L2_conv_fc1_b"], 8).reshape(128, 1), fc2v=np.tile(i["L2_conv_fc2_w"].T, (8, 1)),
        fc2b=i["L2_conv_fc2_b"][:1].reshape(1, 1),
        m1=halves(i["L2_conv_mlp1_w"].T), m1b=i["L2_conv_mlp1_b"].reshape(NF, 128).T, m2=chunks(i["L2_conv_mlp2_w"].T),
        rows=np.tile(np.stack(rows)[None], (96, 1, 1)),
        f1=halves(i["L3_conv_fc1_w"]), f1b=i["L3_conv_fc1_b"].reshape(NF, 128).T, f2=chunks(i["L3_conv_fc2_w"]),
        proj=halves(i["L3_conv_proj_w"]),
        out_w=halves(i["L0_conv_out_proj_w"]), fuse_w=halves(i["L0_conv_fuse_w"].reshape(C, C).T),
        fc1w=np.tile(i["L2_conv_fc1_w"].T[None], (96, 1, 1)),
        wsed=i["L3_conv_w_sed"].reshape(16, 2, 96, C).transpose(2, 1, 0, 3),
        row_f=row_f, row_i=row_i, col=col, back=back, ident=ident)
    return {n: np.ascontiguousarray(v) for n, v in out.items()}


def kernel(**inputs):
    import concourse.bacc as bacc
    from concourse.bass_utils import run_bass_kernel_spmd

    arrays = laid_out({n: np.asarray(v) for n, v in inputs.items()})
    nb = arrays["x"].shape[0]
    nc = bacc.Bacc("TRN2", target_bir_lowering=False, num_devices=1)
    d = {n: nc.dram_tensor("in_" + n, a.shape, F32, kind="ExternalInput").ap() for n, a in arrays.items()}
    d["out"] = nc.dram_tensor("out", (nb, 96, WH, C), F32, kind="ExternalOutput").ap()
    d["bc"] = nc.dram_tensor("bc_scratch", (2 * NS, TT), F32, kind="Internal").ap()
    d["spec_in"] = nc.dram_tensor("spec_in_scratch", (48, 48, C), F32, kind="Internal").ap()
    d["spec_out"] = nc.dram_tensor("spec_out_scratch", (48, 48, C), F32, kind="Internal").ap()
    layers_kernel(nc, d, nb)
    r = run_bass_kernel_spmd(nc, [{"in_" + n: a for n, a in arrays.items()}], core_ids=[0])
    got = np.asarray(r.results[0]["out"])
    return got.reshape(nb, 2, 48, WH, C).transpose(0, 4, 2, 1, 3).reshape(nb, C, H, W)
```

```python
from contextlib import ExitStack

import numpy as np
import concourse.bass as bass
from concourse import mybir

F32 = mybir.dt.float32
ALU = mybir.AluOpType
ACT = mybir.ActivationFunctionType
AXX = mybir.AxisListType.X

H = W = 48
L = H * W
C = 192
CH = 96
DI = 384
ND = DI // 128
NS = 16
R = 12
FF = 768
NF = FF // 128
Q = 384
TR = 8
TT = TR * W
NT = H // TR
WH = 24
KH = 25
GRP = 6
HID = 16
PAIR = 23 * C // 12
WIN = 4
NW = (H // WIN) * (W // WIN)
EPS = 1e-5


def in_turn(programs):
    heads = []
    for n, p in enumerate(programs):
        due = next(p, None)
        if due is not None:
            heads.append((due, n, p))
    while heads:
        due, n, p = min(heads, key=lambda h: h[:2])
        heads.remove((due, n, p))
        due_next = next(p, None)
        if due_next is not None:
            heads.append((max(due, due_next), n, p))


class Tally:

    def __init__(self, sem):
        self.sem, self.n = sem, 0

    def inc(self, ins):
        self.n += 1
        ins.then_inc(self.sem, 1)
        return self.n


def sedenion_signs():
    def conj(x):
        if len(x) == 1:
            return x
        h = len(x) // 2
        return np.concatenate([conj(x[:h]), -x[h:]])

    def mult(a, b):
        if len(a) == 1:
            return a * b
        h = len(a) // 2
        a1, a2, b1, b2 = a[:h], a[h:], b[:h], b[h:]
        return np.concatenate([mult(a1, b1) - mult(conj(b2), a2), mult(b2, a1) + mult(a2, conj(b1))])

    eye = np.eye(16)
    return [[int(mult(eye[i], eye[i ^ k])[k]) for k in range(16)] for i in range(16)]


def dft_constants():
    n = np.arange(48)
    cos = np.cos(2 * np.pi * np.outer(n, n) / 48)
    sin = np.sin(2 * np.pi * np.outer(n, n) / 48)
    fwd = np.concatenate([cos[:KH], -sin[1:24]]) / 48.0
    inv = np.concatenate([cos[:KH], -sin[1:24]]) / 48.0
    row_f = np.zeros((96, 96))
    row_i = np.zeros((96, 96))
    for a in range(2):
        row_f[a * 48:a * 48 + 48, a * 48:a * 48 + 48] = fwd.T
        row_i[a * 48:a * 48 + 48, a * 48:a * 48 + 48] = inv
    col = np.stack([np.concatenate([cos, sin]), np.concatenate([-sin, cos]),
                    np.concatenate([cos, -sin]), np.concatenate([-sin, -cos])], 1)
    back = np.stack([np.concatenate([cos, sin], 1), np.concatenate([-sin, cos], 1),
                     np.concatenate([cos, -sin], 1), np.concatenate([-sin, -cos], 1)], 1)
    back = back.reshape(GRP, 8, 1, 4, 96).repeat(HID, 2).reshape(GRP, 128, 4, 96).transpose(1, 2, 0, 3)
    return (row_f.astype(np.float32), row_i.astype(np.float32), col.astype(np.float32),
            np.ascontiguousarray(back).astype(np.float32), np.eye(128, dtype=np.float32))


class Core:

    POOL = 44

    def __init__(self, nc, ctx, d):
        self.nc, self.ctx, self.d = nc, ctx, d
        self.pools = [[ctx.enter_context(nc.semaphore(f"pool{p}_{n}")) for n in range(self.POOL)] for p in range(2)]
        self.parity = 0
        self.used = 0

    def sb(self, name, shape):
        return self.ctx.enter_context(self.nc.sbuf_tensor(name, shape, F32))

    def sems(self, n):
        self.used += n
        return self.pools[self.parity][self.used - n:self.used]

    def together(self, *stages):
        other = [s.num for s in self.pools[1 - self.parity]]
        with self.nc.Block() as block:
            @block.sync
            def _(sp):
                sp.sem_clear(range(other[0], other[-1] + 1))
                in_turn([st["sync"](sp) for st in stages if "sync" in st])

            @block.tensor
            def _(pe):
                in_turn([st["tensor"](pe) for st in stages if "tensor" in st])

            @block.vector
            def _(dve):
                in_turn([st["vector"](dve) for st in stages if "vector" in st])

            @block.scalar
            def _(act):
                in_turn([st["scalar"](act) for st in stages if "scalar" in st])

            @block.gpsimd
            def _(pool):
                in_turn([st["gpsimd"](pool) for st in stages if "gpsimd" in st])
        self.parity ^= 1
        self.used = 0

    def even(self):
        if self.parity:
            self.together()



LOADS = dict(w_in=[96, 2, 768], conv_w=[128, ND * 9], vec384=[128, 5, ND], a_log=[128, ND * NS],
             w_xp=[128, ND, R + 2 * NS], w_dt=[R, DI], vec192=[96, 2, 2], w1=[96, 2, 48], bn=[48, 4],
             w2=[48, 4, C], b2=[96, 2, 4], fc1b=[128, 1], fc2v=[128, 2], fc2b=[1, 1],
             m1=[96, 2, FF], m1b=[128, NF], m2=[128, NF, C], rows=[96, 11, C], f1=[96, 2, FF], f1b=[128, NF],
             f2=[128, NF, C], proj=[96, 2, C], row_f=[96, 96], row_i=[96, 96], ident=[128, 128])
CONV_B, D_PAR, LN_G, LN_B, DT_B = range(5)
N1G, N1B, N2G, N2B, M2B, L3N1G, L3N1B, L3N2G, L3N2B, PROJ_B, F2B = range(11)


def setup(k):
    nc, d = k.nc, k.d
    loaded, built, tmp_s, mm, done = k.sems(5)
    late = ("out_w", "fuse_w", "fc1w", "col", "back")
    ar = k.arena
    out_w = ar[0:96, 0:768].rearrange("p (a n) -> p a n", a=2)
    fuse_w = ar[0:96, 768:1152].rearrange("p (a n) -> p a n", a=2)
    fc1w = ar[0:96, 1152:1184].rearrange("p (a n) -> p a n", a=2)
    col = ar[0:96, 1184:1376].rearrange("p (a n) -> p a n", a=4)
    back = ar[:, 1376:1376 + 2304].rearrange("p (s g n) -> p s g n", s=4, g=GRP)
    tmp = ar[:, 4096:4864]
    tmp2 = ar[:, 4864:5632]
    n_load = len(LOADS) + len(late)

    def sync(sp):
        yield 0
        for name in LOADS:
            sp.dma_start(k.t[name][:], d[name]).then_inc(loaded, 16)
        for name, to in zip(late, (out_w, fuse_w, fc1w, col, back)):
            sp.dma_start(to, d[name]).then_inc(loaded, 16)

    def gpsimd(pool):
        yield 0
        nc.gpsimd.memset(k.ones[:], 1.0 / DI).then_inc(built, 1)
        nc.gpsimd.memset(k.eps[:], EPS).then_inc(built, 1)

    def scalar(act):
        yield 0
        act.wait_ge(loaded, 16 * n_load)
        act.wait_ge(built, 2)
        nc.scalar.activation(k.A[:], k.t["a_log"][:], ACT.Exp).then_inc(done, 1)
        nc.scalar.activation(k.bn_r[:], k.t["bn"][:, 3:4], ACT.Sqrt, bias=k.eps[0:48, :]).then_inc(done, 1)

    def vector(dve):
        yield 0
        own = Tally(tmp_s)

        def link(ins):
            dve.wait_ge(tmp_s, own.inc(ins))

        dve.wait_ge(loaded, 16 * n_load)
        dve.wait_ge(done, 2)
        link(nc.vector.tensor_scalar(k.A[:], k.A[:], -1.0, None, ALU.mult))
        link(nc.vector.reciprocal(k.bn_r[:], k.bn_r[:]))
        for s in range(2):
            for part, to in ((0, tmp), (1, tmp2)):
                own.inc(nc.vector.tensor_tensor(
                    to[0:96, :].rearrange("p (n k) -> p n k", k=HID),
                    col[:, 2 * s + part, :].unsqueeze(2).to_broadcast([96, 48, HID]),
                    fc1w[:, part, :].unsqueeze(1).to_broadcast([96, 48, HID]), ALU.mult))
            dve.wait_ge(tmp_s, own.n)
            link(nc.vector.tensor_tensor(k.G[:, s, :], tmp[0:96, :], tmp2[0:96, :], ALU.add))
        for s in range(2):
            link(nc.vector.tensor_scalar(tmp[:, 0:576], back[:, 2 * s, :, :].rearrange("p g n -> p (g n)"),
                                         k.t["fc2v"][:, 0:1], None, ALU.mult))
            link(nc.vector.scalar_tensor_tensor(
                k.V[:, s, :, :].rearrange("p g n -> p (g n)"), back[:, 2 * s + 1, :, :].rearrange("p g n -> p (g n)"),
                k.t["fc2v"][:, 1:2], tmp[:, 0:576], ALU.mult, ALU.add))
        link(nc.vector.tensor_scalar(k.t["fc2b"][:], k.t["fc2b"][:], 48.0, None, ALU.mult))
        dve.wait_ge(mm, ND)
        link(nc.vector.tensor_copy(k.w_of[:], k.P[:, 0:ND, 0:C]))

    def tensor(pe):
        yield 0
        pe.wait_ge(loaded, 16 * n_load)
        for m in range(ND):
            for kc in range(2):
                last = nc.tensor.matmul(k.P[:, m, 0:C], out_w[:, kc, m * 128:m * 128 + 128], fuse_w[:, kc, :],
                                        start=kc == 0, stop=kc == 1)
            last.then_inc(mm, 1)

    k.together(dict(sync=sync, gpsimd=gpsimd, scalar=scalar, vector=vector, tensor=tensor))



def prepare(k, b, j):
    nc, v = k.nc, k.t["vec384"]
    (loaded, kept_rows, border, in_mm, copied, conv, u_done, xp_mm, xp_done, dt_mm, soft, biased, bc_out,
     delta) = k.sems(14)
    at = 1 if j == 0 else 2
    row0 = 0 if j == 0 else TR * j + 1
    rows = min(TR * j + TR + 1, H) - row0
    n_tok = rows * W
    off = (row0 - TR * j) * W
    xp = k.xpc[:, j % 2, :, :]
    bank = [k.P[:, 5 + m, :] for m in range(ND)]
    dt_bank = [bank[(m + 1) % 3] for m in range(ND)]

    def sync(sp):
        if j == 0:
            yield 0
            load_piece(k, sp, b, 0, loaded)
        yield .6
        sp.wait_ge(xp_done, 1)
        sp.dma_start(k.d["bc"], k.xp[R:R + 2 * NS, :]).then_inc(bc_out, 16)
        yield 1
        sp.wait_ge(bc_out, 16)

    def gpsimd(pool):
        yield 0
        if j == 0:
            nc.gpsimd.memset(k.xin[:, :, 0, 1:W + 1], 0.0).then_inc(border, 1)
            nc.gpsimd.memset(k.xin[:, :, :, 0], 0.0).then_inc(border, 1)
            nc.gpsimd.memset(k.xin[:, :, :, W + 1], 0.0).then_inc(border, 1)
            nc.gpsimd.memset(k.state[:], 0.0).then_inc(border, 1)
        else:
            nc.gpsimd.tensor_copy(k.xin[:, :, 0:2, :], k.xin[:, :, TR:TR + 2, :]).then_inc(kept_rows, 1)
            if j == NT - 1:
                pool.wait_ge(kept_rows, 1)
                nc.gpsimd.memset(k.xin[:, :, TR + 1, :], 0.0).then_inc(border, 1)

    def tensor(pe):
        yield .02
        if j == 0:
            pe.wait_ge(loaded, 16)
        for m in range(ND):
            for kc in range(2):
                last = nc.tensor.matmul(bank[m][:, 0:n_tok], k.t["w_in"][:, kc, m * 128:m * 128 + 128],
                                        xp[:, kc, off:off + n_tok], start=kc == 0, stop=kc == 1)
            last.then_inc(in_mm, 1)
        yield .6
        for m in range(ND):
            pe.wait_ge(copied, m + 1)
            pe.wait_ge(u_done, m + 1)
            last = nc.tensor.matmul(bank[0][0:R + 2 * NS, 0:TT], k.t["w_xp"][:, m, :], k.u[:, m, :],
                                    start=m == 0, stop=m == ND - 1)
        last.then_inc(xp_mm, 1)
        yield .65
        pe.wait_ge(xp_done, 1)
        for m in range(ND):
            nc.tensor.matmul(dt_bank[m][:, 0:TT], k.t["w_dt"][:, m * 128:m * 128 + 128], k.xp[0:R, :],
                             start=True, stop=True).then_inc(dt_mm, 1)

    def scalar(act):
        for m in range(ND):
            yield .05 + .02 * m
            act.wait_ge(in_mm, m + 1)
            if m == 0 and j > 0:
                act.wait_ge(kept_rows, 1)
            if m == 0 and j == 0:
                act.wait_ge(border, 3)
            nc.scalar.activation(k.xin[:, m, at:at + rows, 1:W + 1],
                                 bank[m][:, 0:n_tok].rearrange("p (r c) -> p r c", c=W), ACT.Copy).then_inc(copied, 1)
        for m in range(ND):
            yield .55 + .01 * m
            act.wait_ge(conv, 8 * ND + m + 1)
            nc.scalar.activation(k.u[:, m, :], k.u[:, m, :], ACT.Silu).then_inc(u_done, 1)
        yield .62
        act.wait_ge(xp_mm, 1)
        nc.scalar.activation(k.xp[:], bank[0][0:R + 2 * NS, 0:TT], ACT.Copy).then_inc(xp_done, 1)
        yield .75
        act.wait_ge(biased, ND)
        nc.scalar.activation(k.delta[:], k.du[:], ACT.Abs).then_inc(soft, 1)
        act.wait_ge(soft, 1)
        nc.scalar.activation(k.delta[:], k.delta[:], ACT.Exp, scale=-1.0).then_inc(soft, 1)
        act.wait_ge(soft, 2)
        nc.scalar.activation(k.delta[:], k.delta[:], ACT.Ln, bias=1.0).then_inc(soft, 1)

    def vector(dve):
        for tap in range(9):
            dy, dx = divmod(tap, 3)
            for m in range(ND):
                yield .12 + .4 * tap / 9 + .01 * m
                src = k.xin[:, m, dy:dy + TR, dx:dx + W]
                acc = k.u[:, m, :].rearrange("p (r c) -> p r c", c=W)
                wt = k.t["conv_w"][:, m * 9 + tap:m * 9 + tap + 1]
                if tap == 0:
                    dve.wait_ge(copied, m + 1)
                    if m == 0 and j in (0, NT - 1):
                        dve.wait_ge(border, 4 if j == 0 else 1)
                    nc.vector.tensor_scalar(acc, src, wt, v[:, CONV_B, m:m + 1], ALU.mult, ALU.add).then_inc(conv, 1)
                else:
                    dve.wait_ge(conv, (tap - 1) * ND + m + 1)
                    nc.vector.scalar_tensor_tensor(acc, src, wt, acc, ALU.mult, ALU.add).then_inc(conv, 1)
        for m in range(ND):
            yield .68 + .02 * m
            dve.wait_ge(dt_mm, m + 1)
            nc.vector.tensor_scalar(k.du[:, m, :], dt_bank[m][:, 0:TT], v[:, DT_B, m:m + 1], None, ALU.add).then_inc(biased, 1)
        yield .9
        dve.wait_ge(biased, ND)
        dve.wait_ge(soft, 3)
        nc.vector.scalar_tensor_tensor(k.delta[:], k.du[:], 0.0, k.delta[:], ALU.max, ALU.add).then_inc(delta, 1)
        dve.wait_ge(delta, 1)
        dve.wait_ge(u_done, ND)
        nc.vector.tensor_tensor(k.du[:], k.delta[:], k.u[:], ALU.mult).then_inc(delta, 1)

    return dict(sync=sync, gpsimd=gpsimd, tensor=tensor, scalar=scalar, vector=vector)


def load_piece(k, sp, b, j, loaded):
    n = min(TT + W, L - TT * j)
    return sp.dma_start(k.xpc[:, j % 2, :, 0:n],
                        k.d["x"][b].rearrange("(a p) n -> p a n", p=96)[:, :, TT * j:TT * j + n]).then_inc(loaded, 16)


def scan(k, b, j):
    nc = k.nc
    loaded, bc_even, bc_odd, decay, inp, scanned, kept, times_c, added, summed = k.sems(10)
    N = NS // 2 * ND
    DG = 2
    END = N + 2.0
    bc_in = (bc_even, bc_odd)

    def sync(sp):
        for p in range(NS // 2):
            yield max(0, ND * (p - 1)) / END
            if p >= 2:
                sp.wait_ge(times_c, ND * (p - 1))
            src = k.d["bc"].rearrange("(a s) n -> a s n", a=2)[:, 2 * p:2 * p + 2, :].unsqueeze(0)
            sp.dma_start(k.bc[:, p % 2, :, :, :], src.to_broadcast([128, 2, 2, TT])).then_inc(bc_in[p % 2], 16)
            if p == 2 and j + 1 < NT:
                load_piece(k, sp, b, j + 1, loaded)
        yield 1
        if j + 1 < NT:
            sp.wait_ge(loaded, 16)

    def scalar(act):
        for g in range(0, N, DG):
            yield max(0, g - DG) / END
            if g >= 2 * ND:
                act.wait_ge(scanned, 2 * (g + DG - 2 * ND))
            for n in range(g, g + DG):
                p, m = divmod(n, ND)
                for sub in range(2):
                    at = m * NS + 2 * p + sub
                    nc.scalar.activation(k.a[:, n % (2 * ND), sub, :], k.delta[:, m, :], ACT.Exp,
                                         scale=k.A[:, at:at + 1]).then_inc(decay, 1)

    def vector(dve):
        def pair_sum(n):
            dve.wait_ge(times_c, n + 1)
            nc.vector.tensor_tensor(k.hw[:, n % 3, 0, :], k.hw[:, n % 3, 0, :], k.hw[:, n % 3, 1, :], ALU.add).then_inc(added, 1)

        for n in range(N):
            yield n / END
            p, m = divmod(n, ND)
            if m == 0:
                dve.wait_ge(bc_in[p % 2], 16 * (p // 2 + 1))
            if n >= 3:
                dve.wait_ge(summed, n - 2)
            nc.vector.tensor_tensor(k.hw[:, n % 3, :, :], k.du[:, m, :].unsqueeze(1).to_broadcast([128, 2, TT]),
                                    k.bc[:, p % 2, 0, :, :], ALU.mult).then_inc(inp, 1)
            dve.wait_ge(inp, n + 1)
            for sub in range(2):
                dve.wait_ge(decay, 2 * n + sub + 1)
                at = m * NS + 2 * p + sub
                nc.vector.tensor_tensor_scan(k.hw[:, n % 3, sub, :], k.a[:, n % (2 * ND), sub, :], k.hw[:, n % 3, sub, :],
                                             k.state[:, at:at + 1], ALU.mult, ALU.add).then_inc(scanned, 1)
            if n >= 1:
                yield (n + .2) / END
                pair_sum(n - 1)
        yield (N + .2) / END
        pair_sum(N - 1)

    def gpsimd(pool):
        for n in range(N):
            yield (n + .1) / END
            p, m = divmod(n, ND)
            if m == 0:
                pool.wait_ge(bc_in[p % 2], 16 * (p // 2 + 1))
            pool.wait_ge(scanned, 2 * n + 2)
            nc.gpsimd.tensor_copy(k.state[:, m * NS + 2 * p:m * NS + 2 * p + 2], k.hw[:, n % 3, :, TT - 1]).then_inc(kept, 1)
            pool.wait_ge(kept, n + 1)
            nc.gpsimd.tensor_tensor(k.hw[:, n % 3, :, :], k.hw[:, n % 3, :, :], k.bc[:, p % 2, 1, :, :],
                                    ALU.mult).then_inc(times_c, 1)

    def tensor(pe):
        for n in range(N):
            yield (n + 1.5) / END
            p, m = divmod(n, ND)
            pe.wait_ge(added, n + 1)
            nc.tensor.matmul(k.P[:, 5 + m, 0:TT], k.t["ident"][:], k.hw[:, n % 3, 0, :],
                             start=p == 0, stop=p == NS // 2 - 1).then_inc(summed, 1)

    return dict(sync=sync, gpsimd=gpsimd, tensor=tensor, scalar=scalar, vector=vector)


def finish(k, j):
    nc, v = k.nc, k.t["vec384"]
    (y_done, z_mm, z_done, ysum, mean_mm, cent, sq, sqsum, var_mm, root, rstd, norm, gate, out_mm, out,
     stored) = k.sems(16)
    y3 = k.y.rearrange("p (a n) -> p a n", a=ND)
    tot = k.tot
    fo = k.fo

    def vector(dve):
        for m in range(ND):
            yield .01 * m
            nc.vector.scalar_tensor_tensor(y3[:, m, :], k.u[:, m, :], v[:, D_PAR, m:m + 1], k.P[:, 5 + m, 0:TT],
                                           ALU.mult, ALU.add).then_inc(y_done, 1)
        yield .05
        dve.wait_ge(y_done, ND)
        nc.vector.tensor_tensor(tot, y3[:, 0, :], y3[:, 1, :], ALU.add).then_inc(ysum, 1)
        dve.wait_ge(ysum, 1)
        nc.vector.tensor_tensor(tot, tot, y3[:, 2, :], ALU.add).then_inc(ysum, 1)
        for m in range(ND):
            yield .2 + .02 * m
            dve.wait_ge(mean_mm, 1)
            nc.vector.tensor_tensor(y3[:, m, :], y3[:, m, :], k.P[:, 5, 0:TT], ALU.subtract).then_inc(cent, 1)
        yield .4
        dve.wait_ge(sq, ND)
        nc.vector.tensor_tensor(tot, k.delta[:, 0, :], k.delta[:, 1, :], ALU.add).then_inc(sqsum, 1)
        dve.wait_ge(sqsum, 1)
        nc.vector.tensor_tensor(tot, tot, k.delta[:, 2, :], ALU.add).then_inc(sqsum, 1)
        yield .6
        dve.wait_ge(root, 1)
        nc.vector.reciprocal(k.rstd, k.rstd).then_inc(rstd, 1)
        for m in range(ND):
            yield .65 + .03 * m
            if m == 0:
                dve.wait_ge(rstd, 1)
                dve.wait_ge(cent, ND)
                dve.wait_ge(z_done, ND)
            nc.vector.tensor_tensor(y3[:, m, :], y3[:, m, :], k.rstd, ALU.mult).then_inc(norm, 1)
            dve.wait_ge(norm, 2 * m + 1)
            nc.vector.tensor_scalar(y3[:, m, :], y3[:, m, :], v[:, LN_G, m:m + 1], v[:, LN_B, m:m + 1],
                                    ALU.mult, ALU.add).then_inc(norm, 1)
            dve.wait_ge(norm, 2 * m + 2)
            nc.vector.tensor_tensor(y3[:, m, :], y3[:, m, :], k.sz[:, m, :], ALU.mult).then_inc(gate, 1)

    def tensor(pe):
        for m in range(ND):
            yield .02 + .01 * m
            pe.wait_ge(y_done, m + 1)
            for kc in range(2):
                last = nc.tensor.matmul(k.P[:, 5 + m, 0:TT], k.t["w_in"][:, kc, DI + m * 128:DI + m * 128 + 128],
                                        k.xpc[:, j % 2, kc, 0:TT], start=kc == 0, stop=kc == 1)
            last.then_inc(z_mm, 1)
        yield .15
        pe.wait_ge(z_done, 1)
        pe.wait_ge(ysum, 2)
        nc.tensor.matmul(k.P[:, 5, 0:TT], k.ones[:], tot, start=True, stop=True).then_inc(mean_mm, 1)
        yield .45
        pe.wait_ge(sqsum, 2)
        pe.wait_ge(z_done, 2)
        nc.tensor.matmul(k.P[:, 6, 0:TT], k.ones[:], tot, start=True, stop=True).then_inc(var_mm, 1)
        yield .75
        pe.wait_ge(gate, ND)
        pe.wait_ge(cent, ND)
        for mo in range(2):
            for m in range(ND):
                last = nc.tensor.matmul(k.P[0:96, (7, 5)[mo], 0:TT], k.w_of[:, m, mo * 96:mo * 96 + 96], y3[:, m, :],
                                        start=m == 0, stop=m == ND - 1)
            last.then_inc(out_mm, 1)

    def scalar(act):
        for m in range(ND):
            yield .06 + .02 * m
            act.wait_ge(z_mm, m + 1)
            nc.scalar.activation(k.sz[:, m, :], k.P[:, 5 + m, 0:TT], ACT.Silu).then_inc(z_done, 1)
        for m in range(ND):
            yield .25 + .03 * m
            act.wait_ge(cent, m + 1)
            nc.scalar.activation(k.delta[:, m, :], y3[:, m, :], ACT.Square).then_inc(sq, 1)
        yield .5
        act.wait_ge(var_mm, 1)
        nc.scalar.activation(k.rstd, k.P[:, 6, 0:TT], ACT.Sqrt, bias=k.eps[:]).then_inc(root, 1)
        for mo in range(2):
            yield .85 + .05 * mo
            act.wait_ge(out_mm, mo + 1)
            nc.scalar.activation(fo[:, mo, :], k.P[0:96, (7, 5)[mo], 0:TT], ACT.Identity,
                                 bias=k.t["vec192"][:, 0, mo:mo + 1]).then_inc(out, 1)

    def sync(sp):
        yield .95
        sp.wait_ge(out, 2)
        sp.dma_start(k.d["fused"][:, :, TT * j:TT * j + TT], fo).then_inc(stored, 16)
        yield 1
        sp.wait_ge(stored, 16)

    return dict(sync=sync, tensor=tensor, scalar=scalar, vector=vector)



def instance_norm_and_conv(k, b):
    nc, t = k.nc, k.t
    loaded, st, root, x1, pooled, t_mm, tvec, w_mm, conv, own = k.sems(10)
    fused = k.fin

    def sync(sp):
        yield 0
        sp.dma_start(fused, k.d["fused"]).then_inc(loaded, 16)
        sp.dma_start(k.xres, k.d["x"][b].rearrange("(a p) n -> p a n", p=96)).then_inc(loaded, 16)

    def vector(dve):
        c = Tally(own)

        def link(ins):
            dve.wait_ge(own, c.inc(ins))

        yield 0
        c.inc(nc.vector.memset(k.x1p[:, :, 0, :], 0.0))
        c.inc(nc.vector.memset(k.x1p[:, :, 1:H + 1, 0], 0.0))
        c.inc(nc.vector.memset(k.x1p[:, :, 1:H + 1, W + 1], 0.0))
        dve.wait_ge(loaded, 32)
        for mo in range(2):
            for q in range(6):
                yield .05 + .01 * q
                c.inc(nc.vector.bn_stats(k.st[:, (mo * 6 + q) * 6:(mo * 6 + q) * 6 + 6], fused[:, mo, q * Q:q * Q + Q]))
        dve.wait_ge(own, c.n)
        for mo in range(2):
            c.inc(nc.vector.bn_aggr(k.mv[:, mo, :], k.st[:, mo * 36:mo * 36 + 36]))
        dve.wait_ge(own, c.n)
        nc.vector.tensor_copy(k.rs[:, 0:2], k.mv[:, 0:2, 1]).then_inc(st, 1)
        yield .2
        dve.wait_ge(root, 1)
        link(nc.vector.reciprocal(k.rs[:, 0:2], k.rs[:, 0:2]))
        for mo in range(2):
            c.inc(nc.vector.tensor_scalar(fused[:, mo, :], fused[:, mo, :], k.mv[:, mo, 0:1], k.rs[:, mo:mo + 1],
                                          ALU.subtract, ALU.mult))
        dve.wait_ge(own, c.n)
        for mo in range(2):
            yield .3
            nc.vector.tensor_tensor(k.x1p[:, mo, 1:H + 1, 1:W + 1], fused[:, mo, :].rearrange("p (r c) -> p r c", c=W),
                                    k.xres[:, mo, :].rearrange("p (r c) -> p r c", c=W), ALU.add).then_inc(x1, 1)
        yield .5
        dve.wait_ge(t_mm, 1)
        bn = t["bn"]
        link(nc.vector.tensor_scalar(k.tv[:], k.P[0:48, 0, 0:1], bn[:, 2:3], bn[:, 0:1], ALU.subtract, ALU.mult))
        link(nc.vector.tensor_scalar(k.tv[:], k.tv[:], k.bn_r[:, 0:1], bn[:, 1:2], ALU.mult, ALU.add))
        nc.vector.tensor_scalar(k.tv[:], k.tv[:], 0.0, None, ALU.max).then_inc(tvec, 1)
        dve.wait_ge(w_mm, 1)
        link(nc.vector.tensor_tensor(k.wts[:], k.P[0:96, 1, 0:8], t["b2"][:].rearrange("p a n -> p (a n)"), ALU.add))
        for tap, (dy, dx) in enumerate(((0, 0), (0, 1), (0, 2), (1, 0))):
            for mo in range(2):
                yield .55 + .1 * tap + .05 * mo
                src = k.x1p[:, mo, dy:dy + H, dx:dx + W]
                dst = k.x2[:, mo, :].rearrange("p (r c) -> p r c", c=W)
                wt = k.wts[:, mo * 4 + tap:mo * 4 + tap + 1]
                if tap == 0:
                    nc.vector.tensor_scalar(dst, src, wt, t["vec192"][:, 1, mo:mo + 1], ALU.mult, ALU.add).then_inc(conv, 1)
                    continue
                dve.wait_ge(conv, 2 * (tap - 1) + mo + 1)
                if tap < 3:
                    nc.vector.scalar_tensor_tensor(dst, src, wt, dst, ALU.mult, ALU.add).then_inc(conv, 1)
                    continue
                for a in range(2):
                    cols = slice(a * WH, a * WH + WH)
                    nc.vector.scalar_tensor_tensor(
                        k.x2t[:, mo, :, a * H:a * H + H].rearrange("p w h -> p h w"),
                        src[:, :, cols], wt, dst[:, :, cols], ALU.mult, ALU.add).then_inc(conv, 1)

    def scalar(act):
        yield .2
        act.wait_ge(st, 1)
        nc.scalar.activation(k.rs[:, 0:2], k.rs[:, 0:2], ACT.Sqrt, bias=k.eps[0:96, :]).then_inc(root, 1)
        for mo in range(2):
            yield .4
            act.wait_ge(x1, 2)
            if mo:
                act.wait_ge(pooled, 1)
            nc.scalar.activation(fused[:, 0, :].rearrange("p (r c) -> p r c", c=W), k.x1p[:, mo, 1:H + 1, 1:W + 1],
                                 ACT.Copy, scale=1.0 / L, accum_out=k.pool[:, mo:mo + 1]).then_inc(pooled, 1)

    def tensor(pe):
        yield .45
        pe.wait_ge(pooled, 2)
        for kc in range(2):
            last = nc.tensor.matmul(k.P[0:48, 0, 0:1], t["w1"][:, kc, :], k.pool[:, kc:kc + 1], start=kc == 0, stop=kc == 1)
        last.then_inc(t_mm, 1)
        yield .5
        pe.wait_ge(tvec, 1)
        for mo in range(2):
            for tap in range(4):
                last = nc.tensor.matmul(k.P[0:96, 1, mo * 4 + tap:mo * 4 + tap + 1], t["w2"][:, tap, mo * 96:mo * 96 + 96],
                                        k.tv[:], start=True, stop=True)
        last.then_inc(w_mm, 1)

    return dict(sync=sync, tensor=tensor, scalar=scalar, vector=vector)



def to_token_major(k):
    nc = k.nc
    tr, copied = k.sems(2)

    def tensor(pe):
        for n in range(WH // 2):
            yield n / 12
            if n >= 5:
                pe.wait_ge(copied, n - 4)
            for w in range(2):
                for kc in range(2):
                    last = nc.tensor.transpose(k.P[0:96, n % 5, w * C + kc * 96:w * C + kc * 96 + 96],
                                               k.x2t[:, kc, 2 * n + w, :], k.t["ident"][0:96, 0:96])
            last.then_inc(tr, 1)

    def scalar(act):
        for n in range(WH // 2):
            yield n / 12
            act.wait_ge(tr, n + 1)
            nc.scalar.activation(k.xT[:, 2 * n:2 * n + 2, :], k.P[0:96, n % 5, 0:2 * C].rearrange("p (w c) -> p w c", c=C),
                                 ACT.Copy).then_inc(copied, 1)

    return dict(tensor=tensor, scalar=scalar)


def layer_norm(k, src, dst, g, b, transposed=None, add_bias=None, store=None):
    nc, rows = k.nc, k.t["rows"]
    stat, aggr, root, rinv, norm, scaled, shifted, biased, tr, copied, stored = k.sems(11)
    half = WH // 2

    def row(i, n):
        return rows[:, i, :].unsqueeze(1).to_broadcast([96, n, C])

    def vector(dve):
        for w in range(WH):
            yield .01 * w
            nc.vector.bn_stats(k.st[:, w * 6:w * 6 + 6], src[:, w, :]).then_inc(stat, 1)
        yield .25
        for w in range(WH):
            dve.wait_ge(stat, w + 1)
            nc.vector.bn_aggr(k.mv[:, w, :], k.st[:, w * 6:w * 6 + 6]).then_inc(aggr, 1)
        yield .35
        dve.wait_ge(root, 1)
        nc.vector.reciprocal(k.rs[:], k.rs[:]).then_inc(rinv, 1)
        dve.wait_ge(rinv, 1)
        for j in range(4):
            yield .4 + .12 * j
            for w in range(6 * j, 6 * j + 6):
                nc.vector.tensor_scalar(dst[:, w, :], src[:, w, :], k.mv[:, w, 0:1], k.rs[:, w:w + 1],
                                        ALU.subtract, ALU.mult).then_inc(norm, 1)
            dve.wait_ge(norm, 6 * j + 6)
            part = dst[:, 6 * j:6 * j + 6, :]
            nc.vector.tensor_tensor(part, part, row(g, 6), ALU.mult).then_inc(scaled, 1)
            dve.wait_ge(scaled, j + 1)
            nc.vector.tensor_tensor(part, part, row(b, 6), ALU.add).then_inc(shifted, 1)

    def scalar(act):
        yield .3
        act.wait_ge(aggr, WH)
        nc.scalar.activation(k.rs[:], k.mv[:, :, 1], ACT.Sqrt, bias=k.eps[0:96, :]).then_inc(root, 1)
        if transposed is not None:
            for n in range(half):
                yield .5 + .04 * n
                act.wait_ge(tr, n + 1)
                nc.scalar.activation(transposed[:, :, 2 * n:2 * n + 2, :],
                                     k.P[0:96, n % 5, 0:2 * C].rearrange("p (a w n) -> p a w n", a=2, w=2),
                                     ACT.Copy).then_inc(copied, 1)

    def gpsimd(pool):
        for j in range(4):
            yield .5 + .12 * j
            pool.wait_ge(norm, 6 * j + 6)
            part = src[:, 6 * j:6 * j + 6, :]
            nc.gpsimd.tensor_tensor(part, part, row(add_bias, 6), ALU.add).then_inc(biased, 1)

    def sync(sp):
        yield .9
        sp.wait_ge(biased, 4)
        sp.dma_start(store, src).then_inc(stored, 16)
        yield 1
        sp.wait_ge(stored, 16)

    def tensor(pe):
        for n in range(half):
            yield .5 + .04 * n
            pe.wait_ge(shifted, n // 3 + 1)
            if n >= 5:
                pe.wait_ge(copied, n - 4)
            for kc in range(2):
                for w in range(2):
                    at = kc * C + w * 96
                    last = nc.tensor.transpose(k.P[0:96, n % 5, at:at + 96], dst[:, 2 * n + w, kc * 96:kc * 96 + 96],
                                               k.t["ident"][0:96, 0:96])
            last.then_inc(tr, 1)

    programs = dict(scalar=scalar, vector=vector)
    if transposed is not None:
        programs["tensor"] = tensor
    if add_bias is not None:
        programs["gpsimd"] = gpsimd
    if store is not None:
        programs["sync"] = sync
    return programs


def channel_mlp(k, src, res, out, w1, b1, w2, store=None):
    nc, t = k.nc, k.t
    up, act_done, down, added, stored = k.sems(5)
    NCH = 6
    END = NCH + .5

    def tensor(pe):
        def first(j):
            for m in range(NF):
                yield max(0, j - 1 + m / 12) / END
                n = j * NF + m
                if n >= 3:
                    pe.wait_ge(act_done, n - 2)
                for kc in range(2):
                    last = nc.tensor.matmul(k.P[:, n % 3, 0:Q], t[w1][:, kc, m * 128:m * 128 + 128],
                                            src[:, kc, 4 * j:4 * j + 4, :].rearrange("p w n -> p (w n)"),
                                            start=kc == 0, stop=kc == 1)
                last.then_inc(up, 1)

        def second(j):
            for w in range(4):
                yield (j + .5 + w / 8) / END
                pe.wait_ge(act_done, NF * (j + 1))
                n = 4 * j + w
                if n >= 2:
                    pe.wait_ge(added, n - 1)
                for m in range(NF):
                    last = nc.tensor.matmul(k.P[0:96, 3 + n % 2, 0:C], k.hid[:, j % 2, m, w * 96:w * 96 + 96],
                                            t[w2][:, m, :], start=m == 0, stop=m == NF - 1)
                last.then_inc(down, 1)

        yield from first(0)
        for j in range(NCH):
            if j + 1 < NCH:
                yield from first(j + 1)
            yield from second(j)

    def scalar(act):
        for j in range(NCH):
            for m in range(NF):
                yield max(0, j - 1 + (m + .5) / 12) / END
                if j >= 2 and m == 0:
                    act.wait_ge(down, 4 * (j - 1))
                n = j * NF + m
                act.wait_ge(up, n + 1)
                nc.scalar.activation(k.hid[:, j % 2, m, :], k.P[:, n % 3, 0:Q], ACT.Gelu,
                                     bias=t[b1][:, m:m + 1]).then_inc(act_done, 1)

    def vector(dve):
        for n in range(WH):
            yield (n // 4 + .5 + (n % 4 + 1) / 8) / END
            dve.wait_ge(down, n + 1)
            nc.vector.tensor_tensor(out[:, n, :], k.P[0:96, 3 + n % 2, 0:C], res[:, n, :], ALU.add).then_inc(added, 1)

    def sync(sp):
        for j in range(4):
            yield min(1, (6 * j + 8) / WH)
            sp.wait_ge(added, 6 * j + 6)
            sp.dma_start(store[:, 6 * j:6 * j + 6, :], out[:, 6 * j:6 * j + 6, :]).then_inc(stored, 16)
        sp.wait_ge(stored, 64)

    programs = dict(tensor=tensor, scalar=scalar, vector=vector)
    if store is not None:
        programs["sync"] = sync
    return programs



def rows_dft(k):
    nc = k.nc
    mm, copied, out, back, zero = k.sems(5)
    scr = k.d["spec_in"]

    def tensor(pe):
        for n in range(12):
            yield n / 24
            if n >= 5:
                pe.wait_ge(copied, n - 4)
            nc.tensor.matmul(k.P[0:96, n % 5, 0:Q], k.t["row_f"][:],
                             k.xn[:, 2 * n:2 * n + 2, :].rearrange("p w c -> p (w c)"), start=True, stop=True).then_inc(mm, 1)

    def scalar(act):
        for n in range(12):
            yield n / 24
            act.wait_ge(mm, n + 1)
            nc.scalar.activation(k.spec[:, n * Q:n * Q + Q], k.P[0:96, n % 5, 0:Q], ACT.Copy).then_inc(copied, 1)

    def vector(dve):
        yield .5
        dve.wait_ge(mm, 12)
        nc.vector.memset(k.Rb[:, 23 * C:25 * C], 0.0).then_inc(zero, 1)

    def sync(sp):
        for j in range(3):
            yield (4 * j + 4) / 24
            sp.wait_ge(copied, 4 * j + 4)
            for a in range(2):
                sp.dma_start(scr[:, a * WH + 8 * j:a * WH + 8 * j + 8, :],
                             k.spec[a * 48:a * 48 + 48, 8 * j * C:(8 * j + 8) * C].rearrange("p (w c) -> p w c", c=C)
                             ).then_inc(out, 16)
        yield .6
        sp.wait_ge(out, 96)
        sp.wait_ge(zero, 1)
        Rk = k.Rb.rearrange("p (k c) -> p k c", c=C)
        sp.dma_start(Rk[0:48, 0:23, :], scr[1:24].rearrange("k w c -> w k c")).then_inc(back, 16)
        sp.dma_start(Rk[48:96, 0:23, :], scr[25:48].rearrange("k w c -> w k c")).then_inc(back, 16)
        sp.dma_start(Rk[0:48, 23, :], scr[0]).then_inc(back, 16)
        sp.dma_start(Rk[0:48, 24, :], scr[24]).then_inc(back, 16)
        yield 1
        sp.wait_ge(back, 64)

    return dict(sync=sync, tensor=tensor, scalar=scalar, vector=vector)


CHUNKS = [(PAIR * j, PAIR, 2) for j in range(12)] + [(23 * C, 2 * C, 1)]


def frequencies(k, first, end):
    nc = k.nc
    hid_mm, gel, acc_mm, got = k.sems(4)
    chunks = CHUNKS[first:end]
    steps = [(j, s, g) for j, (_, _, ns) in enumerate(chunks) for s in range(ns) for g in range(GRP)]
    ends = {j: n for n, (j, _, _) in enumerate(steps)}
    END = len(steps) + 1.0
    NB = 4

    def tensor(pe):
        def hidden(n):
            j, s, g = steps[n]
            c0, cols, _ = chunks[j]
            if n >= 3:
                pe.wait_ge(gel, n - 2)
            nc.tensor.matmul(k.P[:, n % 3, 0:cols], k.G[:, s, g * 128:g * 128 + 128], k.Rb[:, c0:c0 + cols],
                             start=True, stop=True).then_inc(hid_mm, 1)

        yield 0
        hidden(0)
        hidden(1)
        for n, (j, s, g) in enumerate(steps):
            yield n / END
            if n + 2 < len(steps):
                hidden(n + 2)
            cols, ns = chunks[j][1:]
            pe.wait_ge(gel, n + 1)
            if j >= 2 and s == 0 and g == 0:
                pe.wait_ge(got, j - 1)
            nc.tensor.matmul(k.P[0:96, 3 + j % 2, 0:cols], k.V[:, s, g, :], k.fh[:, n % NB, 0:cols],
                             start=(s == 0 and g == 0), stop=(s == ns - 1 and g == GRP - 1)).then_inc(acc_mm, 1)

    def scalar(act):
        for n, (j, s, g) in enumerate(steps):
            yield max(0, n - 1) / END
            cols = chunks[j][1]
            act.wait_ge(hid_mm, n + 1)
            if n >= NB:
                act.wait_ge(acc_mm, n - NB + 1)
            nc.scalar.activation(k.fh[:, n % NB, 0:cols], k.P[:, n % 3, 0:cols], ACT.Gelu,
                                 bias=k.t["fc1b"][:, 0:1]).then_inc(gel, 1)

    def vector(dve):
        for j, (c0, cols, _) in enumerate(chunks):
            yield (ends[j] + .5) / END
            dve.wait_ge(acc_mm, ends[j] + 1)
            nc.vector.tensor_copy(k.spec[:, c0:c0 + cols], k.P[0:96, 3 + j % 2, 0:cols]).then_inc(got, 1)

    return dict(tensor=tensor, scalar=scalar, vector=vector)


def rows_inverse(k):
    nc = k.nc
    mm, added, fixed, out, back = k.sems(5)
    scr = k.d["spec_out"]

    def sync(sp):
        gk = k.spec.rearrange("p (k c) -> p k c", c=C)
        yield 0
        sp.dma_start(scr[1:24].rearrange("k w c -> w k c"), gk[0:48, 0:23, :]).then_inc(out, 16)
        sp.dma_start(scr[25:48].rearrange("k w c -> w k c"), gk[48:96, 0:23, :]).then_inc(out, 16)
        sp.dma_start(scr[0], gk[0:48, 23, :]).then_inc(out, 16)
        sp.dma_start(scr[24], gk[0:48, 24, :]).then_inc(out, 16)
        yield .3
        sp.wait_ge(out, 64)
        for a in range(2):
            sp.dma_start(k.back[a * 48:a * 48 + 48, :].rearrange("p (w c) -> p w c", c=C),
                         scr[:, a * WH:a * WH + WH, :]).then_inc(back, 16)

    def tensor(pe):
        for n in range(12):
            yield .5 + n / 24
            if n == 0:
                pe.wait_ge(back, 32)
            if n >= 5:
                pe.wait_ge(added, n - 4)
            nc.tensor.matmul(k.P[0:96, n % 5, 0:Q], k.t["row_i"][:], k.back[:, n * Q:n * Q + Q],
                             start=True, stop=True).then_inc(mm, 1)

    def vector(dve):
        for n in range(12):
            yield .5 + n / 24
            dve.wait_ge(mm, n + 1)
            part = k.xT[:, 2 * n:2 * n + 2, :].rearrange("p w c -> p (w c)")
            nc.vector.tensor_tensor(part, k.P[0:96, n % 5, 0:Q], part, ALU.add).then_inc(added, 1)
        dve.wait_ge(added, 1)
        nc.vector.tensor_scalar(k.xT[0:1, 0, :], k.xT[0:1, 0, :], k.t["fc2b"][:, 0:1], None, ALU.add).then_inc(fixed, 1)

    return dict(sync=sync, tensor=tensor, vector=vector)



def positions(t, half, i):
    ih, iw = divmod(i, WIN)
    return t[:, half, :, :].rearrange("p (b w) (a r h) -> p w h b a r", w=WIN, a=2, h=WIN)[:, iw, ih, :, :, :]


def sedenion(k, first, end):
    nc = k.nc
    loaded, neg, mm, gel = k.sems(4)
    sign = sedenion_signs()
    END = end - first + 1.5

    def sync(sp):
        if first == 0:
            yield 0
            for j in range(4):
                sp.dma_start(k.wsed[:, :, 4 * j:4 * j + 4, :], k.d["wsed"][:, :, 4 * j:4 * j + 4, :]).then_inc(loaded, 16)

    def vector(dve):
        if first == 0:
            for kc in range(2):
                yield 0
                nc.vector.tensor_scalar(k.cmn[:, kc, :, :], k.cm[:, kc, :, :], -1.0, None, ALU.mult).then_inc(neg, 1)

    def tensor(pe):
        for n in range(end - first):
            kk, mo = divmod(first + n, 2)
            for kc in range(2):
                for i in range(16):
                    if i % 4 == 0:
                        yield (n + kc / 2 + i / 32) / END
                    if n == 0 and kc == 0 and i == 0 and first == 0:
                        pe.wait_ge(loaded, 64)
                        pe.wait_ge(neg, 2)
                    if n >= 5 and kc == 0 and i == 0:
                        pe.wait_ge(gel, n - 4)
                    src = k.cm if sign[i][kk] > 0 else k.cmn
                    last = nc.tensor.matmul(k.P[0:96, n % 5, 0:NW].rearrange("p (b a r) -> p b a r", b=6, a=2),
                                            k.wsed[:, kc, i ^ kk, mo * 96:mo * 96 + 96],
                                            positions(src, kc, i), start=(kc == 0 and i == 0), stop=(kc == 1 and i == 15))
            last.then_inc(mm, 1)

    def scalar(act):
        for n in range(end - first):
            yield (n + 1.2) / END
            kk, mo = divmod(first + n, 2)
            act.wait_ge(mm, n + 1)
            nc.scalar.activation(positions(k.yg, mo, kk), k.P[0:96, n % 5, 0:NW].rearrange("p (b a r) -> p b a r", b=6, a=2),
                                 ACT.Gelu).then_inc(gel, 1)

    return dict(sync=sync, tensor=tensor, scalar=scalar, vector=vector)


def project(k):
    nc = k.nc
    loaded, pr_mm, added = k.sems(3)

    def sync(sp):
        yield 0
        sp.dma_start(k.res, k.d["resid"]).then_inc(loaded, 16)

    def tensor(pe):
        for n in range(WH):
            yield n / WH
            if n >= 5:
                pe.wait_ge(added, n - 4)
            for kc in range(2):
                last = nc.tensor.matmul(k.P[0:96, n % 5, 0:C], k.yg[:, kc, n, :], k.t["proj"][:, kc, :],
                                        start=kc == 0, stop=kc == 1)
            last.then_inc(pr_mm, 1)

    def vector(dve):
        for n in range(WH):
            yield n / WH
            if n == 0:
                dve.wait_ge(loaded, 16)
            dve.wait_ge(pr_mm, n + 1)
            nc.vector.tensor_tensor(k.xT[:, n, :], k.P[0:96, n % 5, 0:C], k.res[:, n, :], ALU.add).then_inc(added, 1)

    return dict(sync=sync, tensor=tensor, vector=vector)



def layer_0_alone(k, b):
    for j in range(NT):
        k.together(prepare(k, b, j))
        k.together(scan(k, b, j))
        k.together(finish(k, j))


def later_layers(k, b, nxt):
    def l0(stage, *args):
        return [] if nxt is None else [stage(k, *args)]

    both = k.together
    both(instance_norm_and_conv(k, b), *l0(prepare, nxt, 0))
    both(to_token_major(k))
    both(layer_norm(k, k.xT, k.xn, N1G, N1B))
    both(rows_dft(k))
    both(frequencies(k, 0, 6), *l0(scan, nxt, 0))
    both(frequencies(k, 6, 7), *l0(finish, 0))
    both(frequencies(k, 7, 8), *l0(prepare, nxt, 1))
    both(frequencies(k, 8, 13), *l0(scan, nxt, 1))
    both(rows_inverse(k), *l0(finish, 1))
    both(layer_norm(k, k.xT, k.xn, N2G, N2B, transposed=k.cm, add_bias=M2B), *l0(prepare, nxt, 2))
    both(channel_mlp(k, k.cm, k.xT, k.xT, "m1", "m1b", "m2"), *l0(scan, nxt, 2))
    both(layer_norm(k, k.xT, k.xn, L3N1G, L3N1B, transposed=k.cm, add_bias=PROJ_B, store=k.d["resid"]), *l0(finish, 2))
    both(sedenion(k, 0, 4), *l0(prepare, nxt, 3))
    both(sedenion(k, 4, 14), *l0(scan, nxt, 3))
    both(sedenion(k, 14, 17), *l0(finish, 3))
    both(sedenion(k, 17, 20), *l0(prepare, nxt, 4))
    both(sedenion(k, 20, 32), *l0(scan, nxt, 4))
    both(project(k), *l0(finish, 4))
    both(layer_norm(k, k.xT, k.xn, L3N2G, L3N2B, transposed=k.cm, add_bias=F2B), *l0(prepare, nxt, 5))
    both(channel_mlp(k, k.cm, k.xT, k.xn, "f1", "f1b", "f2", store=k.d["out"][b]), *l0(scan, nxt, 5))
    if nxt is not None:
        both(finish(k, 5))


def layers_kernel(nc, d, nb):
    with ExitStack() as ctx:
        k = Core(nc, ctx, d)
        k.t = {name: k.sb(name, shape) for name, shape in LOADS.items()}
        k.ones = k.sb("ones_over_di", [128, 128])
        k.eps = k.sb("eps", [128, 1])
        k.A = k.sb("A", [128, ND * NS])
        k.bn_r = k.sb("bn_rstd", [48, 1])
        k.G = k.sb("dft_fc1", [96, 2, GRP * 128])
        k.V = k.sb("fc2_idft", [128, 2, GRP, 96])
        k.w_of = k.sb("w_out_fuse", [128, ND, C])
        k.state = k.sb("state", [128, ND * NS])
        k.st = k.sb("bn_parts", [96, WH * 6])
        k.mv = k.sb("mean_var", [96, WH, 2])
        k.rs = k.sb("rstd_tok", [96, WH])
        k.pool = k.sb("pooled", [96, 2])
        k.tv = k.sb("t_vec", [48, 1])
        k.wts = k.sb("tap_weights", [96, 8])
        k.xpc = k.sb("x_piece", [96, 2, 2, TT + W])
        k.xin = k.sb("conv_in", [128, ND, TR + 2, W + 2])
        k.u, k.delta, k.du = (k.sb(n, [128, ND, TT]) for n in ("u", "delta", "delta_u"))
        k.xp = k.sb("x_proj", [R + 2 * NS, TT])
        a_all = k.sb("decay", [128, 12 * TT])
        hw_all = k.sb("scan_work", [128, 6 * TT])
        bc_all = k.sb("b_and_c", [128, 8 * TT])
        k.a = a_all[:].rearrange("p (r s n) -> p r s n", r=2 * ND, s=2)
        k.hw = hw_all[:].rearrange("p (r s n) -> p r s n", r=3, s=2)
        k.bc = bc_all[:].rearrange("p (r a s n) -> p r a s n", r=2, a=2, s=2)
        k.y = a_all[:, 0:3 * TT]
        k.rstd = a_all[:, 3 * TT:4 * TT]
        k.sz = a_all[:, 4 * TT:7 * TT].rearrange("p (a n) -> p a n", a=ND)
        k.tot = a_all[:, 7 * TT:8 * TT]
        k.fo = bc_all[0:96, 0:2 * TT].rearrange("p (a n) -> p a n", a=2)
        k.arena = ctx.enter_context(nc.sbuf_tensor("arena", [128, ARENA], F32))

        def part(parts, at, *shape):
            n = int(np.prod(shape))
            assert at + n <= ARENA
            v = k.arena[0:parts, at:at + n]
            if len(shape) == 1:
                return v
            names = "abcd"[:len(shape)]
            return v.rearrange(f"p ({' '.join(names)}) -> p {' '.join(names)}", **{c: s for c, s in zip(names, shape)})

        M = 2 * L
        k.fin = part(96, 0, 2, L)
        k.xres = part(96, M, 2, L)
        k.x2t = part(96, M, 2, WH, 96)
        k.x1p = part(96, 2 * M, 2, H + 1, W + 2)
        k.x2 = part(96, 2 * M + 4900, 2, L)
        k.xT = part(96, 0, WH, C)
        k.xn = part(96, M, WH, C)
        k.Rb = part(96, M, KH * C)
        k.spec = part(96, M + KH * C, KH * C)
        k.back = part(96, M, WH * C)
        k.fh = part(128, M + 2 * KH * C, 4, 2 * C)
        WS = 2 * 16 * C
        k.cm = part(96, WS + M, 2, WH, 96)
        k.hid = part(128, WS + 2 * M, 2, NF, Q)
        k.wsed = part(96, 0, 2, 16, C)
        k.yg = part(96, WS, 2, WH, 96)
        k.cmn = part(96, WS + 2 * M, 2, WH, 96)
        k.res = part(96, WS + 2 * M, WH, C)
        k.P = ctx.enter_context(nc.psum_tensor("psum", [128, 8, 512], F32))

        setup(k)
        layer_0_alone(k, 0)
        k.even()
        if nb > 1:
            with nc.Fori(0, nb - 1) as b:
                later_layers(k, b, b + 1)
                k.even()
        later_layers(k, nb - 1, None)


ARENA = 6144 + 3 * 4608


def laid_out(i):
    nb = i["x"].shape[0]

    def v384(v):
        return v.reshape(ND, 128).T

    def v192(v):
        return v.reshape(2, 96).T

    def halves(w):
        return w.reshape(2, 96, -1).transpose(1, 0, 2)

    def chunks(w):
        return w.reshape(-1, 128, w.shape[-1]).transpose(1, 0, 2)

    row_f, row_i, col, back, ident = dft_constants()
    rows = [i[n] for n in ("L2_conv_n1_g", "L2_conv_n1_b", "L2_conv_n2_g", "L2_conv_n2_b", "L2_conv_mlp2_b",
                           "L3_conv_norm1_g", "L3_conv_norm1_b", "L3_conv_norm2_g", "L3_conv_norm2_b",
                           "L3_conv_proj_b", "L3_conv_fc2_b")]
    out = dict(
        x=i["x"].reshape(nb, C, L),
        w_in=halves(i["L0_conv_in_proj_w"].T), conv_w=i["L0_conv_conv_w"].reshape(ND, 128, 9).transpose(1, 0, 2).reshape(128, 27),
        vec384=np.stack([v384(i["L0_conv_" + n]) for n in ("conv_b", "D_param", "ln_g", "ln_b", "dt_proj_b")], 1),
        a_log=i["L0_conv_A_log"].reshape(ND, 128, NS).transpose(1, 0, 2).reshape(128, ND * NS),
        w_xp=chunks(i["L0_conv_x_proj_w"].T), w_dt=i["L0_conv_dt_proj_w"].T,
        vec192=np.stack([v192(i["L0_conv_fuse_b"]), v192(i["L1_conv_bias"])], 1),
        w1=halves(i["L1_conv_w1"].T),
        bn=np.stack([i["L1_conv_" + n] for n in ("gamma", "beta", "running_mean", "running_var")], 1),
        w2=i["L1_conv_w2"].reshape(C, 9, 48)[:, :4].transpose(2, 1, 0),
        b2=i["L1_conv_b2"].reshape(2, 96, 9)[:, :, :4].transpose(1, 0, 2),
        fc1b=np.tile(i["L2_conv_fc1_b"], 8).reshape(128, 1), fc2v=np.tile(i["L2_conv_fc2_w"].T, (8, 1)),
        fc2b=i["L2_conv_fc2_b"][:1].reshape(1, 1),
        m1=halves(i["L2_conv_mlp1_w"].T), m1b=i["L2_conv_mlp1_b"].reshape(NF, 128).T, m2=chunks(i["L2_conv_mlp2_w"].T),
        rows=np.tile(np.stack(rows)[None], (96, 1, 1)),
        f1=halves(i["L3_conv_fc1_w"]), f1b=i["L3_conv_fc1_b"].reshape(NF, 128).T, f2=chunks(i["L3_conv_fc2_w"]),
        proj=halves(i["L3_conv_proj_w"]),
        out_w=halves(i["L0_conv_out_proj_w"]), fuse_w=halves(i["L0_conv_fuse_w"].reshape(C, C).T),
        fc1w=np.tile(i["L2_conv_fc1_w"].T[None], (96, 1, 1)),
        wsed=i["L3_conv_w_sed"].reshape(16, 2, 96, C).transpose(2, 1, 0, 3),
        row_f=row_f, row_i=row_i, col=col, back=back, ident=ident)
    return {n: np.ascontiguousarray(v) for n, v in out.items()}


def kernel(**inputs):
    import concourse.bacc as bacc
    from concourse.bass_utils import run_bass_kernel_spmd

    arrays = laid_out({n: np.asarray(v) for n, v in inputs.items()})
    nb = arrays["x"].shape[0]
    nc = bacc.Bacc("TRN2", target_bir_lowering=False, num_devices=1)
    d = {n: nc.dram_tensor("in_" + n, a.shape, F32, kind="ExternalInput").ap() for n, a in arrays.items()}
    d["out"] = nc.dram_tensor("out", (nb, 96, WH, C), F32, kind="ExternalOutput").ap()
    d["bc"] = nc.dram_tensor("bc_scratch", (2 * NS, TT), F32, kind="Internal").ap()
    d["fused"] = nc.dram_tensor("fused_scratch", (96, 2, L), F32, kind="Internal").ap()
    d["resid"] = nc.dram_tensor("residual_scratch", (96, WH, C), F32, kind="Internal").ap()
    d["spec_in"] = nc.dram_tensor("spec_in_scratch", (48, 48, C), F32, kind="Internal").ap()
    d["spec_out"] = nc.dram_tensor("spec_out_scratch", (48, 48, C), F32, kind="Internal").ap()
    layers_kernel(nc, d, nb)
    r = run_bass_kernel_spmd(nc, [{"in_" + n: a for n, a in arrays.items()}], core_ids=[0])
    got = np.asarray(r.results[0]["out"])
    return got.reshape(nb, 2, 48, WH, C).transpose(0, 4, 2, 1, 3).reshape(nb, C, H, W)
```

```python
from contextlib import ExitStack

import numpy as np
import concourse.bass as bass
from concourse import mybir

F32 = mybir.dt.float32
ALU = mybir.AluOpType
ACT = mybir.ActivationFunctionType
AXX = mybir.AxisListType.X

H = W = 48
L = H * W
C = 192
CH = 96
DI = 384
ND = DI // 128
NS = 16
R = 12
FF = 768
NF = FF // 128
Q = 384
TR = 8
TT = TR * W
NT = H // TR
WH = 24
KH = 25
GRP = 6
HID = 16
PAIR = 23 * C // 12
WIN = 4
NW = (H // WIN) * (W // WIN)
EPS = 1e-5


def merged(programs):
    heads = []
    for n, p in enumerate(programs):
        due = next(p, None)
        if due is not None:
            heads.append((due, n, p))
    while heads:
        due, n, p = min(heads, key=lambda h: h[:2])
        heads.remove((due, n, p))
        yield due
        due_next = next(p, None)
        if due_next is not None:
            heads.append((max(due, due_next), n, p))


def in_turn(programs):
    for _ in merged(programs):
        pass


class Tally:

    def __init__(self, sem):
        self.sem, self.n = sem, 0

    def inc(self, ins):
        self.n += 1
        ins.then_inc(self.sem, 1)
        return self.n


def sedenion_signs():
    def conj(x):
        if len(x) == 1:
            return x
        h = len(x) // 2
        return np.concatenate([conj(x[:h]), -x[h:]])

    def mult(a, b):
        if len(a) == 1:
            return a * b
        h = len(a) // 2
        a1, a2, b1, b2 = a[:h], a[h:], b[:h], b[h:]
        return np.concatenate([mult(a1, b1) - mult(conj(b2), a2), mult(b2, a1) + mult(a2, conj(b1))])

    eye = np.eye(16)
    return [[int(mult(eye[i], eye[i ^ k])[k]) for k in range(16)] for i in range(16)]


def dft_constants():
    n = np.arange(48)
    cos = np.cos(2 * np.pi * np.outer(n, n) / 48)
    sin = np.sin(2 * np.pi * np.outer(n, n) / 48)
    fwd = np.concatenate([cos[:KH], -sin[1:24]]) / 48.0
    inv = np.concatenate([cos[:KH], -sin[1:24]]) / 48.0
    row_f = np.zeros((96, 96))
    row_i = np.zeros((96, 96))
    for a in range(2):
        row_f[a * 48:a * 48 + 48, a * 48:a * 48 + 48] = fwd.T
        row_i[a * 48:a * 48 + 48, a * 48:a * 48 + 48] = inv
    col = np.stack([np.concatenate([cos, sin]), np.concatenate([-sin, cos]),
                    np.concatenate([cos, -sin]), np.concatenate([-sin, -cos])], 1)
    back = np.stack([np.concatenate([cos, sin], 1), np.concatenate([-sin, cos], 1),
                     np.concatenate([cos, -sin], 1), np.concatenate([-sin, -cos], 1)], 1)
    back = back.reshape(GRP, 8, 1, 4, 96).repeat(HID, 2).reshape(GRP, 128, 4, 96).transpose(1, 2, 0, 3)
    return (row_f.astype(np.float32), row_i.astype(np.float32), col.astype(np.float32),
            np.ascontiguousarray(back).astype(np.float32), np.eye(128, dtype=np.float32))


class Core:

    POOL = 78

    def __init__(self, nc, ctx, d):
        self.nc, self.ctx, self.d = nc, ctx, d
        self.pools = [[ctx.enter_context(nc.semaphore(f"pool{p}_{n}")) for n in range(self.POOL)] for p in range(2)]
        self.parity = 0
        self.used = 0

    def sb(self, name, shape):
        return self.ctx.enter_context(self.nc.sbuf_tensor(name, shape, F32))

    def sems(self, n):
        self.used += n
        return self.pools[self.parity][self.used - n:self.used]

    def in_sequence(self, shares, *stages):
        through, = self.sems(1)
        names = [name for name in ("sync", "tensor", "vector", "scalar", "gpsimd") if any(name in st for st in stages)]
        starts = [sum(shares[:n + 1]) / sum(shares) for n in range(len(stages) + 1)]

        def program(name):
            def steps(eng):
                for n, st in enumerate(stages):
                    if name in st:
                        for due in st[name](eng):
                            yield starts[n] + (starts[n + 1] - starts[n]) * due
                    if n + 1 < len(stages):
                        yield starts[n + 1]
                        eng.drain().then_inc(through, 1)
                        eng.wait_ge(through, len(names) * (n + 1))
            return steps

        return {name: program(name) for name in names}

    def together(self, *stages):
        other = [s.num for s in self.pools[1 - self.parity]]
        with self.nc.Block() as block:
            @block.sync
            def _(sp):
                sp.sem_clear(range(other[0], other[-1] + 1))
                in_turn([st["sync"](sp) for st in stages if "sync" in st])

            @block.tensor
            def _(pe):
                in_turn([st["tensor"](pe) for st in stages if "tensor" in st])

            @block.vector
            def _(dve):
                in_turn([st["vector"](dve) for st in stages if "vector" in st])

            @block.scalar
            def _(act):
                in_turn([st["scalar"](act) for st in stages if "scalar" in st])

            @block.gpsimd
            def _(pool):
                in_turn([st["gpsimd"](pool) for st in stages if "gpsimd" in st])
        self.parity ^= 1
        self.used = 0

    def even(self):
        if self.parity:
            self.together()



LOADS = dict(w_in=[96, 2, 768], conv_w=[128, ND * 9], vec384=[128, 5, ND], a_log=[128, ND * NS],
             w_xp=[128, ND, R + 2 * NS], w_dt=[R, DI], vec192=[96, 2, 2], w1=[96, 2, 48], bn=[48, 4],
             w2=[48, 4, C], b2=[96, 2, 4], fc1b=[128, 1], fc2v=[128, 2], fc2b=[1, 1],
             m1=[96, 2, FF], m1b=[128, NF], m2=[128, NF, C], rows=[96, 5, C], lnv=[96, 6, 2], signs=[96, 16, 16], f1=[96, 2, FF], f1b=[128, NF],
             f2=[128, NF, C], proj=[96, 2, C], row_f=[96, 96], row_i=[96, 96], ident=[128, 128])
CONV_B, D_PAR, LN_G, LN_B, DT_B = range(5)
N1G, N1B, M2B, PROJ_B, F2B = range(5)
N2G, N2B, L3N1G, L3N1B, L3N2G, L3N2B = range(6)


FIRST = ("w_in", "conv_w", "vec384", "a_log", "w_xp", "w_dt", "ident")


def setup_layer_0(k):
    nc, d = k.nc, k.d
    loaded, built, a_exp, a_done = k.sems(4)

    def sync(sp):
        yield 0
        for name in FIRST:
            sp.dma_start(k.t[name][:], d[name]).then_inc(loaded, 16)
        yield 1
        sp.wait_ge(loaded, 16 * len(FIRST))

    def gpsimd(pool):
        yield 0
        nc.gpsimd.memset(k.ones[:], 1.0 / DI).then_inc(built, 1)
        nc.gpsimd.memset(k.eps[:], EPS).then_inc(built, 1)

    def scalar(act):
        yield .9
        act.wait_ge(loaded, 16 * len(FIRST))
        nc.scalar.activation(k.A[:], k.t["a_log"][:], ACT.Exp).then_inc(a_exp, 1)

    def vector(dve):
        yield .95
        dve.wait_ge(a_exp, 1)
        nc.vector.tensor_scalar(k.A[:], k.A[:], -1.0, None, ALU.mult).then_inc(a_done, 1)
        for tap in range(9):
            nc.vector.tensor_scalar(k.conv_diag[:, tap, :], k.t["ident"][:], k.t["conv_w"][:, (ND - 1) * 9 + tap:(ND - 1) * 9 + tap + 1],
                                    None, ALU.mult).then_inc(a_done, 1)

    return dict(sync=sync, gpsimd=gpsimd, scalar=scalar, vector=vector)


def setup_weights(k):
    nc, d = k.nc, k.d
    loaded, tmp_s, mm, rooted, b_mm = k.sems(5)
    late = ("out_w", "fuse_w", "fc1w", "col", "back")
    ar = k.arena
    out_w = ar[0:96, 0:768].rearrange("p (a n) -> p a n", a=2)
    fuse_w = ar[0:96, 768:1152].rearrange("p (a n) -> p a n", a=2)
    fc1w = ar[0:96, 1152:1184].rearrange("p (a n) -> p a n", a=2)
    col = ar[0:96, 1184:1376].rearrange("p (a n) -> p a n", a=4)
    back = ar[:, 1376:1376 + 2304].rearrange("p (s g n) -> p s g n", s=4, g=GRP)
    tmp = ar[:, 4096:4864]
    tmp2 = ar[:, 4864:5632]
    rest = [name for name in LOADS if name not in FIRST]
    n_load = len(rest) + len(late)

    def sync(sp):
        yield .02
        for name in rest:
            sp.dma_start(k.t[name][:], d[name]).then_inc(loaded, 16)
        for name, to in zip(late, (out_w, fuse_w, fc1w, col, back)):
            sp.dma_start(to, d[name]).then_inc(loaded, 16)

    def scalar(act):
        yield .5
        act.wait_ge(loaded, 16 * n_load)
        nc.scalar.activation(k.bn_r[:], k.t["bn"][:, 3:4], ACT.Sqrt, bias=k.eps[0:48, :]).then_inc(rooted, 1)

    def vector(dve):
        own = Tally(tmp_s)

        def link(ins):
            dve.wait_ge(tmp_s, own.inc(ins))

        yield .55
        dve.wait_ge(rooted, 1)
        dve.wait_ge(loaded, 16 * n_load)
        link(nc.vector.reciprocal(k.bn_r[:], k.bn_r[:]))
        for s in range(2):
            yield .6
            for part, to in ((0, tmp), (1, tmp2)):
                own.inc(nc.vector.tensor_tensor(
                    to[0:96, :].rearrange("p (n k) -> p n k", k=HID),
                    col[:, 2 * s + part, :].unsqueeze(2).to_broadcast([96, 48, HID]),
                    fc1w[:, part, :].unsqueeze(1).to_broadcast([96, 48, HID]), ALU.mult))
            dve.wait_ge(tmp_s, own.n)
            link(nc.vector.tensor_tensor(k.G[:, s, :], tmp[0:96, :], tmp2[0:96, :], ALU.add))
        for s in range(2):
            yield .7
            link(nc.vector.tensor_scalar(tmp[:, 0:576], back[:, 2 * s, :, :].rearrange("p g n -> p (g n)"),
                                         k.t["fc2v"][:, 0:1], None, ALU.mult))
            link(nc.vector.scalar_tensor_tensor(
                k.V[:, s, :, :].rearrange("p g n -> p (g n)"), back[:, 2 * s + 1, :, :].rearrange("p g n -> p (g n)"),
                k.t["fc2v"][:, 1:2], tmp[:, 0:576], ALU.mult, ALU.add))
        yield .8
        link(nc.vector.tensor_scalar(k.t["fc2b"][:], k.t["fc2b"][:], 48.0, None, ALU.mult))
        dve.wait_ge(mm, ND)
        link(nc.vector.tensor_copy(k.w_of[:], k.P[:, 0:ND, 0:C]))
        dve.wait_ge(b_mm, 1)
        for m, (name, row) in enumerate((("m1b", 0), ("f1b", 8))):
            link(nc.vector.tensor_tensor(k.t[name][:], k.t[name][:], k.P[:, 4, row:row + NF], ALU.add))
        for kc in range(2):
            for w, g in ((k.t["m1"][:, kc, :], N2G), (k.t["f1"][:, kc, :], L3N2G)):
                link(nc.vector.tensor_scalar(w, w, k.t["lnv"][:, g, kc:kc + 1], None, ALU.mult))

    def tensor(pe):
        yield .5
        pe.wait_ge(loaded, 16 * n_load)
        for m in range(ND):
            for kc in range(2):
                last = nc.tensor.matmul(k.P[:, m, 0:C], out_w[:, kc, m * 128:m * 128 + 128], fuse_w[:, kc, :],
                                        start=kc == 0, stop=kc == 1)
            last.then_inc(mm, 1)
        for w, b, at in (("m1", N2B, 0), ("f1", L3N2B, 8)):
            for m in range(NF):
                for kc in range(2):
                    last = nc.tensor.matmul(k.P[:, 4, at + m:at + m + 1], k.t[w][:, kc, m * 128:m * 128 + 128],
                                            k.t["lnv"][:, b, kc:kc + 1], start=kc == 0, stop=kc == 1)
        last.then_inc(b_mm, 1)

    return dict(sync=sync, scalar=scalar, vector=vector, tensor=tensor)


def setup_sedenion(k):
    nc, d = k.nc, k.d
    loaded, w_ready, b_mm, tmp_s, stored = k.sems(5)
    ar = k.arena
    ws = ar[0:96, 5632:5632 + 6144].rearrange("p (a j n) -> p a j n", a=2, j=16)
    ws2 = ar[0:96, 11776:11776 + 6144].rearrange("p (a j n) -> p a j n", a=2, j=16)
    prod = ar[0:96, 17920:18176].rearrange("p (k j) -> p k j", k=16)

    def sync(sp):
        yield 0
        sp.dma_start(ws, d["wsed"]).then_inc(loaded, 16)
        yield .4
        sp.wait_ge(w_ready, 1)
        sp.dma_start(d["w_minus"], ws2).then_inc(stored, 16)
        yield .95
        sp.wait_ge(w_ready, 2)
        sp.dma_start(d["w_hat"], ws).then_inc(stored, 16)
        yield 1
        sp.wait_ge(stored, 32)

    def vector(dve):
        own = Tally(tmp_s)

        def link(ins):
            dve.wait_ge(tmp_s, own.inc(ins))

        for mo in range(2):
            yield .3
            dve.wait_ge(b_mm, 1)
            v = k.P[0:96, 3, mo * 16:mo * 16 + 16].unsqueeze(1).to_broadcast([96, 16, 16])
            link(nc.vector.tensor_tensor(prod, k.t["signs"][:], v, ALU.mult))
            link(nc.vector.tensor_reduce(k.sed_b[:, mo * 16:mo * 16 + 16], prod, AXX, ALU.add))
        for kc in range(2):
            yield .3
            link(nc.vector.tensor_scalar(ws[:, kc, :, :], ws[:, kc, :, :], k.t["lnv"][:, L3N1G, kc:kc + 1], None, ALU.mult))
        yield .35
        nc.vector.tensor_scalar(ws2, ws, -2.0, None, ALU.mult).then_inc(w_ready, 1)
        path = (ws, ws2, ws, ws2, ws)
        for n in range(4):
            for kc in range(2):
                def half(t, h):
                    return t[:, kc, :, :].rearrange("p (m b l) n -> p m b (l n)", b=2, l=1 << n)[:, :, h, :]
                for op, h in ((ALU.add, 0), (ALU.subtract, 1)):
                    yield .6 + .08 * n
                    if n == 0 and kc == 0 and h == 0:
                        dve.wait_ge(stored, 16)
                    link(nc.vector.tensor_tensor(half(path[n + 1], h), half(path[n], 0), half(path[n], 1), op))
        yield .92
        nc.vector.tensor_scalar(ws, ws, 1.0 / 16, None, ALU.mult).then_inc(w_ready, 1)

    def tensor(pe):
        for mo in range(2):
            for j in range(16):
                yield .25
                if mo == 0 and j == 0:
                    pe.wait_ge(loaded, 16)
                for kc in range(2):
                    last = nc.tensor.matmul(k.P[0:96, 3, mo * 16 + j:mo * 16 + j + 1], ws[:, kc, j, mo * 96:mo * 96 + 96],
                                            k.t["lnv"][:, L3N1B, kc:kc + 1], start=kc == 0, stop=kc == 1)
        last.then_inc(b_mm, 1)

    return dict(sync=sync, vector=vector, tensor=tensor)



class PieceMemory:

    def __init__(self, loads_ahead, conv_shared, pe_sums, **parts):
        self.loads_ahead, self.conv_shared, self.pe_sums = loads_ahead, conv_shared, pe_sums
        self.x, self.u, self.delta, self.du, self.bc, self.banks = (parts[n] for n in ("x", "u", "delta", "du", "bc", "banks"))
        self.y, self.rstd, self.sz, self.tot, self.fo = (parts[n] for n in ("y", "rstd", "sz", "tot", "fo"))
        self.next = None


def prepare(k, b, j, mem):
    nc, v = k.nc, k.t["vec384"]
    (loaded, kept_rows, border, in_mm, copied, conv, conv_pe, u_done, xp_mm, xp_done, dt_mm, soft, bc_out,
     delta) = k.sems(14)
    n_dve = ND - 1 if mem.conv_shared else ND
    at = 1 if j == 0 else 2
    row0 = 0 if j == 0 else TR * j + 1
    rows = min(TR * j + TR + 1, H) - row0
    n_tok = rows * W
    off = (row0 - TR * j) * W
    bank = mem.banks
    dt_bank = [bank[(m + 1) % 3] for m in range(ND)]

    def sync(sp):
        if mem.loads_ahead == 0 or j == 0:
            yield 0
            load_piece(k, sp, b, j, mem, loaded)
        yield .6
        sp.wait_ge(xp_done, 1)
        sp.dma_start(mem.bc, k.xp[R:R + 2 * NS, :]).then_inc(bc_out, 16)
        yield 1
        sp.wait_ge(bc_out, 16)

    def gpsimd(pool):
        yield 0
        if j == 0:
            nc.gpsimd.memset(k.xin[:, :, 0, 1:W + 1], 0.0).then_inc(border, 1)
            nc.gpsimd.memset(k.xin[:, :, :, 0], 0.0).then_inc(border, 1)
            nc.gpsimd.memset(k.xin[:, :, :, W + 1], 0.0).then_inc(border, 1)
            nc.gpsimd.memset(k.state[:], 0.0).then_inc(border, 1)
        else:
            nc.gpsimd.tensor_copy(k.xin[:, :, 0:2, :], k.xin[:, :, TR:TR + 2, :]).then_inc(kept_rows, 1)
            if j == NT - 1:
                pool.wait_ge(kept_rows, 1)
                nc.gpsimd.memset(k.xin[:, :, TR + 1, :], 0.0).then_inc(border, 1)

    def tensor(pe):
        yield .02
        if mem.loads_ahead == 0 or j == 0:
            pe.wait_ge(loaded, 16)
        for m in range(ND):
            for kc in range(2):
                last = nc.tensor.matmul(bank[m][:, 0:n_tok], k.t["w_in"][:, kc, m * 128:m * 128 + 128],
                                        mem.x[:, kc, off:off + n_tok], start=kc == 0, stop=kc == 1)
            last.then_inc(in_mm, 1)
        for tap in range(9 if mem.conv_shared else 0):
            yield .12 + .3 * tap / 9
            if tap == 0:
                pe.wait_ge(copied, ND)
                if j in (0, NT - 1):
                    pe.wait_ge(border, 4 if j == 0 else 1)
            dy, dx = divmod(tap, 3)
            last = nc.tensor.matmul(bank[ND - 1][:, 0:TT].rearrange("p (r c) -> p r c", c=W), k.conv_diag[:, tap, :],
                                    k.xin[:, ND - 1, dy:dy + TR, dx:dx + W], start=tap == 0, stop=tap == 8)
            if tap == 8:
                last.then_inc(conv_pe, 1)
        yield .6
        for m in range(ND):
            pe.wait_ge(copied, m + 1)
            pe.wait_ge(u_done, min(ND, m + 1 + ND - n_dve))
            last = nc.tensor.matmul(bank[0][0:R + 2 * NS, 0:TT], k.t["w_xp"][:, m, :], mem.u[:, m, :],
                                    start=m == 0, stop=m == ND - 1)
        last.then_inc(xp_mm, 1)
        yield .65
        pe.wait_ge(xp_done, 1)
        for m in range(ND):
            nc.tensor.matmul(dt_bank[m][:, 0:TT], k.t["w_dt"][:, m * 128:m * 128 + 128], k.xp[0:R, :],
                             start=True, stop=True).then_inc(dt_mm, 1)

    def scalar(act):
        for m in range(ND):
            yield .05 + .02 * m
            act.wait_ge(in_mm, m + 1)
            if m == 0 and j > 0:
                act.wait_ge(kept_rows, 1)
            if m == 0 and j == 0:
                act.wait_ge(border, 3)
            nc.scalar.activation(k.xin[:, m, at:at + rows, 1:W + 1],
                                 bank[m][:, 0:n_tok].rearrange("p (r c) -> p r c", c=W), ACT.Copy).then_inc(copied, 1)
        if mem.conv_shared:
            yield .5
            act.wait_ge(conv_pe, 1)
            nc.scalar.activation(mem.u[:, ND - 1, :], bank[ND - 1][:, 0:TT], ACT.Silu,
                                 bias=v[:, CONV_B, ND - 1:ND]).then_inc(u_done, 1)
        for m in range(n_dve):
            yield .55 + .01 * m
            act.wait_ge(conv, 8 * n_dve + m + 1)
            nc.scalar.activation(mem.u[:, m, :], mem.u[:, m, :], ACT.Silu).then_inc(u_done, 1)
        yield .62
        act.wait_ge(xp_mm, 1)
        nc.scalar.activation(k.xp[:], bank[0][0:R + 2 * NS, 0:TT], ACT.Copy).then_inc(xp_done, 1)
        for m in range(ND):
            yield .68 + .02 * m
            act.wait_ge(dt_mm, m + 1)
            nc.scalar.activation(mem.delta[:, m, :], dt_bank[m][:, 0:TT], ACT.Abs, bias=v[:, DT_B, m:m + 1]).then_inc(soft, 1)
        yield .75
        act.wait_ge(soft, ND)
        nc.scalar.activation(mem.delta, mem.delta, ACT.Exp, scale=-1.0).then_inc(soft, 1)
        act.wait_ge(soft, ND + 1)
        nc.scalar.activation(mem.delta, mem.delta, ACT.Ln, bias=1.0).then_inc(soft, 1)

    def vector(dve):
        for tap in range(9):
            dy, dx = divmod(tap, 3)
            for m in range(n_dve):
                yield .12 + .4 * tap / 9 + .01 * m
                src = k.xin[:, m, dy:dy + TR, dx:dx + W]
                acc = mem.u[:, m, :].rearrange("p (r c) -> p r c", c=W)
                wt = k.t["conv_w"][:, m * 9 + tap:m * 9 + tap + 1]
                if tap == 0:
                    dve.wait_ge(copied, m + 1)
                    if m == 0 and j in (0, NT - 1):
                        dve.wait_ge(border, 4 if j == 0 else 1)
                    nc.vector.tensor_scalar(acc, src, wt, v[:, CONV_B, m:m + 1], ALU.mult, ALU.add).then_inc(conv, 1)
                else:
                    dve.wait_ge(conv, (tap - 1) * n_dve + m + 1)
                    nc.vector.scalar_tensor_tensor(acc, src, wt, acc, ALU.mult, ALU.add).then_inc(conv, 1)
        for m in range(ND):
            yield .7 + .02 * m
            dve.wait_ge(soft, m + 1)
            nc.vector.tensor_scalar(mem.du[:, m, :], dt_bank[m][:, 0:TT], v[:, DT_B, m:m + 1], None, ALU.add).then_inc(delta, 1)
        yield .9
        dve.wait_ge(delta, ND)
        dve.wait_ge(soft, ND + 2)
        nc.vector.scalar_tensor_tensor(mem.delta, mem.du, 0.0, mem.delta, ALU.max, ALU.add).then_inc(delta, 1)
        dve.wait_ge(delta, ND + 1)
        dve.wait_ge(u_done, ND)
        nc.vector.tensor_tensor(mem.du, mem.delta, mem.u, ALU.mult).then_inc(delta, 1)

    return dict(sync=sync, gpsimd=gpsimd, tensor=tensor, scalar=scalar, vector=vector)


def load_piece(k, sp, b, j, mem, loaded):
    n = min(TT + W, L - TT * j)
    return sp.dma_start(mem.x[:, :, 0:n],
                        k.d["x"][b].rearrange("(a p) n -> p a n", p=96)[:, :, TT * j:TT * j + n]).then_inc(loaded, 16)


def scan(k, b, j, mem):
    nc = k.nc
    loaded, bc_even, bc_odd, decay, inp, scanned, kept, times_c, added, summed = k.sems(10)
    N = NS // 2 * ND
    DG = 2
    END = N + 2.0
    bc_in = (bc_even, bc_odd)

    def sync(sp):
        for p in range(NS // 2):
            yield max(0, ND * (p - 1)) / END
            if p >= 2:
                sp.wait_ge(times_c, ND * (p - 1))
            src = mem.bc.rearrange("(a s) n -> a s n", a=2)[:, 2 * p:2 * p + 2, :].unsqueeze(0)
            sp.dma_start(k.bc[:, p % 2, :, :, :], src.to_broadcast([128, 2, 2, TT])).then_inc(bc_in[p % 2], 16)
            if p == 2 and mem.loads_ahead and j + 1 < NT:
                load_piece(k, sp, b, j + 1, mem.next, loaded)
        yield 1
        if mem.loads_ahead and j + 1 < NT:
            sp.wait_ge(loaded, 16)

    def scalar(act):
        for g in range(0, N, DG):
            yield max(0, g - DG) / END
            if g >= 2 * ND:
                act.wait_ge(scanned, 2 * (g + DG - 2 * ND))
            for n in range(g, g + DG):
                p, m = divmod(n, ND)
                for sub in range(2):
                    at = m * NS + 2 * p + sub
                    nc.scalar.activation(k.a[:, n % (2 * ND), sub, :], mem.delta[:, m, :], ACT.Exp,
                                         scale=k.A[:, at:at + 1]).then_inc(decay, 1)

    def vector(dve):
        def pair_sum(n):
            dve.wait_ge(times_c, n + 1)
            nc.vector.tensor_tensor(k.hw[:, n % 3, 0, :], k.hw[:, n % 3, 0, :], k.hw[:, n % 3, 1, :], ALU.add).then_inc(added, 1)

        for n in range(N):
            yield n / END
            p, m = divmod(n, ND)
            if m == 0:
                dve.wait_ge(bc_in[p % 2], 16 * (p // 2 + 1))
            if n >= 3:
                dve.wait_ge(summed, n - 2)
            nc.vector.tensor_tensor(k.hw[:, n % 3, :, :], mem.du[:, m, :].unsqueeze(1).to_broadcast([128, 2, TT]),
                                    k.bc[:, p % 2, 0, :, :], ALU.mult).then_inc(inp, 1)
            dve.wait_ge(inp, n + 1)
            for sub in range(2):
                dve.wait_ge(decay, 2 * n + sub + 1)
                at = m * NS + 2 * p + sub
                nc.vector.tensor_tensor_scan(k.hw[:, n % 3, sub, :], k.a[:, n % (2 * ND), sub, :], k.hw[:, n % 3, sub, :],
                                             k.state[:, at:at + 1], ALU.mult, ALU.add).then_inc(scanned, 1)
            if n >= 1 and not mem.pe_sums:
                yield (n + .2) / END
                pair_sum(n - 1)
        if not mem.pe_sums:
            yield (N + .2) / END
            pair_sum(N - 1)

    def gpsimd(pool):
        for n in range(N):
            yield (n + .1) / END
            p, m = divmod(n, ND)
            if m == 0:
                pool.wait_ge(bc_in[p % 2], 16 * (p // 2 + 1))
            pool.wait_ge(scanned, 2 * n + 2)
            nc.gpsimd.tensor_copy(k.state[:, m * NS + 2 * p:m * NS + 2 * p + 2], k.hw[:, n % 3, :, TT - 1]).then_inc(kept, 1)
            pool.wait_ge(kept, n + 1)
            nc.gpsimd.tensor_tensor(k.hw[:, n % 3, :, :], k.hw[:, n % 3, :, :], k.bc[:, p % 2, 1, :, :],
                                    ALU.mult).then_inc(times_c, 1)

    def tensor(pe):
        for n in range(N):
            yield (n + 1.5) / END
            p, m = divmod(n, ND)
            if mem.pe_sums:
                pe.wait_ge(times_c, n + 1)
                nc.tensor.matmul(mem.banks[m][:, 0:TT], k.t["ident"][:], k.hw[:, n % 3, 1, :], start=p == 0, stop=False)
            else:
                pe.wait_ge(added, n + 1)
            nc.tensor.matmul(mem.banks[m][:, 0:TT], k.t["ident"][:], k.hw[:, n % 3, 0, :],
                             start=p == 0 and not mem.pe_sums, stop=p == NS // 2 - 1).then_inc(summed, 1)

    return dict(sync=sync, gpsimd=gpsimd, tensor=tensor, scalar=scalar, vector=vector)


def finish(k, j, mem):
    nc, v = k.nc, k.t["vec384"]
    (y_done, z_mm, z_done, ysum, mean_mm, cent, sq, sqsum, var_mm, root, rstd, norm, affine, gate, out_mm, out,
     stored) = k.sems(17)
    y3 = mem.y.rearrange("p (a n) -> p a n", a=ND)
    tot = mem.tot
    fo = mem.fo

    def vector(dve):
        for m in range(ND):
            yield .01 * m
            nc.vector.scalar_tensor_tensor(y3[:, m, :], mem.u[:, m, :], v[:, D_PAR, m:m + 1], mem.banks[m][:, 0:TT],
                                           ALU.mult, ALU.add).then_inc(y_done, 1)
        yield .05
        dve.wait_ge(y_done, ND)
        nc.vector.tensor_tensor(tot, y3[:, 0, :], y3[:, 1, :], ALU.add).then_inc(ysum, 1)
        dve.wait_ge(ysum, 1)
        nc.vector.tensor_tensor(tot, tot, y3[:, 2, :], ALU.add).then_inc(ysum, 1)
        for m in range(ND):
            yield .2 + .02 * m
            dve.wait_ge(mean_mm, 1)
            nc.vector.tensor_tensor(y3[:, m, :], y3[:, m, :], mem.banks[0][:, 0:TT], ALU.subtract).then_inc(cent, 1)
        yield .4
        dve.wait_ge(sq, ND)
        nc.vector.tensor_tensor(tot, mem.delta[:, 0, :], mem.delta[:, 1, :], ALU.add).then_inc(sqsum, 1)
        dve.wait_ge(sqsum, 1)
        nc.vector.tensor_tensor(tot, tot, mem.delta[:, 2, :], ALU.add).then_inc(sqsum, 1)
        yield .6
        dve.wait_ge(root, 1)
        nc.vector.reciprocal(mem.rstd, mem.rstd).then_inc(rstd, 1)
        for m in range(ND):
            yield .65 + .02 * m
            if m == 0:
                dve.wait_ge(rstd, 1)
                dve.wait_ge(cent, ND)
                dve.wait_ge(z_done, ND)
            nc.vector.tensor_tensor(y3[:, m, :], y3[:, m, :], mem.rstd, ALU.mult).then_inc(norm, 1)
        for m in range(ND):
            yield .74 + .03 * m
            dve.wait_ge(affine, m + 1)
            nc.vector.tensor_tensor(y3[:, m, :], y3[:, m, :], mem.sz[:, m, :], ALU.mult).then_inc(gate, 1)

    def tensor(pe):
        for m in range(ND):
            yield .02 + .01 * m
            pe.wait_ge(y_done, m + 1)
            for kc in range(2):
                last = nc.tensor.matmul(mem.banks[m][:, 0:TT], k.t["w_in"][:, kc, DI + m * 128:DI + m * 128 + 128],
                                        mem.x[:, kc, 0:TT], start=kc == 0, stop=kc == 1)
            last.then_inc(z_mm, 1)
        yield .15
        pe.wait_ge(z_done, 1)
        pe.wait_ge(ysum, 2)
        nc.tensor.matmul(mem.banks[0][:, 0:TT], k.ones[:], tot, start=True, stop=True).then_inc(mean_mm, 1)
        yield .45
        pe.wait_ge(sqsum, 2)
        pe.wait_ge(z_done, 2)
        nc.tensor.matmul(mem.banks[1][:, 0:TT], k.ones[:], tot, start=True, stop=True).then_inc(var_mm, 1)
        yield .82
        pe.wait_ge(gate, ND)
        pe.wait_ge(cent, ND)
        for mo in range(2):
            for m in range(ND):
                last = nc.tensor.matmul(mem.banks[(2, 0)[mo]][0:96, 0:TT], k.w_of[:, m, mo * 96:mo * 96 + 96], y3[:, m, :],
                                        start=m == 0, stop=m == ND - 1)
            last.then_inc(out_mm, 1)

    def scalar(act):
        for m in range(ND):
            yield .06 + .02 * m
            act.wait_ge(z_mm, m + 1)
            nc.scalar.activation(mem.sz[:, m, :], mem.banks[m][:, 0:TT], ACT.Silu).then_inc(z_done, 1)
        for m in range(ND):
            yield .25 + .03 * m
            act.wait_ge(cent, m + 1)
            nc.scalar.activation(mem.delta[:, m, :], y3[:, m, :], ACT.Square).then_inc(sq, 1)
        yield .5
        act.wait_ge(var_mm, 1)
        nc.scalar.activation(mem.rstd, mem.banks[1][:, 0:TT], ACT.Sqrt, bias=k.eps[:]).then_inc(root, 1)
        for m in range(ND):
            yield .66 + .03 * m
            act.wait_ge(norm, m + 1)
            nc.scalar.activation(y3[:, m, :], y3[:, m, :], ACT.Identity, bias=v[:, LN_B, m:m + 1],
                                 scale=v[:, LN_G, m:m + 1]).then_inc(affine, 1)
        for mo in range(2):
            yield .85 + .05 * mo
            act.wait_ge(out_mm, mo + 1)
            nc.scalar.activation(fo[:, mo, :], mem.banks[(2, 0)[mo]][0:96, 0:TT], ACT.Identity,
                                 bias=k.t["vec192"][:, 0, mo:mo + 1]).then_inc(out, 1)

    def sync(sp):
        yield .95
        sp.wait_ge(out, 2)
        sp.dma_start(k.d["fused"][:, :, TT * j:TT * j + TT], fo).then_inc(stored, 16)
        yield 1
        sp.wait_ge(stored, 16)

    return dict(sync=sync, tensor=tensor, scalar=scalar, vector=vector)



def instance_norm_and_conv(k, b):
    nc, t = k.nc, k.t
    loaded, st, root, rstd, normed, x1, pooled, t_mm, tvec, w_mm, taps, first_tap, conv, border, own = k.sems(15)
    fused = k.fin
    shift = k.rs[:, 2:4]

    def sync(sp):
        yield 0
        sp.dma_start(fused, k.d["fused"]).then_inc(loaded, 16)
        sp.dma_start(k.xres, k.d["x"][b].rearrange("(a p) n -> p a n", p=96)).then_inc(loaded, 16)

    def vector(dve):
        c = Tally(own)

        def link(ins):
            dve.wait_ge(own, c.inc(ins))

        yield 0
        dve.wait_ge(loaded, 32)
        for mo in range(2):
            for q in range(6):
                yield .05 + .01 * q
                c.inc(nc.vector.bn_stats(k.st[:, (mo * 6 + q) * 6:(mo * 6 + q) * 6 + 6], fused[:, mo, q * Q:q * Q + Q]))
        dve.wait_ge(own, c.n)
        for mo in range(2):
            c.inc(nc.vector.bn_aggr(k.mv[:, mo, :], k.st[:, mo * 36:mo * 36 + 36]))
        dve.wait_ge(own, c.n)
        nc.vector.tensor_copy(k.rs[:, 0:2], k.mv[:, 0:2, 1]).then_inc(st, 1)
        yield .2
        dve.wait_ge(root, 1)
        link(nc.vector.reciprocal(k.rs[:, 0:2], k.rs[:, 0:2]))
        nc.vector.scalar_tensor_tensor(shift, k.mv[:, 0:2, 0], -1.0, k.rs[:, 0:2], ALU.mult, ALU.mult).then_inc(rstd, 1)
        for mo in range(2):
            yield .3 + .05 * mo
            dve.wait_ge(normed, mo + 1)
            nc.vector.tensor_tensor(k.x1p[:, mo, 1:H + 1, 1:W + 1], fused[:, mo, :].rearrange("p (r c) -> p r c", c=W),
                                    k.xres[:, mo, :].rearrange("p (r c) -> p r c", c=W), ALU.add).then_inc(x1, 1)
        yield .5
        dve.wait_ge(t_mm, 1)
        bn = t["bn"]
        link(nc.vector.tensor_scalar(k.tv[:], k.P[0:48, 0, 0:1], bn[:, 2:3], bn[:, 0:1], ALU.subtract, ALU.mult))
        link(nc.vector.tensor_scalar(k.tv[:], k.tv[:], k.bn_r[:, 0:1], bn[:, 1:2], ALU.mult, ALU.add))
        nc.vector.tensor_scalar(k.tv[:], k.tv[:], 0.0, None, ALU.max).then_inc(tvec, 1)
        dve.wait_ge(w_mm, 1)
        nc.vector.tensor_tensor(k.wts[:], k.P[0:96, 1, 0:8], t["b2"][:].rearrange("p a n -> p (a n)"), ALU.add).then_inc(taps, 1)
        for tap, (dy, dx) in ((1, (0, 1)), (2, (0, 2)), (3, (1, 0))):
            for mo in range(2):
                yield .55 + .1 * tap + .05 * mo
                src = k.x1p[:, mo, dy:dy + H, dx:dx + W]
                dst = k.x2[:, mo, :].rearrange("p (r c) -> p r c", c=W)
                wt = k.wts[:, mo * 4 + tap:mo * 4 + tap + 1]
                if tap == 1:
                    dve.wait_ge(first_tap, mo + 1)
                    dve.wait_ge(border, 3)
                else:
                    dve.wait_ge(conv, 2 * (tap - 2) + mo + 1)
                if tap < 3:
                    nc.vector.scalar_tensor_tensor(dst, src, wt, dst, ALU.mult, ALU.add).then_inc(conv, 1)
                    continue
                for a in range(2):
                    cols = slice(a * WH, a * WH + WH)
                    nc.vector.scalar_tensor_tensor(
                        k.x2t[:, mo, :, a * H:a * H + H].rearrange("p w h -> p h w"),
                        src[:, :, cols], wt, dst[:, :, cols], ALU.mult, ALU.add).then_inc(conv, 1)

    def scalar(act):
        yield .2
        act.wait_ge(st, 1)
        nc.scalar.activation(k.rs[:, 0:2], k.rs[:, 0:2], ACT.Sqrt, bias=k.eps[0:96, :]).then_inc(root, 1)
        for mo in range(2):
            yield .25 + .05 * mo
            act.wait_ge(rstd, 1)
            nc.scalar.activation(fused[:, mo, :], fused[:, mo, :], ACT.Identity, bias=shift[:, mo:mo + 1],
                                 scale=k.rs[:, mo:mo + 1]).then_inc(normed, 1)
        for mo in range(2):
            yield .4
            act.wait_ge(x1, 2)
            if mo:
                act.wait_ge(pooled, 1)
            nc.scalar.activation(fused[:, 0, :].rearrange("p (r c) -> p r c", c=W), k.x1p[:, mo, 1:H + 1, 1:W + 1],
                                 ACT.Copy, scale=1.0 / L, accum_out=k.pool[:, mo:mo + 1]).then_inc(pooled, 1)
        for mo in range(2):
            yield .55 + .05 * mo
            act.wait_ge(taps, 1)
            if mo == 0:
                act.wait_ge(border, 3)
            nc.scalar.activation(k.x2[:, mo, :].rearrange("p (r c) -> p r c", c=W), k.x1p[:, mo, 0:H, 0:W], ACT.Identity,
                                 bias=t["vec192"][:, 1, mo:mo + 1], scale=k.wts[:, mo * 4:mo * 4 + 1]).then_inc(first_tap, 1)

    def gpsimd(pool):
        yield 0
        nc.gpsimd.memset(k.x1p[:, :, 0, :], 0.0).then_inc(border, 1)
        nc.gpsimd.memset(k.x1p[:, :, 1:H + 1, 0], 0.0).then_inc(border, 1)
        nc.gpsimd.memset(k.x1p[:, :, 1:H + 1, W + 1], 0.0).then_inc(border, 1)

    def tensor(pe):
        yield .45
        pe.wait_ge(pooled, 2)
        for kc in range(2):
            last = nc.tensor.matmul(k.P[0:48, 0, 0:1], t["w1"][:, kc, :], k.pool[:, kc:kc + 1], start=kc == 0, stop=kc == 1)
        last.then_inc(t_mm, 1)
        yield .5
        pe.wait_ge(tvec, 1)
        for mo in range(2):
            for tap in range(4):
                last = nc.tensor.matmul(k.P[0:96, 1, mo * 4 + tap:mo * 4 + tap + 1], t["w2"][:, tap, mo * 96:mo * 96 + 96],
                                        k.tv[:], start=True, stop=True)
        last.then_inc(w_mm, 1)

    return dict(sync=sync, tensor=tensor, scalar=scalar, vector=vector, gpsimd=gpsimd)



def to_token_major(k):
    nc = k.nc
    tr, copied, stat = k.sems(3)

    def tensor(pe):
        for n in range(WH // 2):
            yield n / 12
            if n >= 5:
                pe.wait_ge(copied, n - 4)
            for w in range(2):
                for kc in range(2):
                    last = nc.tensor.transpose(k.P[0:96, n % 5, w * C + kc * 96:w * C + kc * 96 + 96],
                                               k.x2t[:, kc, 2 * n + w, :], k.t["ident"][0:96, 0:96])
            last.then_inc(tr, 1)

    def scalar(act):
        for n in range(WH // 2):
            yield n / 12
            act.wait_ge(tr, n + 1)
            nc.scalar.activation(k.xT[:, 2 * n:2 * n + 2, :], k.P[0:96, n % 5, 0:2 * C].rearrange("p (w c) -> p w c", c=C),
                                 ACT.Copy).then_inc(copied, 1)

    def vector(dve):
        for w in range(WH):
            yield (w // 2 + 1) / 13
            dve.wait_ge(copied, w // 2 + 1)
            slice_statistics(k, dve, k.xT, w, stat)

    return dict(tensor=tensor, scalar=scalar, vector=vector)


def slice_statistics(k, dve, src, w, stat, at=None):
    k.nc.vector.bn_stats(k.st[:, w * 6:w * 6 + 6], src[:, w, :]).then_inc(stat, 1)
    dve.wait_ge(stat, 2 * w + 1 if at is None else at)
    k.nc.vector.bn_aggr(k.mv[:, w, :], k.st[:, w * 6:w * 6 + 6]).then_inc(stat, 1)


def layer_norm(k, src, dst, g=None, b=None, transposed=None, add_bias=None, store=None):
    nc, rows = k.nc, k.t["rows"]
    root, rinv, norm = k.sems(3)
    if g is not None:
        scaled, shifted = k.sems(2)
    if add_bias is not None:
        biased, = k.sems(1)
    if transposed is not None:
        tr, copied = k.sems(2)
    if store is not None:
        stored, = k.sems(1)
    half = WH // 2

    def row(i, n):
        return rows[:, i, :].unsqueeze(1).to_broadcast([96, n, C])

    def vector(dve):
        yield .15
        dve.wait_ge(root, 1)
        nc.vector.reciprocal(k.rs[:], k.rs[:]).then_inc(rinv, 1)
        dve.wait_ge(rinv, 1)
        for j in range(4):
            yield .2 + .15 * j
            for w in range(6 * j, 6 * j + 6):
                nc.vector.tensor_scalar(dst[:, w, :], src[:, w, :], k.mv[:, w, 0:1], k.rs[:, w:w + 1],
                                        ALU.subtract, ALU.mult).then_inc(norm, 1)
            if g is not None:
                dve.wait_ge(norm, 6 * j + 6)
                part = dst[:, 6 * j:6 * j + 6, :]
                nc.vector.tensor_tensor(part, part, row(g, 6), ALU.mult).then_inc(scaled, 1)

    def scalar(act):
        yield 0
        nc.scalar.activation(k.rs[:], k.mv[:, :, 1], ACT.Sqrt, bias=k.eps[0:96, :]).then_inc(root, 1)
        if transposed is not None:
            for n in range(half):
                yield .26 + .05 * n
                act.wait_ge(tr, n + 1)
                nc.scalar.activation(transposed[:, :, 2 * n:2 * n + 2, :],
                                     k.P[0:96, n % 5, 0:2 * C].rearrange("p (a w n) -> p a w n", a=2, w=2),
                                     ACT.Copy).then_inc(copied, 1)

    def gpsimd(pool):
        for j in range(4):
            if b is not None:
                yield .3 + .15 * j
                pool.wait_ge(scaled, j + 1)
                part = dst[:, 6 * j:6 * j + 6, :]
                nc.gpsimd.tensor_tensor(part, part, row(b, 6), ALU.add).then_inc(shifted, 1)
            if add_bias is not None:
                yield .3 + .15 * j
                pool.wait_ge(norm, 6 * j + 6)
                part = src[:, 6 * j:6 * j + 6, :]
                nc.gpsimd.tensor_tensor(part, part, row(add_bias, 6), ALU.add).then_inc(biased, 1)

    def sync(sp):
        yield .9
        sp.wait_ge(biased, 4)
        sp.dma_start(store, src).then_inc(stored, 16)
        yield 1
        sp.wait_ge(stored, 16)

    def tensor(pe):
        for n in range(half):
            yield .26 + .05 * n
            pe.wait_ge(norm, 2 * n + 2)
            if n >= 5:
                pe.wait_ge(copied, n - 4)
            for kc in range(2):
                for w in range(2):
                    at = kc * C + w * 96
                    last = nc.tensor.transpose(k.P[0:96, n % 5, at:at + 96], dst[:, 2 * n + w, kc * 96:kc * 96 + 96],
                                               k.t["ident"][0:96, 0:96])
            last.then_inc(tr, 1)

    programs = dict(scalar=scalar, vector=vector, gpsimd=gpsimd)
    if g is not None:
        programs["shifted"] = shifted
    if transposed is not None:
        programs["tensor"] = tensor
    if store is not None:
        programs["sync"] = sync
    return programs


def channel_mlp(k, begin, end, src, res, out, w1, b1, w2, store=None):
    nc, t = k.nc, k.t
    up, act_done, down, added, stored, stat = k.sems(6)
    NCH = end - begin
    END = NCH + .5

    def tensor(pe):
        def first(j):
            for m in range(NF):
                yield max(0, j - 1 + m / 12) / END
                n = j * NF + m
                if n >= 3:
                    pe.wait_ge(act_done, n - 2)
                for kc in range(2):
                    last = nc.tensor.matmul(k.P[:, n % 3, 0:Q], t[w1][:, kc, m * 128:m * 128 + 128],
                                            src[:, kc, 4 * (begin + j):4 * (begin + j) + 4, :].rearrange("p w n -> p (w n)"),
                                            start=kc == 0, stop=kc == 1)
                last.then_inc(up, 1)

        def second(j):
            for w in range(4):
                yield (j + .5 + w / 8) / END
                pe.wait_ge(act_done, NF * (j + 1))
                n = 4 * j + w
                if n >= 2:
                    pe.wait_ge(added, n - 1)
                for m in range(NF):
                    last = nc.tensor.matmul(k.P[0:96, 3 + n % 2, 0:C], k.hid[:, j % 2, m, w * 96:w * 96 + 96],
                                            t[w2][:, m, :], start=m == 0, stop=m == NF - 1)
                last.then_inc(down, 1)

        yield from first(0)
        for j in range(NCH):
            if j + 1 < NCH:
                yield from first(j + 1)
            yield from second(j)

    def scalar(act):
        for j in range(NCH):
            for m in range(NF):
                yield max(0, j - 1 + (m + .5) / 12) / END
                if j >= 2 and m == 0:
                    act.wait_ge(down, 4 * (j - 1))
                n = j * NF + m
                act.wait_ge(up, n + 1)
                nc.scalar.activation(k.hid[:, j % 2, m, :], k.P[:, n % 3, 0:Q], ACT.Gelu,
                                     bias=t[b1][:, m:m + 1]).then_inc(act_done, 1)

    def vector(dve):
        for n in range(4 * NCH):
            yield (n // 4 + .5 + (n % 4 + 1) / 8) / END
            w = 4 * begin + n
            dve.wait_ge(down, n + 1)
            nc.vector.tensor_tensor(out[:, w, :], k.P[0:96, 3 + n % 2, 0:C], res[:, w, :], ALU.add).then_inc(added, 1)
            if store is None and n >= 1:
                dve.wait_ge(added, n)
                slice_statistics(k, dve, out, w - 1, stat, 2 * n - 1)
        if store is None:
            dve.wait_ge(added, 4 * NCH)
            slice_statistics(k, dve, out, 4 * end - 1, stat, 8 * NCH - 1)

    def sync(sp):
        for j in range(NCH):
            yield (j + 1.2) / END
            sp.wait_ge(added, 4 * j + 4)
            w = 4 * (begin + j)
            sp.dma_start(store[:, w:w + 4, :], out[:, w:w + 4, :]).then_inc(stored, 16)
        sp.wait_ge(stored, 16 * NCH)

    programs = dict(tensor=tensor, scalar=scalar, vector=vector)
    if store is not None:
        programs["sync"] = sync
    return programs



FIRST_KH = 6


def load_frequencies(k, sp, first, end, back):
    Rk, scr = k.Rb.rearrange("p (k c) -> p k c", c=C), k.d["spec_in"]
    for a in range(2):
        sp.dma_start(Rk[a * 48:a * 48 + 48, first:end, :],
                     scr[24 * a + 1 + first:24 * a + 1 + end].rearrange("k w c -> w k c")).then_inc(back, 16)


def rows_dft(k):
    nc = k.nc
    norm = layer_norm(k, k.xT, k.xn, N1G, N1B)
    mm, copied, out, back, zero = k.sems(5)
    scr = k.d["spec_in"]
    NORM = .6

    def beside_norm(name, eng, *steps):
        return merged([(NORM * due for due in norm[name](eng))] + [st(eng) for st in steps])

    def tensor(pe):
        for n in range(12):
            yield .3 + n / 30
            if n % 3 == 0:
                pe.wait_ge(norm["shifted"], n // 3 + 1)
            if n >= 5:
                pe.wait_ge(copied, n - 4)
            nc.tensor.matmul(k.P[0:96, n % 5, 0:Q], k.t["row_f"][:],
                             k.xn[:, 2 * n:2 * n + 2, :].rearrange("p w c -> p (w c)"), start=True, stop=True).then_inc(mm, 1)

    def scalar(act):
        for n in range(12):
            yield .3 + n / 30
            act.wait_ge(mm, n + 1)
            nc.scalar.activation(k.spec[:, n * Q:n * Q + Q], k.P[0:96, n % 5, 0:Q], ACT.Copy).then_inc(copied, 1)

    def vector(dve):
        yield .68
        dve.wait_ge(mm, 12)
        nc.vector.memset(k.Rb[:, 23 * C:25 * C], 0.0).then_inc(zero, 1)

    def sync(sp):
        for j in range(3):
            yield .3 + (4 * j + 4) / 30
            sp.wait_ge(copied, 4 * j + 4)
            for a in range(2):
                sp.dma_start(scr[:, a * WH + 8 * j:a * WH + 8 * j + 8, :],
                             k.spec[a * 48:a * 48 + 48, 8 * j * C:(8 * j + 8) * C].rearrange("p (w c) -> p w c", c=C)
                             ).then_inc(out, 16)
        yield .7
        sp.wait_ge(out, 96)
        sp.wait_ge(zero, 1)
        load_frequencies(k, sp, 0, FIRST_KH, back)
        yield 1
        sp.wait_ge(back, 32)

    return dict(sync=sync, tensor=tensor, gpsimd=lambda pool: beside_norm("gpsimd", pool), scalar=lambda act: beside_norm("scalar", act, scalar),
                vector=lambda dve: beside_norm("vector", dve, vector))


CHUNKS = [(PAIR * j, PAIR, 2) for j in range(12)] + [(23 * C, 2 * C, 1)]


def frequencies(k, first, end):
    nc = k.nc
    hid_mm, gel, acc_mm, got, back, out = k.sems(6)
    assert first > 0 or end * PAIR <= FIRST_KH * C
    chunks = CHUNKS[first:end]
    steps = [(j, s, g) for j, (_, _, ns) in enumerate(chunks) for s in range(ns) for g in range(GRP)]
    ends = {j: n for n, (j, _, _) in enumerate(steps)}
    END = len(steps) + 1.0
    NB = 4

    def tensor(pe):
        def hidden(n):
            j, s, g = steps[n]
            c0, cols, _ = chunks[j]
            if n >= 3:
                pe.wait_ge(gel, n - 2)
            nc.tensor.matmul(k.P[:, n % 3, 0:cols], k.G[:, s, g * 128:g * 128 + 128], k.Rb[:, c0:c0 + cols],
                             start=True, stop=True).then_inc(hid_mm, 1)

        yield 0
        hidden(0)
        hidden(1)
        for n, (j, s, g) in enumerate(steps):
            yield n / END
            if n + 2 < len(steps):
                hidden(n + 2)
            cols, ns = chunks[j][1:]
            pe.wait_ge(gel, n + 1)
            if j >= 2 and s == 0 and g == 0:
                pe.wait_ge(got, j - 1)
            nc.tensor.matmul(k.P[0:96, 3 + j % 2, 0:cols], k.V[:, s, g, :], k.fh[:, n % NB, 0:cols],
                             start=(s == 0 and g == 0), stop=(s == ns - 1 and g == GRP - 1)).then_inc(acc_mm, 1)

    def scalar(act):
        for n, (j, s, g) in enumerate(steps):
            yield max(0, n - 1) / END
            cols = chunks[j][1]
            act.wait_ge(hid_mm, n + 1)
            if n >= NB:
                act.wait_ge(acc_mm, n - NB + 1)
            nc.scalar.activation(k.fh[:, n % NB, 0:cols], k.P[:, n % 3, 0:cols], ACT.Gelu,
                                 bias=k.t["fc1b"][:, 0:1]).then_inc(gel, 1)

    def vector(dve):
        for j, (c0, cols, _) in enumerate(chunks):
            yield (ends[j] + .5) / END
            dve.wait_ge(acc_mm, ends[j] + 1)
            nc.vector.tensor_copy(k.spec[:, c0:c0 + cols], k.P[0:96, 3 + j % 2, 0:cols]).then_inc(got, 1)

    def sync(sp):
        yield 0
        if first == 0:
            load_frequencies(k, sp, FIRST_KH, 23, back)
            for n in range(2):
                sp.dma_start(k.Rb[0:48, (23 + n) * C:(24 + n) * C], k.d["spec_in"][24 * n]).then_inc(back, 16)
        yield (ends[len(chunks) - 1] - 1) / END
        if len(chunks) > 1:
            sp.wait_ge(got, len(chunks) - 1)
        lo, hi = sums_stored(first), sums_stored(end)
        if hi > lo:
            store_sums(k, sp, lo, hi, out)
        yield 1
        if hi > lo:
            sp.wait_ge(out, 32)
        if first == 0:
            sp.wait_ge(back, 64)

    return dict(sync=sync, tensor=tensor, scalar=scalar, vector=vector)


def sums_stored(chunk):
    return PAIR * max(0, min(chunk, 12) - 1) // C


def store_sums(k, sp, first, end, out):
    gk, scr = k.spec.rearrange("p (k c) -> p k c", c=C), k.d["spec_out"]
    for a in range(2):
        sp.dma_start(scr[24 * a + 1 + first:24 * a + 1 + end].rearrange("k w c -> w k c"),
                     gk[a * 48:a * 48 + 48, first:end, :]).then_inc(out, 16)


def rows_inverse(k):
    nc = k.nc
    mm, added, fixed, out, back, stat = k.sems(6)
    scr = k.d["spec_out"]

    def sync(sp):
        gk = k.spec.rearrange("p (k c) -> p k c", c=C)
        yield 0
        store_sums(k, sp, sums_stored(len(CHUNKS)), 23, out)
        sp.dma_start(scr[0], gk[0:48, 23, :]).then_inc(out, 16)
        sp.dma_start(scr[24], gk[0:48, 24, :]).then_inc(out, 16)
        yield .3
        sp.wait_ge(out, 64)
        for a in range(2):
            sp.dma_start(k.back[a * 48:a * 48 + 48, :].rearrange("p (w c) -> p w c", c=C),
                         scr[:, a * WH:a * WH + WH, :]).then_inc(back, 16)

    def tensor(pe):
        for n in range(12):
            yield .5 + n / 24
            if n == 0:
                pe.wait_ge(back, 32)
            if n >= 5:
                pe.wait_ge(added, n - 4)
            nc.tensor.matmul(k.P[0:96, n % 5, 0:Q], k.t["row_i"][:], k.back[:, n * Q:n * Q + Q],
                             start=True, stop=True).then_inc(mm, 1)

    def vector(dve):
        for n in range(12):
            yield .5 + n / 24
            dve.wait_ge(mm, n + 1)
            part = k.xT[:, 2 * n:2 * n + 2, :].rearrange("p w c -> p (w c)")
            nc.vector.tensor_tensor(part, k.P[0:96, n % 5, 0:Q], part, ALU.add).then_inc(added, 1)
            if n == 0:
                dve.wait_ge(added, 1)
                nc.vector.tensor_scalar(k.xT[0:1, 0, :], k.xT[0:1, 0, :], k.t["fc2b"][:, 0:1], None, ALU.add).then_inc(fixed, 1)
                dve.wait_ge(fixed, 1)
            else:
                dve.wait_ge(added, n)
                for w in (2 * n - 2, 2 * n - 1):
                    slice_statistics(k, dve, k.xT, w, stat)
        dve.wait_ge(added, 12)
        for w in (WH - 2, WH - 1):
            slice_statistics(k, dve, k.xT, w, stat)

    return dict(sync=sync, tensor=tensor, vector=vector)



def positions(t, half, i):
    ih, iw = divmod(i, WIN)
    return t[:, half, :, :].rearrange("p (b w) (a r h) -> p w h b a r", w=WIN, a=2, h=WIN)[:, iw, ih, :, :, :]


def butterflies(engine, src, dst, bit, at, done):
    for op, half in ((ALU.add, 0), (ALU.subtract, 1)):
        engine.tensor_tensor(bit(dst[at], half), bit(src[at], 0), bit(src[at], 1), op).then_inc(done, 1)


def row_bit(n):
    if n == 0:
        return lambda t, half: t.rearrange("p w (m b) -> p (w m) b", b=2)[:, :, half]
    return lambda t, half: t.rearrange("p w (m b l) -> p (w m) b l", b=2, l=2)[:, :, half, :]


def column_bit(n):
    if n == 0:
        return lambda t, half: t.rearrange("p (m b) h -> p m b h", b=2)[:, :, half, :]
    return lambda t, half: t.rearrange("p (m b l) h -> p m b (l h)", b=2, l=2)[:, :, half, :]


BITS = [row_bit(0), row_bit(1), column_bit(0), column_bit(1)]


DVE_PARTS = ((slice(None), 0), (slice(None), 1, slice(16, WH)))
POOL_PARTS = ((slice(None), 1, slice(0, 16)),)


def transform(eng, engine, path, parts, done, begin, share):
    for n, bit in enumerate(BITS):
        for m, at in enumerate(parts):
            yield begin + share * (n + m / len(parts)) / 4
            if n:
                eng.wait_ge(done, 2 * (len(parts) * (n - 1) + m + 1))
            butterflies(engine, path[n], path[n + 1], bit, at, done)


def forward_transform(k):
    nc = k.nc
    dve_done, pool_done, loaded = k.sems(3)
    path = [k.cm, k.wa, k.yg, k.wa, k.yg]

    def vector(dve):
        yield from transform(dve, nc.vector, path, DVE_PARTS, dve_done, 0, .8)

    def gpsimd(pool):
        yield from transform(pool, nc.gpsimd, path, POOL_PARTS, pool_done, 0, 1)

    def sync(sp):
        yield 0
        sp.dma_start(k.wsed, k.d["w_hat"]).then_inc(loaded, 16)
        yield 1
        sp.wait_ge(loaded, 16)

    return dict(sync=sync, vector=vector, gpsimd=gpsimd)


def sedenion_plan():
    sign = sedenion_signs()
    return [[i for i in range(16) if sign[i][kk] < 0] for kk in range(16)]


def transformed_products(k):
    nc = k.nc
    mm, copied, dve_back, pool_back, loaded = k.sems(5)
    path = [k.wa, k.yg, k.wa, k.yg, k.wa]

    def tensor(pe):
        for n in range(32):
            yield n / 64
            p, mo = divmod(n, 2)
            if n >= 5:
                pe.wait_ge(copied, n - 4)
            for kc in range(2):
                last = nc.tensor.matmul(k.P[0:96, n % 5, 0:NW].rearrange("p (b a r) -> p b a r", b=6, a=2),
                                        k.wsed[:, kc, p, mo * 96:mo * 96 + 96], positions(k.yg, kc, p),
                                        start=kc == 0, stop=kc == 1)
            last.then_inc(mm, 1)

    def scalar(act):
        for n in range(32):
            yield n / 64
            p, mo = divmod(n, 2)
            act.wait_ge(mm, n + 1)
            nc.scalar.activation(positions(k.wa, mo, p), k.P[0:96, n % 5, 0:NW].rearrange("p (b a r) -> p b a r", b=6, a=2),
                                 ACT.Copy).then_inc(copied, 1)

    def vector(dve):
        yield .5
        dve.wait_ge(copied, 32)
        dve.wait_ge(mm, 32)
        yield from transform(dve, nc.vector, path, DVE_PARTS, dve_back, .5, .4)

    def gpsimd(pool):
        yield .5
        pool.wait_ge(copied, 32)
        pool.wait_ge(mm, 32)
        yield from transform(pool, nc.gpsimd, path, POOL_PARTS, pool_back, .5, .5)

    def sync(sp):
        for q in range(4):
            yield (8 * q + 8) / 64
            sp.wait_ge(mm, 8 * q + 8)
            sp.dma_start(k.wsed[:, :, 4 * q:4 * q + 4, :], k.d["w_minus"][:, :, 4 * q:4 * q + 4, :]).then_inc(loaded, 16)
        yield 1
        sp.wait_ge(loaded, 64)

    return dict(sync=sync, tensor=tensor, scalar=scalar, vector=vector, gpsimd=gpsimd)


def corrections(k, first, end):
    nc = k.nc
    mm, added = k.sems(2)
    minus = sedenion_plan()
    weight = [len(minus[n // 2]) for n in range(first, end)]
    END = sum(weight) + 2.0
    due = [sum(weight[:n]) / END for n in range(end - first + 1)]

    def tensor(pe):
        for n in range(end - first):
            kk, mo = divmod(first + n, 2)
            terms = [(kc, i) for kc in range(2) for i in minus[kk]]
            for m, (kc, i) in enumerate(terms):
                if m % 4 == 0:
                    yield due[n] + (due[n + 1] - due[n]) * m / len(terms)
                if m == 0 and n >= 5:
                    pe.wait_ge(added, n - 4)
                last = nc.tensor.matmul(k.P[0:96, n % 5, 0:NW].rearrange("p (b a r) -> p b a r", b=6, a=2),
                                        k.wsed[:, kc, i ^ kk, mo * 96:mo * 96 + 96], positions(k.cm, kc, i),
                                        start=m == 0, stop=m == len(terms) - 1)
            last.then_inc(mm, 1)

    def vector(dve):
        for n in range(end - first):
            yield due[n + 1]
            kk, mo = divmod(first + n, 2)
            dve.wait_ge(mm, n + 1)
            at = positions(k.wa, mo, kk)
            nc.vector.tensor_tensor(at, k.P[0:96, n % 5, 0:NW].rearrange("p (b a r) -> p b a r", b=6, a=2), at,
                                    ALU.add).then_inc(added, 1)

    return dict(tensor=tensor, vector=vector)


def project(k):
    nc = k.nc
    loaded, gel, pr_mm, added, stat = k.sems(5)
    order = [4 * n + iw for iw in range(WIN) for n in range(WH // WIN)]

    def sync(sp):
        yield 0
        sp.dma_start(k.res, k.d["resid"]).then_inc(loaded, 16)

    def scalar(act):
        for n in range(32):
            yield .6 * n / 32
            iw, ih, mo = n // 8, n // 2 % 4, n % 2
            kk = WIN * ih + iw
            nc.scalar.activation(positions(k.yg, mo, kk), positions(k.wa, mo, kk), ACT.Gelu,
                                 bias=k.sed_b[:, mo * 16 + kk:mo * 16 + kk + 1]).then_inc(gel, 1)

    def tensor(pe):
        for n, w in enumerate(order):
            yield .17 + .78 * n / WH
            if n % (WH // WIN) == 0:
                pe.wait_ge(gel, 8 * (w % WIN + 1))
            if n >= 5:
                pe.wait_ge(added, n - 4)
            for kc in range(2):
                last = nc.tensor.matmul(k.P[0:96, n % 5, 0:C], k.yg[:, kc, w, :], k.t["proj"][:, kc, :],
                                        start=kc == 0, stop=kc == 1)
            last.then_inc(pr_mm, 1)

    def vector(dve):
        for n, w in enumerate(order):
            yield .17 + .78 * (n + 1) / WH
            if n == 0:
                dve.wait_ge(loaded, 16)
            dve.wait_ge(pr_mm, n + 1)
            nc.vector.tensor_tensor(k.xT[:, w, :], k.P[0:96, n % 5, 0:C], k.res[:, w, :], ALU.add).then_inc(added, 1)
            if n >= 1:
                dve.wait_ge(added, n)
                slice_statistics(k, dve, k.xT, order[n - 1], stat, 2 * n - 1)
        dve.wait_ge(added, WH)
        slice_statistics(k, dve, k.xT, order[-1], stat, 2 * WH - 1)

    return dict(sync=sync, tensor=tensor, scalar=scalar, vector=vector)



def setup_and_layer_0(k, b):
    k.together(k.in_sequence((0, 35, 35, 0), setup_layer_0(k), prepare(k, b, 0, k.alone[0])), setup_weights(k))
    for j in range(NT):
        beside = ([finish(k, j - 1, k.alone[j - 1])] if j else []) + ([prepare(k, b, j + 1, k.alone[j + 1])] if j + 1 < NT else [])
        k.together(scan(k, b, j, k.alone[j]), k.in_sequence((0,) + (1,) * len(beside) + (0,), *beside),
                   *([] if j else [setup_sedenion(k)]))
    k.together(finish(k, NT - 1, k.alone[NT - 1]))


CONV_SHARED = (1, 0, 1, 1, 0, 1)
PE_SUMS = (0, 0, 1, 1, 0, 0)

UNITS = (["norm_conv", "token_major", "rows"] + ["freq"] * 13 + ["rows_inv", "norm_2"] + ["mlp"] * 6
         + ["norm_3", "transform", "products"] + ["correct"] * 16 + ["project", "norm_4"] + ["mlp_out"] * 6)
CUTS = (0, 5, 13, 20, 27, 43)
SHARES = (((9.6, 23.3, 4.0, 17.5, 45.6, 0.0), (6.9, 29.1, 45.4, 15.2, 3.4)),
          ((3.6, 96.4, 0.0), (1.1, 24.3, 47.2, 26.5, 0.9)),
          ((1.9, 56.5, 13.6, 8.8, 8.5, 10.7), (0.0, 15.9, 47.9, 25.9, 10.3)),
          ((1.0, 52.2, 5.2, 8.3, 26.0, 7.3), (1.6, 21.1, 39.5, 21.6, 16.2)),
          ((2.3, 97.7, 0.0), (4.5, 29.7, 48.6, 17.2, 0.0)),
          ((0.0, 24.0, 10.4, 65.6, 0.0), (2.2, 32.9, 39.6, 22.3, 2.9)))


def later_layers(k, b, nxt):
    stages = dict(
        norm_conv=lambda first, end: instance_norm_and_conv(k, b),
        token_major=lambda first, end: to_token_major(k),
        rows=lambda first, end: rows_dft(k),
        freq=lambda first, end: frequencies(k, first, end),
        rows_inv=lambda first, end: rows_inverse(k),
        norm_2=lambda first, end: layer_norm(k, k.xT, k.xn, transposed=k.cm, add_bias=M2B),
        mlp=lambda first, end: channel_mlp(k, first, end, k.cm, k.xT, k.xT, "m1", "m1b", "m2"),
        norm_3=lambda first, end: layer_norm(k, k.xT, k.xn, transposed=k.cm, add_bias=PROJ_B, store=k.d["resid"]),
        transform=lambda first, end: forward_transform(k),
        products=lambda first, end: transformed_products(k),
        correct=lambda first, end: corrections(k, 2 * first, 2 * end),
        project=lambda first, end: project(k),
        norm_4=lambda first, end: layer_norm(k, k.xT, k.xn, transposed=k.cm, add_bias=F2B),
        mlp_out=lambda first, end: channel_mlp(k, first, end, k.cm, k.xT, k.xn, "f1", "f1b", "f2", store=k.d["out"][b]))
    for j in range(NT):
        first, end = (CUTS + (len(UNITS),))[j:j + 2]
        later = []
        for name in sorted(set(UNITS[first:end]), key=UNITS.index):
            at = [n for n in range(first, end) if UNITS[n] == name]
            later.append(stages[name](at[0] - UNITS.index(name), at[-1] + 1 - UNITS.index(name)))
        shares, piece = SHARES[j]
        side_by_side = [k.in_sequence(shares, *later)]
        if nxt is not None:
            side_by_side.append(k.in_sequence(
                piece, *(prepare(k, nxt, j, k.beside[j]), scan(k, nxt, j, k.beside[j]), finish(k, j, k.beside[j]))))
        k.together(*side_by_side)


def layers_kernel(nc, d, nb):
    with ExitStack() as ctx:
        k = Core(nc, ctx, d)
        k.t = {name: k.sb(name, shape) for name, shape in LOADS.items()}
        k.ones = k.sb("ones_over_di", [128, 128])
        k.eps = k.sb("eps", [128, 1])
        k.A = k.sb("A", [128, ND * NS])
        k.sed_b = k.sb("sedenion_bias", [96, 32])
        k.bn_r = k.sb("bn_rstd", [48, 1])
        k.G = k.sb("dft_fc1", [96, 2, GRP * 128])
        k.V = k.sb("fc2_idft", [128, 2, GRP, 96])
        k.conv_diag = k.sb("conv_diagonals", [128, 9, 128])
        k.w_of = k.sb("w_out_fuse", [128, ND, C])
        k.state = k.sb("state", [128, ND * NS])
        k.st = k.sb("bn_parts", [96, WH * 6])
        k.mv = k.sb("mean_var", [96, WH, 2])
        k.rs = k.sb("rstd_tok", [96, WH])
        k.pool = k.sb("pooled", [96, 2])
        k.tv = k.sb("t_vec", [48, 1])
        k.wts = k.sb("tap_weights", [96, 8])
        xpc = k.sb("x_piece", [96, 2, 2, TT + W])
        k.xin = k.sb("conv_in", [128, ND, TR + 2, W + 2])
        u, delta, du = (k.sb(n, [128, ND, TT])[:] for n in ("u", "delta", "delta_u"))
        k.xp = k.sb("x_proj", [R + 2 * NS, TT])
        a_all = k.sb("decay", [128, 12 * TT])
        hw_all = k.sb("scan_work", [128, 6 * TT])
        bc_all = k.sb("b_and_c", [128, 8 * TT])
        k.a = a_all[:].rearrange("p (r s n) -> p r s n", r=2 * ND, s=2)
        k.hw = hw_all[:].rearrange("p (r s n) -> p r s n", r=3, s=2)
        k.bc = bc_all[:].rearrange("p (r a s n) -> p r a s n", r=2, a=2, s=2)
        k.arena = ctx.enter_context(nc.sbuf_tensor("arena", [128, ARENA], F32))

        def part(parts, at, *shape):
            n = int(np.prod(shape))
            assert at + n <= ARENA
            v = k.arena[0:parts, at:at + n]
            if len(shape) == 1:
                return v
            names = "abcd"[:len(shape)]
            return v.rearrange(f"p ({' '.join(names)}) -> p {' '.join(names)}", **{c: s for c, s in zip(names, shape)})

        M = 2 * L
        k.fin = part(96, 0, 2, L)
        k.xres = part(96, M, 2, L)
        k.x2t = part(96, M, 2, WH, 96)
        k.x1p = part(96, 2 * M, 2, H + 1, W + 2)
        k.x2 = part(96, 2 * M + 4900, 2, L)
        k.xT = part(96, 0, WH, C)
        k.xn = part(96, M, WH, C)
        k.Rb = part(96, M, KH * C)
        k.spec = part(96, M + KH * C, KH * C)
        k.back = part(96, M, WH * C)
        k.fh = part(128, M + 2 * KH * C, 4, 2 * C)
        WS = 2 * 16 * C
        k.cm = part(96, WS + M, 2, WH, 96)
        k.hid = part(128, WS + 2 * M, 2, NF, Q)
        k.wsed = part(96, 0, 2, 16, C)
        k.yg = part(96, WS, 2, WH, 96)
        k.wa = part(96, WS + 2 * M, 2, WH, 96)
        k.res = part(96, WS + M, WH, C)
        k.P = ctx.enter_context(nc.psum_tensor("psum", [128, 8, 512], F32))

        bc_dram = [d["bc"][n] for n in range(2)]
        banks = [[k.P[:, n + m, :] for m in range(ND)] for n in (5, 0)]
        ends = dict(y=a_all[:, 0:3 * TT], rstd=a_all[:, 3 * TT:4 * TT], tot=a_all[:, 7 * TT:8 * TT],
                    sz=a_all[:, 4 * TT:7 * TT].rearrange("p (a n) -> p a n", a=ND),
                    fo=bc_all[0:96, 0:2 * TT].rearrange("p (a n) -> p a n", a=2))
        k.beside = [PieceMemory(1, CONV_SHARED[j], PE_SUMS[j], x=xpc[:, j % 2, :, :], u=u, delta=delta, du=du, bc=bc_dram[0], banks=banks[0], **ends)
                    for j in range(NT)]
        for j in range(NT - 1):
            k.beside[j].next = k.beside[j + 1]
        second = [part(128, n * ND * TT, ND, TT) for n in range(3)]
        at = 3 * ND * TT
        ends = dict(y=part(128, at, 3 * TT), rstd=part(128, at + 3 * TT, TT), tot=part(128, at + 4 * TT, TT),
                    sz=part(128, at + 5 * TT, ND, TT), fo=part(96, at + 8 * TT, 2, TT))
        x_alone = [xpc[:, 0, :, :], xpc[:, 1, :, :], part(96, at + 10 * TT, 2, TT + W)]
        k.alone = []
        for j in range(NT):
            set_u, set_delta, set_du = second if j % 2 else (u, delta, du)
            k.alone.append(PieceMemory(0, 1, 1, x=x_alone[j % 3], u=set_u, delta=set_delta, du=set_du, bc=bc_dram[j % 2],
                                       banks=banks[j % 2], **ends))

        setup_and_layer_0(k, 0)
        k.even()
        if nb > 1:
            with nc.Fori(0, nb - 1) as b:
                later_layers(k, b, b + 1)
                k.even()
        later_layers(k, nb - 1, None)


ARENA = 6144 + 3 * 4608


def laid_out(i):
    nb = i["x"].shape[0]

    def v384(v):
        return v.reshape(ND, 128).T

    def v192(v):
        return v.reshape(2, 96).T

    def halves(w):
        return w.reshape(2, 96, -1).transpose(1, 0, 2)

    def chunks(w):
        return w.reshape(-1, 128, w.shape[-1]).transpose(1, 0, 2)

    row_f, row_i, col, back, ident = dft_constants()
    rows = [i[n] for n in ("L2_conv_n1_g", "L2_conv_n1_b", "L2_conv_mlp2_b", "L3_conv_proj_b", "L3_conv_fc2_b")]
    lnv = [v192(i[n]) for n in ("L2_conv_n2_g", "L2_conv_n2_b", "L3_conv_norm1_g", "L3_conv_norm1_b",
                                "L3_conv_norm2_g", "L3_conv_norm2_b")]
    sign = sedenion_signs()
    signs = np.array([[sign[j ^ kk][kk] for j in range(16)] for kk in range(16)], np.float32)
    out = dict(
        x=i["x"].reshape(nb, C, L),
        w_in=halves(i["L0_conv_in_proj_w"].T), conv_w=i["L0_conv_conv_w"].reshape(ND, 128, 9).transpose(1, 0, 2).reshape(128, 27),
        vec384=np.stack([v384(i["L0_conv_" + n]) for n in ("conv_b", "D_param", "ln_g", "ln_b", "dt_proj_b")], 1),
        a_log=i["L0_conv_A_log"].reshape(ND, 128, NS).transpose(1, 0, 2).reshape(128, ND * NS),
        w_xp=chunks(i["L0_conv_x_proj_w"].T), w_dt=i["L0_conv_dt_proj_w"].T,
        vec192=np.stack([v192(i["L0_conv_fuse_b"]), v192(i["L1_conv_bias"])], 1),
        w1=halves(i["L1_conv_w1"].T),
        bn=np.stack([i["L1_conv_" + n] for n in ("gamma", "beta", "running_mean", "running_var")], 1),
        w2=i["L1_conv_w2"].reshape(C, 9, 48)[:, :4].transpose(2, 1, 0),
        b2=i["L1_conv_b2"].reshape(2, 96, 9)[:, :, :4].transpose(1, 0, 2),
        fc1b=np.tile(i["L2_conv_fc1_b"], 8).reshape(128, 1), fc2v=np.tile(i["L2_conv_fc2_w"].T, (8, 1)),
        fc2b=i["L2_conv_fc2_b"][:1].reshape(1, 1),
        m1=halves(i["L2_conv_mlp1_w"].T), m1b=i["L2_conv_mlp1_b"].reshape(NF, 128).T, m2=chunks(i["L2_conv_mlp2_w"].T),
        rows=np.tile(np.stack(rows)[None], (96, 1, 1)), lnv=np.stack(lnv, 1), signs=np.tile(signs[None], (96, 1, 1)),
        f1=halves(i["L3_conv_fc1_w"]), f1b=i["L3_conv_fc1_b"].reshape(NF, 128).T, f2=chunks(i["L3_conv_fc2_w"]),
        proj=halves(i["L3_conv_proj_w"]),
        out_w=halves(i["L0_conv_out_proj_w"]), fuse_w=halves(i["L0_conv_fuse_w"].reshape(C, C).T),
        fc1w=np.tile(i["L2_conv_fc1_w"].T[None], (96, 1, 1)),
        wsed=i["L3_conv_w_sed"].reshape(16, 2, 96, C).transpose(2, 1, 0, 3),
        row_f=row_f, row_i=row_i, col=col, back=back, ident=ident)
    return {n: np.ascontiguousarray(v) for n, v in out.items()}


def kernel(**inputs):
    import concourse.bacc as bacc
    from concourse.bass_utils import run_bass_kernel_spmd

    arrays = laid_out({n: np.asarray(v) for n, v in inputs.items()})
    nb = arrays["x"].shape[0]
    nc = bacc.Bacc("TRN2", target_bir_lowering=False, num_devices=1)
    d = {n: nc.dram_tensor("in_" + n, a.shape, F32, kind="ExternalInput").ap() for n, a in arrays.items()}
    d["out"] = nc.dram_tensor("out", (nb, 96, WH, C), F32, kind="ExternalOutput").ap()
    d["bc"] = nc.dram_tensor("bc_scratch", (2, 2 * NS, TT), F32, kind="Internal").ap()
    for name in ("w_minus", "w_hat"):
        d[name] = nc.dram_tensor(name + "_scratch", (96, 2, 16, C), F32, kind="Internal").ap()
    d["fused"] = nc.dram_tensor("fused_scratch", (96, 2, L), F32, kind="Internal").ap()
    d["resid"] = nc.dram_tensor("residual_scratch", (96, WH, C), F32, kind="Internal").ap()
    d["spec_in"] = nc.dram_tensor("spec_in_scratch", (48, 48, C), F32, kind="Internal").ap()
    d["spec_out"] = nc.dram_tensor("spec_out_scratch", (48, 48, C), F32, kind="Internal").ap()
    layers_kernel(nc, d, nb)
    r = run_bass_kernel_spmd(nc, [{"in_" + n: a for n, a in arrays.items()}], core_ids=[0])
    got = np.asarray(r.results[0]["out"])
    return got.reshape(nb, 2, 48, WH, C).transpose(0, 4, 2, 1, 3).reshape(nb, C, H, W)
```
